# Optimizing a Trainium2 kernel written in Bass

```python
import numpy as np
import jax
import jax.numpy as jnp

def _softmax(x, axis=-1):
    return jax.nn.softmax(x, axis=axis)

def _gelu(x):
    return jax.nn.gelu(x, approximate=True)

def _silu(x):
    return jax.nn.silu(x)

def _sigmoid(x):
    return jax.nn.sigmoid(x)

def _layernorm(x, axis=-1, eps=1e-05):
    m = jnp.mean(x, axis=axis, keepdims=True)
    v = jnp.var(x, axis=axis, keepdims=True)
    return (x - m) / jnp.sqrt(v + eps)

def _scatter_add(tgt, idx, src, axis=0):
    return tgt.at[idx].add(src)

def _segment_sum(src, seg, n):
    return jax.ops.segment_sum(src, seg, n)
kernel_name = 'mk_gnn_resnorm_d4_gnn_r8_db24b8'

def setup_inputs(seed: int=0):
    np.random.seed(seed)
    _w = jnp.asarray

    def _rec_inputs():
        import jax
        import jax.numpy as jnp
        _gk = jax.random.key(seed)
        x = -0.0004942 + 1 * jax.random.normal(jax.random.fold_in(_gk, 1), (6250, 128), jnp.float32)
        src = jax.random.randint(jax.random.fold_in(_gk, 2), (100000,), 0, 6250, jnp.int32)
        dst = jax.random.randint(jax.random.fold_in(_gk, 3), (100000,), 0, 6250, jnp.int32)
        _o = jnp.argsort(dst, stable=True)
        src = src[_o]
        dst = dst[_o]
        edge_attr_128 = -6.37281e-06 + 0.999856 * jax.random.normal(jax.random.fold_in(_gk, 12), (100000, 128), jnp.float32)
        edge_attr_20 = jax.random.uniform(jax.random.fold_in(_gk, 13), (100000, 20), jnp.float32, 0.0, 1)
        edge_weight = jax.random.uniform(jax.random.fold_in(_gk, 15), (100000,), jnp.float32, 0.0, 0.999998)
        return (x, src, dst, edge_attr_128, edge_attr_20, edge_weight)
    x, src, dst, edge_attr_128, edge_attr_20, edge_weight = _rec_inputs()

    def _L0_gnn_setup():
        import jax, jax.numpy as jnp
        import numpy as np
        N_NODES = 3750
        DEGREE = 16
        N_EDGES = N_NODES * DEGREE
        F = 128
        F_OUT = 128
        ONSET = 0.8
        CUTOFF = 1.0

        def _ssp(x):
            return jax.nn.softplus(x) - jnp.log(2.0).astype(x.dtype)

        def _smooth_cutoff(d):
            t = (d - ONSET) / (CUTOFF - ONSET)
            ramp = 0.5 * (jnp.cos(jnp.float32(np.pi) * t) + 1.0)
            return jnp.where(d < ONSET, 1.0, jnp.where(d > CUTOFF, 0.0, ramp))
        key = jax.random.key(seed)
        ks = jax.random.split(key, 10)
        h = jax.random.normal(ks[0], (N_NODES, F), dtype=jnp.float32)
        edge_feat = jax.random.normal(ks[1], (N_EDGES, F), dtype=jnp.float32)
        dist = jax.random.uniform(ks[2], (N_EDGES,), dtype=jnp.float32)
        src = jax.random.randint(ks[3], (N_EDGES,), 0, N_NODES, dtype=jnp.int32)
        dst = jnp.repeat(jnp.arange(N_NODES, dtype=jnp.int32), DEGREE)
        s = 1.0 / np.sqrt(F)
        W1 = jax.random.normal(ks[4], (F, F), dtype=jnp.float32) * s
        b1 = jnp.zeros((F,), dtype=jnp.float32)
        W2 = jax.random.normal(ks[5], (F, F), dtype=jnp.float32) * s
        b2 = jnp.zeros((F,), dtype=jnp.float32)
        W3 = jax.random.normal(ks[6], (F, F_OUT), dtype=jnp.float32) * s
        b3 = jnp.zeros((F_OUT,), dtype=jnp.float32)
        return {'h': h, 'edge_feat': edge_feat, 'dist': dist, 'src': src, 'dst': dst, 'W1': W1, 'b1': b1, 'W2': W2, 'b2': b2, 'W3': W3, 'b3': b3}
    _L0_gnn_all = _L0_gnn_setup()
    _L0_gnn_in = {k: v for k, v in _L0_gnn_all.items() if k in ('W1', 'b1', 'W2', 'b2', 'W3', 'b3')}
    del _L0_gnn_all

    def _L1_gnn_setup():
        import jax, jax.numpy as jnp
        import numpy as np
        N_ATOMS = 2500
        N_PAIRS = 80000
        N_BASIS = 128
        N_FILTERS = 128
        N_RBF = 20

        def ssp(v):
            return jax.nn.softplus(v) - jnp.log(2.0)
        key = jax.random.key(seed)
        ks = jax.random.split(key, 16)
        s = 0.05
        return {'x': jax.random.normal(ks[0], (N_ATOMS, N_BASIS), dtype=jnp.float32), 'f_ij': jax.random.uniform(ks[1], (N_PAIRS, N_RBF), dtype=jnp.float32), 'rcut_ij': jax.random.uniform(ks[2], (N_PAIRS,), dtype=jnp.float32), 'idx_i': jax.random.randint(ks[3], (N_PAIRS,), 0, N_ATOMS), 'idx_j': jax.random.randint(ks[4], (N_PAIRS,), 0, N_ATOMS), 'W_in': jax.random.normal(ks[5], (N_BASIS, N_FILTERS), dtype=jnp.float32) * s, 'b_in': jnp.zeros((N_FILTERS,), dtype=jnp.float32), 'Wf1': jax.random.normal(ks[6], (N_RBF, N_FILTERS), dtype=jnp.float32) * s, 'bf1': jnp.zeros((N_FILTERS,), dtype=jnp.float32), 'Wf2': jax.random.normal(ks[7], (N_FILTERS, N_FILTERS), dtype=jnp.float32) * s, 'bf2': jnp.zeros((N_FILTERS,), dtype=jnp.float32), 'Wo1': jax.random.normal(ks[8], (N_FILTERS, N_BASIS), dtype=jnp.float32) * s, 'bo1': jnp.zeros((N_BASIS,), dtype=jnp.float32), 'Wo2': jax.random.normal(ks[9], (N_BASIS, N_BASIS), dtype=jnp.float32) * s, 'bo2': jnp.zeros((N_BASIS,), dtype=jnp.float32)}
    _L1_gnn_all = _L1_gnn_setup()
    _L1_gnn_in = {k: v for k, v in _L1_gnn_all.items() if k in ('W_in', 'b_in', 'Wf1', 'bf1', 'Wf2', 'bf2', 'Wo1', 'bo1', 'Wo2', 'bo2')}
    del _L1_gnn_all

    def _L2_gnn_setup():
        import jax, jax.numpy as jnp
        import numpy as np
        N_NODES = 6250
        N_EDGES = 100000
        IN_F = 128
        OUT_F = 32
        HEADS = 4
        NEG_SLOPE = 0.2
        EPS = 1e-10

        def _xavier(key, shape):
            fan_in, fan_out = (shape[-2], shape[-1])
            bound = float(np.sqrt(6.0 / (fan_in + fan_out)))
            return jax.random.uniform(key, shape, jnp.float32, -bound, bound)
        key = jax.random.key(seed)
        kx, ke, kw, ks, kd = jax.random.split(key, 5)
        x = jax.random.normal(kx, (N_NODES, IN_F), jnp.float32)
        edge_index = jax.random.randint(ke, (2, N_EDGES), 0, N_NODES, jnp.int32)
        W = _xavier(kw, (HEADS, IN_F, OUT_F))
        a_src = _xavier(ks, (HEADS, OUT_F, 1))
        a_dst = _xavier(kd, (HEADS, OUT_F, 1))
        return {'x': x, 'edge_index': edge_index, 'W': W, 'a_src': a_src, 'a_dst': a_dst}
    _L2_gnn_all = _L2_gnn_setup()
    _L2_gnn_in = {k: v for k, v in _L2_gnn_all.items() if k in ('W', 'a_src', 'a_dst')}
    del _L2_gnn_all

    def _L3_gnn_setup():
        import jax, jax.numpy as jnp
        import numpy as np
        N_NODES = 6250
        N_EDGES = 100000
        D_FEAT = 128
        N_HEADS = 4
        HEAD_DIM = 32

        def mish(x):
            return x * jnp.tanh(jax.nn.softplus(x))
        key = jax.random.key(seed)
        ks = jax.random.split(key, 12)
        s = 1.0 / np.sqrt(D_FEAT)
        return {'nodes': jax.random.normal(ks[0], (N_NODES, D_FEAT), jnp.float32), 'edges': jax.random.normal(ks[1], (N_EDGES, D_FEAT), jnp.float32), 'Ws_k': jax.random.normal(ks[2], (D_FEAT, N_HEADS, HEAD_DIM), jnp.float32) * s, 'Ws_b': jnp.zeros((N_HEADS, HEAD_DIM), jnp.float32), 'Wr_k': jax.random.normal(ks[3], (D_FEAT, N_HEADS, HEAD_DIM), jnp.float32) * s, 'Wr_b': jnp.zeros((N_HEADS, HEAD_DIM), jnp.float32), 'We_k': jax.random.normal(ks[4], (D_FEAT, N_HEADS, HEAD_DIM), jnp.float32) * s, 'We_b': jnp.zeros((N_HEADS, HEAD_DIM), jnp.float32), 'attn_w': jax.random.normal(ks[5], (HEAD_DIM, 1), jnp.float32) / np.sqrt(HEAD_DIM), 'attn_b': jnp.zeros((1,), jnp.float32), 'senders': jax.random.randint(ks[6], (N_EDGES,), 0, N_NODES, jnp.int32), 'receivers': jax.random.randint(ks[7], (N_EDGES,), 0, N_NODES, jnp.int32)}
    _L3_gnn_all = _L3_gnn_setup()
    _L3_gnn_in = {k: v for k, v in _L3_gnn_all.items() if k in ('Ws_k', 'Ws_b', 'Wr_k', 'Wr_b', 'We_k', 'We_b', 'attn_w', 'attn_b')}
    del _L3_gnn_all
    return {'x': x, 'src': src, 'dst': dst, 'edge_attr_128': edge_attr_128, 'edge_attr_20': edge_attr_20, 'edge_weight': edge_weight, 'L0_gnn_W1': _L0_gnn_in['W1'], 'L0_gnn_b1': _L0_gnn_in['b1'], 'L0_gnn_W2': _L0_gnn_in['W2'], 'L0_gnn_b2': _L0_gnn_in['b2'], 'L0_gnn_W3': _L0_gnn_in['W3'], 'L0_gnn_b3': _L0_gnn_in['b3'], 'L1_gnn_W_in': _L1_gnn_in['W_in'], 'L1_gnn_b_in': _L1_gnn_in['b_in'], 'L1_gnn_Wf1': _L1_gnn_in['Wf1'], 'L1_gnn_bf1': _L1_gnn_in['bf1'], 'L1_gnn_Wf2': _L1_gnn_in['Wf2'], 'L1_gnn_bf2': _L1_gnn_in['bf2'], 'L1_gnn_Wo1': _L1_gnn_in['Wo1'], 'L1_gnn_bo1': _L1_gnn_in['bo1'], 'L1_gnn_Wo2': _L1_gnn_in['Wo2'], 'L1_gnn_bo2': _L1_gnn_in['bo2'], 'L2_gnn_W': _L2_gnn_in['W'], 'L2_gnn_a_src': _L2_gnn_in['a_src'], 'L2_gnn_a_dst': _L2_gnn_in['a_dst'], 'L3_gnn_Ws_k': _L3_gnn_in['Ws_k'], 'L3_gnn_Ws_b': _L3_gnn_in['Ws_b'], 'L3_gnn_Wr_k': _L3_gnn_in['Wr_k'], 'L3_gnn_Wr_b': _L3_gnn_in['Wr_b'], 'L3_gnn_We_k': _L3_gnn_in['We_k'], 'L3_gnn_We_b': _L3_gnn_in['We_b'], 'L3_gnn_attn_w': _L3_gnn_in['attn_w'], 'L3_gnn_attn_b': _L3_gnn_in['attn_b']}

def reference(x, src, dst, edge_attr_128, edge_attr_20, edge_weight, L0_gnn_W1, L0_gnn_b1, L0_gnn_W2, L0_gnn_b2, L0_gnn_W3, L0_gnn_b3, L1_gnn_W_in, L1_gnn_b_in, L1_gnn_Wf1, L1_gnn_bf1, L1_gnn_Wf2, L1_gnn_bf2, L1_gnn_Wo1, L1_gnn_bo1, L1_gnn_Wo2, L1_gnn_bo2, L2_gnn_W, L2_gnn_a_src, L2_gnn_a_dst, L3_gnn_Ws_k, L3_gnn_Ws_b, L3_gnn_Wr_k, L3_gnn_Wr_b, L3_gnn_We_k, L3_gnn_We_b, L3_gnn_attn_w, L3_gnn_attn_b):
    import jax
    import jax.numpy as jnp

    def _L0_gnn_ref(h, edge_feat, dist, src, dst, W1, b1, W2, b2, W3, b3):
        import jax, jax.numpy as jnp
        import numpy as np
        N_NODES = 3750
        DEGREE = 16
        N_EDGES = N_NODES * DEGREE
        F = 128
        F_OUT = 128
        ONSET = 0.8
        CUTOFF = 1.0

        def _ssp(x):
            return jax.nn.softplus(x) - jnp.log(2.0).astype(x.dtype)

        def _smooth_cutoff(d):
            t = (d - ONSET) / (CUTOFF - ONSET)
            ramp = 0.5 * (jnp.cos(jnp.float32(np.pi) * t) + 1.0)
            return jnp.where(d < ONSET, 1.0, jnp.where(d > CUTOFF, 0.0, ramp))
        N, Fdim = h.shape
        gamma = jnp.float32(Fdim)
        muk = jnp.linspace(0.0, 1.0, Fdim, dtype=jnp.float32)
        bf = jnp.exp(-gamma * (dist[:, None] - muk) ** 2)
        bf = _ssp(bf @ W1 + b1)
        bf = _ssp(bf @ W2 + b2)
        cut = _smooth_cutoff(dist)[:, None]
        msg = h[src] * edge_feat * bf * cut
        node_h = jax.ops.segment_prod(msg, dst, num_segments=N)
        return _ssp(node_h @ W3 + b3)

    def _L1_gnn_ref(x, f_ij, rcut_ij, idx_i, idx_j, W_in, b_in, Wf1, bf1, Wf2, bf2, Wo1, bo1, Wo2, bo2):
        import jax, jax.numpy as jnp
        import numpy as np
        N_ATOMS = 2500
        N_PAIRS = 80000
        N_BASIS = 128
        N_FILTERS = 128
        N_RBF = 20

        def ssp(v):
            return jax.nn.softplus(v) - jnp.log(2.0)
        n_atoms = x.shape[0]
        h = x @ W_in + b_in
        Wij = ssp(f_ij @ Wf1 + bf1) @ Wf2 + bf2
        Wij = Wij * rcut_ij[:, None]
        x_ij = h[idx_j] * Wij
        agg = jax.ops.segment_sum(x_ij, idx_i, num_segments=n_atoms)
        out = ssp(agg @ Wo1 + bo1) @ Wo2 + bo2
        return out

    def _L2_gnn_ref(x, edge_index, W, a_src, a_dst):
        import jax, jax.numpy as jnp
        import numpy as np
        N_NODES = 6250
        N_EDGES = 100000
        IN_F = 128
        OUT_F = 32
        HEADS = 4
        NEG_SLOPE = 0.2
        EPS = 1e-10

        def _xavier(key, shape):
            fan_in, fan_out = (shape[-2], shape[-1])
            bound = float(np.sqrt(6.0 / (fan_in + fan_out)))
            return jax.random.uniform(key, shape, jnp.float32, -bound, bound)
        num_nodes = x.shape[0]
        h = jnp.einsum('ni,hio->nho', x, W)
        src, dst = (edge_index[0], edge_index[1])
        e_src = jnp.einsum('nho,ho->nh', h, a_src[..., 0])
        e_dst = jnp.einsum('nho,ho->nh', h, a_dst[..., 0])
        e = e_src[src] + e_dst[dst]
        e = jnp.where(e >= 0, e, NEG_SLOPE * e)
        seg_max = jax.ops.segment_max(e, dst, num_segments=num_nodes)
        e_max = jnp.maximum(seg_max, 0.0)
        exp_e = jnp.exp(e - e_max[dst])
        sum_exp = jax.ops.segment_sum(exp_e, dst, num_segments=num_nodes)
        alpha = exp_e / (sum_exp[dst] + EPS)
        weighted = alpha[..., None] * h[src]
        out = jax.ops.segment_sum(weighted, dst, num_segments=num_nodes)
        return out.reshape(num_nodes, -1)

    def _L3_gnn_ref(nodes, edges, Ws_k, Ws_b, Wr_k, Wr_b, We_k, We_b, attn_w, attn_b, senders, receivers):
        import jax, jax.numpy as jnp
        import numpy as np
        N_NODES = 6250
        N_EDGES = 100000
        D_FEAT = 128
        N_HEADS = 4
        HEAD_DIM = 32

        def mish(x):
            return x * jnp.tanh(jax.nn.softplus(x))
        n = nodes.shape[0]
        sent = jnp.einsum('ef,fhd->ehd', nodes[senders], Ws_k) + Ws_b
        e_att = sent + jnp.einsum('ef,fhd->ehd', edges, We_k) + We_b
        recv = jnp.einsum('ef,fhd->ehd', nodes[receivers], Wr_k) + Wr_b
        logits = jnp.einsum('ehd,do->eho', mish(e_att + recv), attn_w) + attn_b
        seg_max = jax.ops.segment_max(logits, receivers, num_segments=n)
        w = jnp.exp(logits - seg_max[receivers])
        denom = jax.ops.segment_sum(w, receivers, num_segments=n)
        w = w / denom[receivers]
        msg = (w * e_att).reshape(e_att.shape[0], N_HEADS * HEAD_DIM)
        out_nodes = jax.ops.segment_sum(msg, receivers, num_segments=n)
        return out_nodes
    edge_index = jnp.stack([src, dst])
    x = _layernorm(x + _L0_gnn_ref(x, edge_attr_128, edge_weight, src, dst, L0_gnn_W1, L0_gnn_b1, L0_gnn_W2, L0_gnn_b2, L0_gnn_W3, L0_gnn_b3), axis=-1)
    x = _layernorm(x + _L1_gnn_ref(x, edge_attr_20, edge_weight, src, dst, L1_gnn_W_in, L1_gnn_b_in, L1_gnn_Wf1, L1_gnn_bf1, L1_gnn_Wf2, L1_gnn_bf2, L1_gnn_Wo1, L1_gnn_bo1, L1_gnn_Wo2, L1_gnn_bo2), axis=-1)
    x = _layernorm(x + _L2_gnn_ref(x, edge_index, L2_gnn_W, L2_gnn_a_src, L2_gnn_a_dst), axis=-1)
    x = _layernorm(x + _L3_gnn_ref(x, edge_attr_128, L3_gnn_Ws_k, L3_gnn_Ws_b, L3_gnn_Wr_k, L3_gnn_Wr_b, L3_gnn_We_k, L3_gnn_We_b, L3_gnn_attn_w, L3_gnn_attn_b, src, dst), axis=-1)
    return x

_drawn_inputs = setup_inputs


def setup_inputs(seed=0):
    import zlib

    import numpy as np

    out = dict(_drawn_inputs(seed))
    spreads = {'L0_gnn_b1': (0.0, 0.8),
     'L0_gnn_b2': (0.0, 0.8),
     'L0_gnn_b3': (0.0, 0.1),
     'L1_gnn_b_in': (0.0, 0.343),
     'L1_gnn_bf1': (0.0, 0.8),
     'L1_gnn_bf2': (0.0, 0.681),
     'L1_gnn_bo1': (0.0, 2.0),
     'L1_gnn_bo2': (0.0, 0.8),
     'L3_gnn_Ws_b': (0.0, 0.1),
     'L3_gnn_Wr_b': (0.0, 0.586),
     'L3_gnn_We_b': (0.0, 0.1)}
    factors = {'edge_attr_20': 8.0,
     'edge_weight': 4.246,
     'L0_gnn_W1': 8.0,
     'L0_gnn_W2': 8.0,
     'L0_gnn_W3': 8.0,
     'L1_gnn_Wf1': 5.064,
     'L1_gnn_Wf2': 3.679,
     'L2_gnn_a_dst': 3.071}
    for name, (base, spread) in spreads.items():
        noise = np.random.default_rng([zlib.crc32(name.encode()), seed]).standard_normal(out[name].shape)
        drawn = base * np.exp(spread * noise) if base else spread * noise
        out[name] = jnp.asarray(drawn.astype(out[name].dtype))
    for name, factor in factors.items():
        out[name] = (out[name] * factor).astype(out[name].dtype)
    return out
```

```python
from contextlib import ExitStack

import numpy as np
import concourse.bass as bass
from concourse import mybir

F32 = mybir.dt.float32
BF16 = mybir.dt.bfloat16
I32 = mybir.dt.int32
ALU = mybir.AluOpType
ACT = mybir.ActivationFunctionType
AX = mybir.AxisListType
DVE = mybir.EngineType.DVE
PE = mybir.EngineType.PE

P = 128
N, E, F = 6250, 100000, 128
HEADS, HD = 4, 32
GT = 8
GE = GT * P
NG = -(-E // GE)
NG += NG % 2
NT = NG * GT
EP = NT * P
NB = -(-(N + 1) // P)
NP = NB * P
RB = NB + 1
RW = RB * P
NBG = 7
NS = NB // NBG
NW = NBG * P
NA = GT
SEGC = 112
SEGN = NT // SEGC
PB = EP // P
assert NB % NBG == 0 and NT % SEGC == 0 and GT == 8
BIG = 1.5e38
CLAMP = 44.0
MISH_CLAMP = 20.0
LN2 = float(np.log(2.0))
LN_EPS = 1e-5
ALPHA_EPS = 1e-10
SLOPE = 0.2
PAIRS0 = 3


class Shared:
    pass


class Group:

    def __init__(self, pair, slot):
        self.n, self.pair, self.slot = 2 * pair + slot, pair, slot


class Step:

    def __init__(self, pair, odd):
        self.pair, self.odd = pair, odd

    def ago(self, k):
        total = self.odd - k
        g = Group(self.pair + total // 2, total % 2)
        return None if isinstance(g.n, int) and not 0 <= g.n < NG else g


def over_groups(eng, body, lag):
    for i in range(2 * PAIRS0):
        body(Step(i // 2, i % 2))
    with eng.Fori(PAIRS0, NG // 2) as pair:
        body(Step(pair, 0))
        body(Step(pair, 1))
    for i in range(NG, NG + lag):
        body(Step(i // 2, i % 2))


def wait_pos(eng, sem, count):
    if not (isinstance(count, int) and count <= 0):
        eng.wait_ge(sem, count)


class Chain:

    def __init__(self, eng, sem, at=None):
        self.eng, self.sem, self.count, self.at = eng, sem, 0, at

    def __call__(self, ins, name=None):
        self.count += 1
        ins.then_inc(self.sem, 1)
        self.eng.wait_ge(self.sem, self.count)
        if name:
            self.at[name] = self.count


def phase_semaphores(nc, stack, prefix):
    taken = []

    def allocate(name):
        taken.append(nc.alloc_semaphore(name=prefix + name))
        return taken[-1]

    def give_back():
        nc.clear_and_free_semaphores(taken)
        nc.all_engine_barrier()
    stack.callback(give_back)
    return allocate


def bcast(ap, axis, n):
    shape = list(ap.shape)
    shape.insert(axis, n)
    return ap.unsqueeze(axis).broadcast_to(shape)


def psum_half(ps, h):
    return ps[:, 512 * h:512 * h + 512]


def node_cols(b):
    return slice(P * b, P * b + P)


def setup(nc, g, d):
    half = NT // 2
    with ExitStack() as c:
        sb = lambda n, s, t=F32: c.enter_context(nc.sbuf_tensor(n, s, t))
        sem = phase_semaphores(nc, c, "st_")
        loaded, consts, vec, cut_sin, rel_sb, stored = (sem(x) for x in ("loaded", "consts", "vec", "cut_sin", "rel_sb", "stored"))
        tile_sums, base_bc, rel_t, hot, counted, block_sums, turned, scattered, back = (
            sem(x) for x in ("tile_sums", "base_bc", "rel_t", "hot", "counted", "block_sums", "turned", "scattered", "back"))
        dst_i, prev_i = sb("dst_i", [P, NT], I32), sb("prev_i", [P, NT], I32)
        hi, lo = sb("hi", [P, NT]), sb("lo", [P, NT])
        ta, tb = sb("ta", [P, NT]), sb("tb", [P, NT])
        start, ones = sb("start", [P, NT]), sb("ones", [P, NT])
        tri0, tris, ones_sq = sb("tri0", [P, P]), sb("tris", [P, P]), sb("ones_sq", [P, P])
        half_pi = sb("half_pi", [P, 1])
        row_a, row_b = sb("row_a", [1, NT]), sb("row_b", [1, NT])
        relc, keepc = sb("relc", [SEGC, SEGN, P], BF16), sb("keepc", [SEGC, SEGN, P], BF16)
        ohi, olo = sb("ohi", [P, 2, GT, NB], BF16), sb("olo", [P, 2, GT, P], BF16)
        iota_b, zero_b = sb("iota_b", [P, P], BF16), sb("zero_b", [P, P], BF16)
        cnt, has, ccnt, chas = (sb(x, [NB, P]) for x in ("cnt", "has", "ccnt", "chas"))
        tot, pre = sb("tot", [NB, 2]), sb("sums_before", [NB, 3])
        nid, rnk, tmpn = sb("nid", [NB, P]), sb("rnk", [NB, P]), sb("tmpn", [NB, P])
        rank_of = sb("rank_of", [P, NB], I32)
        payload, pay_r = sb("payload", [P, NB, 4]), sb("pay_r", [P, NB, 4])
        A, B, C = g.psA, g.psB, g.psC
        rows = lambda r: r[:, :].rearrange("a (h n) -> a h n", h=2)
        halves = lambda ps, n: ps[0:n, :].rearrange("a (h n) -> a h n", h=2)[:, :, 0:half]
        at = {}

        with nc.Block() as block:
            @block.vector
            def _(eng):
                do = Chain(eng, vec, at)
                eng.wait_ge(consts, 8)
                eng.wait_ge(loaded, 48)
                do(eng.tensor_scalar(g.ident[:, :], g.iota_row[:, :], g.iota_col[:, 0:1], None, ALU.is_equal))
                do(eng.tensor_scalar(g.iota_col2[:, :], g.iota_col[:, :], float(P), None, ALU.add))
                do(eng.tensor_scalar(tri0[:, :], g.iota_row[:, :], g.iota_col[:, 0:1], None, ALU.is_ge))
                do(eng.memset(tri0[0:1, :], 0.0))
                do(eng.tensor_scalar(tris[:, :], g.iota_row[:, :], g.iota_col[:, 0:1], None, ALU.is_gt))
                do(eng.memset(half_pi[:, :], float(np.pi / 2)))
                do(eng.tensor_scalar(tb[:, :], g.ewT[:, :], -0.8, float(1 / (1.0 - 0.8)), ALU.add, ALU.mult))
                do(eng.tensor_scalar(tb[:, :], tb[:, :], 0.0, 1.0, ALU.max, ALU.min), "ramp")
                do(eng.tensor_copy(hi[:, :], dst_i[:, :]))
                do(eng.tensor_copy(lo[:, :], prev_i[:, :]))
                do(eng.tensor_tensor(start[:, :], hi[:, :], lo[:, :], ALU.not_equal), "start")
                eng.wait_ge(cut_sin, 1)
                do(eng.tensor_scalar(ta[:, :], ta[:, :], 1.0, 0.5, ALU.add, ALU.mult))
                do(eng.scalar_tensor_tensor(ta[:, :], g.ewT[:, :], 1.0, ta[:, :], ALU.is_le, ALU.mult))
                do(eng.tensor_copy(g.cut[:, :], ta[:, :]))
                do(eng.tensor_scalar(tb[:, :], start[:, :], -1.0, 1.0, ALU.mult, ALU.add))
                do(eng.tensor_scalar(prev_i[:, :], dst_i[:, :], 7, None, ALU.logical_shift_right))
                do(eng.tensor_scalar(dst_i[:, :], dst_i[:, :], P - 1, None, ALU.bitwise_and))
                do(eng.tensor_copy(hi[:, :], prev_i[:, :]))
                do(eng.tensor_copy(lo[:, :], dst_i[:, :]))
                eng.wait_ge(tile_sums, 1)
                do(eng.tensor_copy(rows(g.lr), halves(A, P)))
                do(eng.tensor_copy(rows(row_a), halves(B, 1)))
                do(eng.tensor_tensor_scan(row_b[:, :], ones[0:1, :], row_a[:, :], -1.0, ALU.mult, ALU.add))
                do(eng.tensor_tensor(row_b[:, :], row_b[:, :], row_a[:, :], ALU.subtract))
                do(eng.tensor_tensor(row_b[:, :], row_b[:, :], start[0:1, :], ALU.add))
                do(eng.tensor_copy(g.rank0[:, :], row_b[:, :]))
                do(eng.tensor_scalar(g.block0[:, :], g.rank0[:, :], 7, None, ALU.logical_shift_right))
                do(eng.tensor_copy(row_a[:, :], g.block0[:, :]))
                do(eng.scalar_tensor_tensor(row_a[:, :], row_a[:, :], -float(P), row_b[:, :], ALU.mult, ALU.add), "base_row")
                eng.wait_ge(base_bc, 1)
                do(eng.tensor_tensor(rows(ta), rows(g.lr), halves(B, P), ALU.add), "rel")

                def one_hots(step):
                    t = step.ago(0)
                    if t is None:
                        return
                    wait_pos(eng, counted, t.n - 1)
                    cols = bass.ds(t.n * GT, GT)
                    eng.tensor_tensor(ohi[:, t.slot], bcast(iota_b[:, 0:NB], 1, GT), bcast(hi[:, cols], 2, NB),
                                      ALU.is_equal).then_inc(hot, 1)
                    eng.tensor_tensor(olo[:, t.slot], bcast(iota_b[:, :], 1, GT), bcast(lo[:, cols], 2, P),
                                      ALU.is_equal).then_inc(hot, 1)
                over_groups(eng, one_hots, 0)

                eng.wait_ge(counted, NG)
                do(eng.tensor_copy(cnt[:, :], C[0:NB, 0:P]))
                do(eng.tensor_scalar(has[:, :], cnt[:, :], 1.0, None, ALU.min))
                do(eng.tensor_tensor_scan(ccnt[:, :], ones[0:NB, 0:P], cnt[:, :], 0.0, ALU.mult, ALU.add))
                do(eng.tensor_tensor_scan(chas[:, :], ones[0:NB, 0:P], has[:, :], 0.0, ALU.mult, ALU.add))
                do(eng.tensor_copy(tot[:, 0:1], ccnt[:, P - 1:P]))
                do(eng.tensor_copy(tot[:, 1:2], chas[:, P - 1:P]), "totals")
                eng.wait_ge(block_sums, 1)
                do(eng.tensor_copy(pre[:, :], B[0:NB, 0:3]))
                do(eng.tensor_scalar(ccnt[:, :], ccnt[:, :], pre[:, 0:1], -1.0, ALU.add, ALU.add))
                do(eng.tensor_scalar(ccnt[:, :], ccnt[:, :], 0.0, None, ALU.max))
                do(eng.tensor_scalar(chas[:, :], chas[:, :], pre[:, 1:2], None, ALU.add))
                do(eng.tensor_tensor(rnk[:, :], nid[:, :], chas[:, :], ALU.subtract))
                do(eng.tensor_scalar(rnk[:, :], rnk[:, :], pre[:, 2:3], None, ALU.add))
                do(eng.tensor_scalar(chas[:, :], chas[:, :], -1.0, None, ALU.add))
                do(eng.tensor_tensor(tmpn[:, :], chas[:, :], rnk[:, :], ALU.subtract))
                do(eng.tensor_tensor(tmpn[:, :], tmpn[:, :], has[:, :], ALU.mult))
                do(eng.tensor_tensor(rnk[:, :], rnk[:, :], tmpn[:, :], ALU.add), "ranks")
                eng.wait_ge(turned, 1)
                do(eng.tensor_copy(rank_of[:, :], A[:, 0:NB]))
                for k in range(3):
                    do(eng.tensor_copy(payload[:, :, k], A[:, 64 * (k + 1):64 * (k + 1) + NB]))
                do(eng.memset(payload[:, :, 3], 0.0), "payload")
                eng.wait_ge(back, 16)
                do(eng.tensor_copy(g.last_edge[:, :], pay_r[:, :, 0]))
                do(eng.tensor_copy(g.has_edge[:, :], pay_r[:, :, 1]))
                do(eng.tensor_copy(g.node[:, :], pay_r[:, :, 2]))

            @block.tensor
            def _(eng):
                eng.wait_ge(vec, at["start"])
                for h in range(2):
                    eng.matmul(A[:, 512 * h:512 * h + half], tri0[:, :], start[:, half * h:half * (h + 1)], start=True, stop=True)
                for h in range(2):
                    ins = eng.matmul(B[0:1, 512 * h:512 * h + half], ones_sq[:, 0:1], start[:, half * h:half * (h + 1)],
                                     start=True, stop=True)
                ins.then_inc(tile_sums, 1)
                eng.wait_ge(vec, at["base_row"])
                for h in range(2):
                    ins = eng.matmul(B[:, 512 * h:512 * h + half], g.ones_row[:, :], row_a[:, half * h:half * (h + 1)],
                                     start=True, stop=True)
                ins.then_inc(base_bc, 1)
                eng.wait_ge(vec, at["rel"])
                for k in range(SEGN):
                    eng.transpose(A[0:SEGC, P * k:P * k + P], ta[:, SEGC * k:SEGC * (k + 1)], g.ident[:, :])
                    ins = eng.transpose(g.psD[0:SEGC, P * k:P * k + P], tb[:, SEGC * k:SEGC * (k + 1)], g.ident[:, :])
                ins.then_inc(rel_t, 1)

                def count(step):
                    t = step.ago(0)
                    if t is None:
                        return
                    eng.wait_ge(hot, 2 * t.n + 2)
                    for k in range(GT):
                        ins = eng.matmul(C[0:NB, 0:P], ohi[:, t.slot, k, :], olo[:, t.slot, k, :], start=False, stop=False,
                                         skip_group_check=True)
                    ins.then_inc(counted, 1)
                eng.wait_ge(consts, 8)
                eng.matmul(C[0:NB, 0:P], zero_b[:, 0:NB], zero_b[:, :], start=True, stop=False, skip_group_check=True)
                over_groups(eng, count, 0)
                eng.wait_ge(vec, at["totals"])
                eng.matmul(B[0:NB, 0:2], tris[0:NB, 0:NB], tot[:, :], start=True, stop=True)
                eng.matmul(B[0:NB, 2:3], ones_sq[0:NB, 0:NB], tot[:, 1:2], start=True, stop=True).then_inc(block_sums, 1)
                eng.wait_ge(vec, at["ranks"])
                eng.wait_ge(rel_sb, 1)
                for k, m in enumerate((rnk, ccnt, has, nid)):
                    ins = eng.transpose(A[:, 64 * k:64 * k + NB], m[:, :], g.ident[0:NB, 0:NB])
                ins.then_inc(turned, 1)

            @block.scalar
            def _(eng):
                eng.wait_ge(vec, at["ramp"])
                eng.activation(ta[:, :], tb[:, :], ACT.Sin, bias=half_pi[:, 0:1], scale=-float(np.pi)).then_inc(cut_sin, 1)
                eng.preload_act_table_set("natural_log_exp_and_others")
                eng.wait_ge(rel_t, 1)
                eng.copy(relc[:, :, :], A[0:SEGC, 0:SEGN * P].rearrange("t (k p) -> t k p", p=P)).then_inc(rel_sb, 1)
                eng.copy(keepc[:, :, :], g.psD[0:SEGC, 0:SEGN * P].rearrange("t (k p) -> t k p", p=P)).then_inc(rel_sb, 1)

            @block.gpsimd
            def _(pool):
                for t, step, mul, n in ((g.iota_row, 1, 0, P), (g.iota_col, 0, 1, 1), (nid, 1, P, P), (iota_b, 1, 0, P)):
                    pool.iota(t[:, :], [[step, n]], base=0, channel_multiplier=mul,
                              allow_small_or_imprecise_dtypes=True).then_inc(consts, 1)
                for t in (ones, ones_sq, g.ones_row):
                    pool.memset(t[:, :], 1.0).then_inc(consts, 1)
                pool.memset(zero_b[:, :], 0.0).then_inc(consts, 1)
                pool.wait_ge(vec, at["payload"])
                for b in range(NB):
                    pool.indirect_dma_start(d["perm"], bass.IndirectOffsetOnAxis(ap=rank_of[:, b:b + 1], axis=0),
                                            payload[:, b, :], None).then_inc(scattered, 16)

            @block.sync
            def _(sp):
                for dst, src in ((dst_i, d["dstT"]), (prev_i, d["prevT"]), (g.ewT, d["ewT"])):
                    sp.dma_start(dst[:, :], src).then_inc(loaded, 16)
                sp.wait_ge(rel_sb, 2)
                sp.dma_start(d["rel"].rearrange("(k t p) -> t k p", k=SEGN, p=P), relc[:, :, :]).then_inc(stored, 16)
                sp.dma_start(d["keep"].rearrange("(k t p) -> t k p", k=SEGN, p=P), keepc[:, :, :]).then_inc(stored, 16)
                sp.wait_ge(stored, 32)
                sp.wait_ge(scattered, 16 * NB)
                sp.dma_start(pay_r[:, :, :], d["perm"].rearrange("(b p) w -> p b w", p=P)).then_inc(back, 16)
                sp.wait_ge(back, 16)


def scan_masks(nc, g, d):
    with ExitStack() as c:
        sb = lambda n, s, t=F32: c.enter_context(nc.sbuf_tensor(n, s, t))
        sem = phase_semaphores(nc, c, "sm_")
        loaded, vec, turned = (sem(x) for x in ("loaded", "vec", "turned"))
        dP, pP, nP = (sb(x, [P, PB], I32) for x in ("dP", "pP", "nP"))
        df, of = sb("df", [P, PB]), sb("of", [P, PB])
        sP, ones = sb("sP", [P, PB]), sb("onesP", [P, PB])
        any_s, any_l, wide = sb("any_s", [P, 1]), sb("any_l", [P, 1]), sb("wide", [P, 3, HEADS])
        at = {}
        with nc.Block() as block:
            @block.vector
            def _(eng):
                do = Chain(eng, vec, at)
                do(eng.memset(ones[:, :], 1.0))
                eng.wait_ge(loaded, 48)
                do(eng.tensor_copy(df[:, :], dP[:, :]))
                do(eng.tensor_copy(of[:, :], pP[:, :]))
                do(eng.tensor_tensor(sP[:, :], df[:, :], of[:, :], ALU.not_equal))
                do(eng.tensor_copy(of[:, :], nP[:, :]))
                do(eng.tensor_tensor(g.last[:, :], df[:, :], of[:, :], ALU.not_equal))
                do(eng.tensor_scalar(g.reset[:, :], sP[:, :], -BIG, None, ALU.mult))
                do(eng.tensor_scalar(g.keep_s[:, :], sP[:, :], -1.0, 1.0, ALU.mult, ALU.add))
                do(eng.tensor_scalar(g.keep_l[:, :], g.last[:, :], -1.0, 1.0, ALU.mult, ALU.add))
                do(eng.tensor_tensor_scan(df[:, :], ones[:, :], sP[:, :], 0.0, ALU.mult, ALU.max))
                do(eng.tensor_copy(any_s[:, :], df[:, PB - 1:PB]))
                do(eng.tensor_scalar(g.pre[:, :], df[:, :], -1.0, 1.0, ALU.mult, ALU.add))
                do(eng.tensor_scalar(g.pre_neg[:, :], df[:, :], -BIG, None, ALU.mult))
                do(eng.tensor_tensor_scan(of[:, ::-1], ones[:, :], g.last[:, ::-1], 0.0, ALU.mult, ALU.max))
                do(eng.tensor_copy(any_l[:, :], of[:, 0:1]))
                do(eng.tensor_scalar(g.suf[:, :], of[:, :], -1.0, 1.0, ALU.mult, ALU.add))
                do(eng.tensor_scalar(wide[:, 0, :], bcast(any_s[:, 0], 1, HEADS), -BIG, None, ALU.mult))
                do(eng.tensor_scalar(wide[:, 1, :], bcast(any_s[:, 0], 1, HEADS), -1.0, 1.0, ALU.mult, ALU.add))
                do(eng.tensor_scalar(wide[:, 2, :], bcast(any_l[:, 0], 1, HEADS), -1.0, 1.0, ALU.mult, ALU.add), "wide")
                eng.wait_ge(turned, 1)
                do(eng.tensor_copy(g.chain_mask[:, :, :], g.psA[0:HEADS, 0:3 * P].rearrange("h (k p) -> h k p", p=P)))

            @block.tensor
            def _(eng):
                eng.wait_ge(vec, at["wide"])
                for k in range(3):
                    ins = eng.transpose(g.psA[0:HEADS, P * k:P * k + P], wide[:, k, :], g.ident[:, :])
                ins.then_inc(turned, 1)

            @block.sync
            def _(sp):
                for dst, src in ((dP, d["dstP"]), (pP, d["prevP"]), (nP, d["nextP"])):
                    sp.dma_start(dst[:, :], src).then_inc(loaded, 16)


def gather_group(pool, t, table, idx, rows, idx_landed, slot_free, go, landed):
    width = table.shape[1]
    pool.wait_ge(idx_landed[t.slot], 16 * (t.pair + 1))
    for sem, count in slot_free:
        wait_pos(pool, sem, count)
    pool.sem_inc(go, 1)
    for k in range(GT):
        pool.indirect_dma_start(rows[t.slot][:, k * width:(k + 1) * width], None, table,
                                bass.IndirectOffsetOnAxis(ap=idx[t.slot][:, k:k + 1], axis=0)).then_inc(landed[t.slot], 16)


def load_ints(nc, engine, row, n, most):
    return nc.values_load_multi_w_load_instructions(
        row[0:1, bass.ds(n * GT, GT)], engines=(engine,), min_val=0, max_val=most,
        skip_runtime_bounds_check_because="ranks are at most the number of nodes")[1]


def expand_destination(eng, ps, hotT, state, block0):
    for k in range(GT):
        for b in range(2):
            ins = eng.matmul(ps[:, P * k:P * k + P], hotT[:, b, P * k:P * k + P], state[:, bass.ds(block0[k] * F + F * b, F)],
                             start=b == 0, stop=b == 1)
    return ins


def softplus_parts(eng, at_44, z, out, ready, n, clamp):
    eng.activation(out, z, ACT.Relu, bias=at_44, scale=-1.0).then_inc(ready, 1)
    eng.wait_ge(ready, n + 1)
    eng.activation(out, out, ACT.Exp, bias=clamp, scale=-1.0).then_inc(ready, 1)
    eng.wait_ge(ready, n + 2)
    eng.activation(out, out, ACT.Ln, bias=1.0).then_inc(ready, 1)


def filter_products(nc, g, d):
    with ExitStack() as c:
        sb = lambda n, s, t=F32: c.enter_context(nc.sbuf_tensor(n, s, t))
        two = lambda n, s, t=F32: [sb(n + "_a", s, t), sb(n + "_b", s, t)]
        sem = phase_semaphores(nc, c, "fp_")
        two_sems = lambda n: [sem(n + "0"), sem(n + "1")]
        w1, w2 = sb("w1", [F, F]), sb("w2", [F, F])
        b1, b2, mu, neg_mu, lift1, lift2, clamp = (sb(x, [P, 1]) for x in ("b1", "b2", "mu", "neg_mu", "lift1", "lift2", "clamp0"))
        dist, idx, ef, G = two("dist", [P, GE]), two("idx", [P, GT], I32), two("ef", [P, GE]), two("G", [P, GE])
        sq, rbf, parts1, sp1 = sb("sq", [P, GE]), two("rbf", [P, GE]), sb("parts1", [P, GE]), two("sp1_", [P, GE])
        parts2, sp2, prod = sb("parts2", [P, GE]), sb("sp2", [P, GE]), sb("prod", [P, GE])
        keep = two("keep", [P, GE], BF16)
        Gc, D, D0, D1 = (sb(x, [P, GE]) for x in ("Gc", "D", "D0", "D1"))
        cut, run, rows = sb("cut_now", [P, GT]), two("run", [P, GE]), two("rows_sb", [P, GE])
        weights, vec = sem("weights"), sem("vec")
        dist_in, idx_in, ef_in, G_in, stored = (two_sems(x) for x in ("dist_in", "idx_in", "ef_in", "G_in", "stored"))
        go, squared, rbf_ok, z1_ok, parts1_ok, sp1_ok, z2_ok, parts2_ok = (
            sem(x) for x in ("go", "squared", "rbf_ok", "z1_ok", "parts1_ok", "sp1_ok", "z2_ok", "parts2_ok"))
        cut_ok, scaled, sp2_ok, prod_ok, turned, D_ok, run_ok, back_ok, rows_ok = (
            sem(x) for x in ("cut_ok", "scaled", "sp2_ok", "prod_ok", "turned", "D_ok", "run_ok", "back_ok", "rows_ok"))
        keep_in = two_sems("keep_in")
        ones_col, shift = sb("ones_col", [P, 1]), g.psD[:, 0:1]
        shift_ok, b2_ok = sem("shift_ok"), sem("b2_ok")
        z1, z2, back, gt = g.psA, g.psB, g.psC, g.psD
        at = {}

        with nc.Block() as block:
            @block.sync
            def _(sp):
                for dst, src in ((w1, d["w1"]), (w2, d["w2"]), (b1, d["b1"]), (b2, d["b2"]), (mu, d["mu"])):
                    sp.dma_start(dst[:, :], src).then_inc(weights, 16)

                def step(s):
                    if (t := s.ago(0)) is not None:
                        wait_pos(sp, squared, t.n - 1)
                        sp.dma_start(dist[t.slot][:, :], d["ew"][:, bass.ds(t.n * GE, GE)].broadcast_to([P, GE])).then_inc(dist_in[t.slot], 16)
                        wait_pos(sp, G_in[t.slot], 16 * GT * t.pair)
                        sp.dma_start(idx[t.slot][:, :], d["srcG"][bass.ds(t.n, 1)].rearrange("o p k -> (o p) k")).then_inc(idx_in[t.slot], 16)
                    if (t := s.ago(2)) is not None:
                        wait_pos(sp, D_ok, 3 * (t.n - 1))
                        wait_pos(sp, prod_ok, t.n - 1)
                        sp.dma_start(ef[t.slot][:, :], d["ef"][:, bass.ds(t.n * GE, GE)]).then_inc(ef_in[t.slot], 16)
                        sp.dma_start(keep[t.slot][:, :], bcast(d["keep"][bass.ds(t.n * GE, GE)], 0, P)).then_inc(keep_in[t.slot], 16)
                    if (t := s.ago(5)) is not None:
                        sp.wait_ge(rows_ok, t.n + 1)
                        sp.dma_start(d["rows"][bass.ds(t.n * GE, GE), :].rearrange("(k p) f -> p k f", p=P),
                                     rows[t.slot][:, :].rearrange("p (k f) -> p k f", k=GT)).then_inc(stored[t.slot], 16)
                over_groups(sp, step, 5)
                for s in stored:
                    sp.wait_ge(s, 16 * (NG // 2))

            @block.gpsimd
            def _(pool):
                def step(s):
                    if (t := s.ago(0)) is not None:
                        gather_group(pool, t, d["x"], idx, G, idx_in, [(scaled, t.n - 1)], go, G_in)
                over_groups(pool, step, 0)

            @block.scalar
            def _(eng):
                eng.wait_ge(vec, 5)

                def step(s):
                    if (t := s.ago(0)) is not None:
                        eng.wait_ge(dist_in[t.slot], 16 * (t.pair + 1))
                        wait_pos(eng, rbf_ok, t.n)
                        eng.activation(sq[:, :], dist[t.slot][:, :], ACT.Square, bias=neg_mu[:, 0:1]).then_inc(squared, 1)
                        eng.wait_ge(squared, t.n + 1)
                        wait_pos(eng, z1_ok, t.n - 1)
                        eng.activation(rbf[t.slot][:, :], sq[:, :], ACT.Exp, scale=-float(F)).then_inc(rbf_ok, 1)
                    if (t := s.ago(1)) is not None:
                        eng.wait_ge(z1_ok, t.n + 1)
                        wait_pos(eng, sp1_ok, t.n)
                        softplus_parts(eng, lift1[:, 0:1], z1[:, :], parts1[:, :], parts1_ok, 3 * t.n, clamp[:, 0:1])
                    if (t := s.ago(2)) is not None:
                        eng.wait_ge(z2_ok, t.n + 1)
                        wait_pos(eng, sp2_ok, t.n)
                        softplus_parts(eng, lift2[:, 0:1], z2[:, :], parts2[:, :], parts2_ok, 3 * t.n, clamp[:, 0:1])
                    if (t := s.ago(4)) is not None:
                        eng.wait_ge(back_ok, t.n + 1)
                        wait_pos(eng, stored[t.slot], 16 * t.pair)
                        eng.copy(rows[t.slot][:, :], back[:, :]).then_inc(rows_ok, 1)
                over_groups(eng, step, 4)

            @block.tensor
            def _(eng):
                eng.wait_ge(weights, 80)
                eng.wait_ge(vec, 1)
                eng.matmul(shift, w2[:, :], ones_col[:, :], start=True, stop=True).then_inc(shift_ok, 1)
                eng.wait_ge(vec, 5)

                def step(s):
                    if (t := s.ago(1)) is not None:
                        eng.wait_ge(rbf_ok, t.n + 1)
                        wait_pos(eng, sp1_ok, t.n)
                        for h in range(2):
                            ins = eng.matmul(psum_half(z1, h), w1[:, :], rbf[t.slot][:, 512 * h:512 * h + 512], start=True, stop=True)
                        ins.then_inc(z1_ok, 1)
                    if (t := s.ago(2)) is not None:
                        eng.wait_ge(sp1_ok, t.n + 1)
                        wait_pos(eng, sp2_ok, t.n)
                        for h in range(2):
                            ins = eng.matmul(psum_half(z2, h), w2[:, :], sp1[t.slot][:, 512 * h:512 * h + 512], start=True, stop=True)
                        ins.then_inc(z2_ok, 1)
                    if (t := s.ago(4)) is not None:
                        eng.wait_ge(run_ok, t.n + 1)
                        wait_pos(eng, rows_ok, t.n)
                        for k in range(GT):
                            ins = eng.transpose(back[:, P * k:P * k + P], run[t.slot][:, P * k:P * k + P], g.ident[:, :])
                        ins.then_inc(back_ok, 1)
                    if (t := s.ago(2)) is not None:
                        eng.wait_ge(scaled, t.n + 1)
                        wait_pos(eng, D_ok, 3 * t.n - 2)
                        for k in range(GT):
                            ins = eng.transpose(gt[:, P * k:P * k + P], Gc[:, P * k:P * k + P], g.ident[:, :])
                        ins.then_inc(turned, 1)
                over_groups(eng, step, 4)

            @block.vector
            def _(eng):
                eng.wait_ge(weights, 80)
                eng.memset(ones_col[:, :], 1.0).then_inc(vec, 1)
                eng.memset(clamp[:, :], CLAMP).then_inc(vec, 1)
                eng.tensor_scalar(neg_mu[:, :], mu[:, :], -1.0, None, ALU.mult).then_inc(vec, 1)
                eng.tensor_scalar(lift1[:, :], b1[:, :], -1.0, CLAMP, ALU.mult, ALU.add).then_inc(vec, 1)
                eng.wait_ge(shift_ok, 1)
                eng.scalar_tensor_tensor(b2[:, :], shift, -LN2, b2[:, :], ALU.mult, ALU.add).then_inc(b2_ok, 1)
                eng.wait_ge(b2_ok, 1)
                eng.tensor_scalar(lift2[:, :], b2[:, :], -1.0, CLAMP, ALU.mult, ALU.add).then_inc(vec, 1)

                def step(s):
                    if (t := s.ago(3)) is not None:
                        eng.wait_ge(parts2_ok, 3 * t.n + 3)
                        wait_pos(eng, prod_ok, t.n)
                        eng.scalar_tensor_tensor(sp2[:, :], z2[:, :], b2[:, 0:1], parts2[:, :], ALU.add, ALU.max).then_inc(sp2_ok, 1)
                        eng.wait_ge(sp2_ok, t.n + 1)
                        eng.wait_ge(ef_in[t.slot], 16 * (t.pair + 1))
                        wait_pos(eng, D_ok, 3 * t.n)
                        eng.scalar_tensor_tensor(prod[:, :], sp2[:, :], -LN2, ef[t.slot][:, :], ALU.add, ALU.mult).then_inc(prod_ok, 1)
                        eng.wait_ge(prod_ok, t.n + 1)
                        eng.wait_ge(turned, t.n + 1)
                        eng.tensor_tensor(D[:, :], prod[:, :], gt[:, :], ALU.mult).then_inc(D_ok, 1)
                    if (t := s.ago(2)) is not None:
                        wait_pos(eng, scaled, t.n)
                        eng.tensor_copy(cut[:, :], g.cut[:, bass.ds(t.n * GT, GT)]).then_inc(cut_ok, 1)
                        eng.wait_ge(G_in[t.slot], 16 * GT * (t.pair + 1))
                        wait_pos(eng, turned, t.n)
                        eng.wait_ge(cut_ok, t.n + 1)
                        for k in range(GT):
                            ins = eng.tensor_scalar(Gc[:, P * k:P * k + P], G[t.slot][:, P * k:P * k + P], cut[:, k:k + 1], None, ALU.mult)
                        ins.then_inc(scaled, 1)
                    if (t := s.ago(3)) is not None:
                        eng.wait_ge(D_ok, 3 * t.n + 1)
                        eng.wait_ge(keep_in[t.slot], 16 * (t.pair + 1))
                        wait_pos(eng, run_ok, t.n)
                        eng.tensor_tensor(D0[:, :], D[:, :], keep[t.slot][:, :], ALU.mult).then_inc(D_ok, 1)
                        eng.wait_ge(D_ok, 3 * t.n + 2)
                        eng.tensor_tensor(D1[:, :], D[:, :], D0[:, :], ALU.subtract).then_inc(D_ok, 1)
                        eng.wait_ge(D_ok, 3 * t.n + 3)
                        wait_pos(eng, back_ok, t.n - 1)
                        initial = 1.0 if isinstance(t.n, int) and t.n == 0 else run[1 - t.slot][:, GE - 1:GE]
                        eng.tensor_tensor_scan(run[t.slot][:, :], D0[:, :], D1[:, :], initial, ALU.mult, ALU.add).then_inc(run_ok, 1)
                    if (t := s.ago(1)) is not None:
                        eng.wait_ge(parts1_ok, 3 * t.n + 3)
                        wait_pos(eng, z2_ok, t.n - 1)
                        eng.scalar_tensor_tensor(sp1[t.slot][:, :], z1[:, :], b1[:, 0:1], parts1[:, :], ALU.add, ALU.max).then_inc(sp1_ok, 1)
                over_groups(eng, step, 3)


def node_stage(nc, g, d, layer):
    with ExitStack() as c:
        sb = lambda n, s, t=F32: c.enter_context(nc.sbuf_tensor(f"n{layer}_{n}", s, t))
        sem = phase_semaphores(nc, c, f"n{layer}_")
        weights, const, gathered, head_ok, mixed, parts_ok, soft_ok, out_ok, vec, rstd_ok, xT_ps, xT_ok, tab_ps, sent = (
            sem(x) for x in ("weights", "const", "gathered", "head_ok", "mixed", "parts_ok", "soft_ok", "out_ok", "vec",
                             "rstd_ok", "xT_ps", "xT_ok", "tab_ps", "sent_a"))
        sent, cleared = [sent, sem("sent_b")], sem("cleared")
        cols = lambda s: slice(NW * s, NW * s + NW)
        blocks = lambda s: slice(NBG * s, NBG * s + NBG)
        view = lambda t: t[:, 0:NW].rearrange("p (b f) -> p b f", b=NBG)
        head, outp, xTp, tabp = g.psA, g.psB, g.psC, g.psD
        wide = F + HEADS if layer == 1 else F
        y, sq, xT, tab = sb("y", [P, NW]), sb("sq", [P, NW]), sb("xT", [P, NW]), sb("tab", [P, 2, NBG, wide])
        mean, var, t0, rstd = (sb(x, [P, NBG]) for x in ("mean", "var", "t0", "rstd"))
        clamp, one_c = sb("clamp", [P, 1]), sb("one_c", [P, 1])
        loads, w = [], {}

        def weight(name, shape):
            w[name] = sb("w_" + name, shape)
            loads.append((w[name], d[name]))
            return w[name]

        if layer == 0:
            zeros = sb("zeros", [P, F])
            w3, b3, w_in, b_in = weight("w3", [F, F]), weight("b3", [1, F]), weight("w_in", [F, F]), weight("b_in", [1, F])
            last_rows, no_edge = sb("last_rows", [P, NB, F]), sb("no_edge", [P, NB])
        elif layer == 1:
            wo1, bo1, wo2, bo2 = weight("wo1", [F, F]), weight("bo1", [F, 1]), weight("wo2", [F, F]), weight("bo2", [1, F])
            wg, wgT, a_heads = weight("wg", [F, F]), weight("wgT", [F, F]), weight("a_heads", [F, 2 * HEADS])
            w_att, lift = sb("w_att", [F, 2 * HEADS]), sb("lift", [P, 1])
            ed, ed_b = sb("ed", [P, NBG, HEADS]), sb("ed_b", [P, NBG, HEADS])
        elif layer == 2:
            ws, wr = weight("ws", [F, F]), weight("wr", [F, F])
            bs, be, br = weight("bs", [1, F]), weight("be", [1, F]), weight("br", [1, F])
            bse = sb("bse", [1, F])
        soft, xT2 = sb("soft", [P, NW]), sb("xT2", [P, NW])
        at = {}

        with nc.Block() as block:
            @block.vector
            def _(eng):
                do = Chain(eng, vec, at)
                do(eng.memset(clamp[:, :], CLAMP))
                do(eng.memset(one_c[:, :], 1.0), "ones")
                eng.wait_ge(weights, 16 * len(loads))
                if layer == 0:
                    do(eng.tensor_scalar(no_edge[:, :], g.has_edge[:, :], -1.0, 1.0, ALU.mult, ALU.add))
                if layer == 1:
                    do(eng.tensor_scalar(lift[:, :], bo1[:, :], -1.0, CLAMP, ALU.mult, ALU.add))
                    eng.wait_ge(const, 1)
                    do(eng.scalar_tensor_tensor(bo2[:, :], tabp[0:1, 0:F], -LN2, bo2[:, :], ALU.mult, ALU.add))
                    do(eng.tensor_copy(w_att[:, :], xTp[:, 0:2 * HEADS]))
                if layer == 2:
                    do(eng.tensor_tensor(bse[:, :], bs[:, :], be[:, :], ALU.add))
                if layer == 0:
                    do(eng.memset(zeros[:, :], 0.0), "zeros")
                    do(eng.memset(g.recv[:, NB * F:RW], 0.0))
                at["consts"] = do.count
                for s in range(NS):
                    if layer == 0:
                        eng.wait_ge(gathered, 16 * 2 * NB)
                        for b in range(NBG * s, NBG * s + NBG):
                            ins = eng.tensor_scalar(last_rows[:, b, :], last_rows[:, b, :], g.has_edge[:, b:b + 1],
                                                    no_edge[:, b:b + 1], ALU.mult, ALU.add)
                        ins.then_inc(mixed, 1)
                        eng.wait_ge(parts_ok, 3 * s + 3)
                        do(eng.tensor_tensor(y[:, :], outp[:, 0:NW], soft[:, :], ALU.max))
                        do(eng.scalar_tensor_tensor(view(y), view(y), -LN2, g.x[:, blocks(s), :], ALU.add, ALU.add), f"out{s}")
                    elif layer == 1:
                        eng.wait_ge(parts_ok, 3 * s + 3)
                        if s:
                            eng.wait_ge(out_ok, s)
                        for h in range(2):
                            ins = eng.scalar_tensor_tensor(xT2[:, 448 * h:448 * h + 448], head[:, 512 * h:512 * h + 448], bo1[:, 0:1],
                                                           soft[:, 448 * h:448 * h + 448], ALU.add, ALU.max)
                            ins.then_inc(soft_ok, 1)
                        eng.wait_ge(out_ok, s + 1)
                        do(eng.tensor_tensor(y[:, :], outp[:, 0:NW], g.x[:, blocks(s), :].rearrange("p b f -> p (b f)"), ALU.add), f"out{s}")
                    else:
                        eng.wait_ge(out_ok, s + 1)
                        do(eng.tensor_tensor(y[:, :], outp[:, 0:NW], g.x[:, blocks(s), :].rearrange("p b f -> p (b f)"), ALU.add), f"out{s}")
                    do(eng.tensor_reduce(mean[:, :], view(y), AX.X, ALU.add))
                    do(eng.tensor_scalar(mean[:, :], mean[:, :], 1.0 / F, None, ALU.mult))
                    do(eng.tensor_tensor(view(y), view(y), bcast(mean[:, :], 2, F), ALU.subtract))
                    do(eng.tensor_tensor(sq[:, :], y[:, :], y[:, :], ALU.mult))
                    do(eng.tensor_reduce(var[:, :], view(sq), AX.X, ALU.add))
                    do(eng.tensor_scalar(var[:, :], var[:, :], 1.0 / F, LN_EPS, ALU.mult, ALU.add), f"var{s}")
                    eng.wait_ge(rstd_ok, 2 * s + 2)
                    do(eng.tensor_tensor(t0[:, :], rstd[:, :], rstd[:, :], ALU.mult))
                    do(eng.tensor_tensor(t0[:, :], t0[:, :], var[:, :], ALU.mult))
                    do(eng.tensor_scalar(t0[:, :], t0[:, :], -0.5, 1.5, ALU.mult, ALU.add))
                    do(eng.tensor_tensor(rstd[:, :], rstd[:, :], t0[:, :], ALU.mult))
                    do(eng.tensor_tensor(g.x[:, blocks(s), :], view(y), bcast(rstd[:, :], 2, F), ALU.mult), f"x{s}")
                    if layer == 3:
                        continue
                    eng.wait_ge(tab_ps, s + 1)
                    if s > 1 and layer > 0:
                        eng.wait_ge(sent[s % 2], 16 * NBG * (s // 2))
                    if layer > 0:
                        do(eng.tensor_copy(tab[:, s % 2, :, 0:F], view(tabp)))
                    if layer == 1:
                        do(eng.tensor_copy(tab[:, s % 2, :, F:wide], head[:, 0:2 * HEADS * NBG].rearrange("p (b k) -> p b k", b=NBG)[:, :, 0:HEADS]))
                        do(eng.tensor_copy(ed[:, :, :], head[:, 0:2 * HEADS * NBG].rearrange("p (b k) -> p b k", b=NBG)[:, :, HEADS:]), f"att{s}")
                        part = lambda k: g.ed[:, blocks(s), k, :]
                        do(eng.tensor_copy(part(0), ed[:, :, :]))
                        do(eng.tensor_copy(ed_b[:, :, :], part(0)))
                        do(eng.tensor_tensor(ed[:, :, :], ed[:, :, :], ed_b[:, :, :], ALU.subtract))
                        do(eng.tensor_copy(part(1), ed[:, :, :]))
                        do(eng.tensor_copy(ed_b[:, :, :], part(1)))
                        do(eng.tensor_tensor(ed[:, :, :], ed[:, :, :], ed_b[:, :, :], ALU.subtract))
                        do(eng.tensor_copy(part(2), ed[:, :, :]))
                    if layer in (0, 2):
                        do(eng.tensor_copy(g.recv[:, cols(s)], (tabp if layer == 0 else head)[:, 0:NW]), f"att{s}")
                    at[f"tab{s}"] = do.count
                if layer == 1:
                    do(eng.memset(g.ed[:, NB, :, :], 0.0))

            @block.scalar
            def _(eng):
                eng.wait_ge(vec, at["consts"])
                for s in range(NS):
                    if layer == 0:
                        eng.wait_ge(head_ok, s + 1)
                        if s:
                            eng.wait_ge(out_ok, s)
                        eng.copy(xT2[:, :], head[:, 0:NW]).then_inc(soft_ok, 1)
                        eng.wait_ge(out_ok, s + 1)
                        if s:
                            eng.wait_ge(vec, at[f"out{s - 1}"])
                        softplus_parts(eng, clamp[:, 0:1], outp[:, 0:NW], soft[:, :], parts_ok, 3 * s, clamp[:, 0:1])
                    if layer == 1:
                        eng.wait_ge(head_ok, s + 1)
                        if s:
                            eng.wait_ge(soft_ok, 2 * s)
                        softplus_parts(eng, lift[:, 0:1], head[:, :].rearrange("p (h n) -> p h n", h=2)[:, :, 0:448],
                                       soft[:, :].rearrange("p (h n) -> p h n", h=2),
                                       parts_ok, 3 * s, clamp[:, 0:1])
                    eng.wait_ge(vec, at[f"var{s}"])
                    eng.activation(rstd[:, :], var[:, :], ACT.Ln).then_inc(rstd_ok, 1)
                    eng.wait_ge(rstd_ok, 2 * s + 1)
                    eng.activation(rstd[:, :], rstd[:, :], ACT.Exp, scale=-0.5).then_inc(rstd_ok, 1)
                    if layer < 3:
                        eng.wait_ge(xT_ps, s + 1)
                        if s:
                            eng.wait_ge(tab_ps, s)
                        eng.copy(xT[:, :], xTp[:, 0:NW]).then_inc(xT_ok, 1)

            @block.tensor
            def _(eng):
                def linear(ps, lhs, wt, bias):
                    for b in range(NBG):
                        if bias is not None:
                            eng.matmul(ps[:, node_cols(b)], g.ones_row[:, :], bias[:, :], start=True, stop=False)
                        ins = eng.matmul(ps[:, node_cols(b)], lhs[:, node_cols(b)], wt[:, :], start=bias is None, stop=True)
                    return ins

                eng.wait_ge(weights, 16 * len(loads))
                if layer == 1:
                    eng.wait_ge(vec, at["ones"])
                    eng.matmul(tabp[0:1, 0:F], one_c[:, :], wo2[:, :], start=True, stop=True)
                    eng.matmul(xTp[:, 0:2 * HEADS], wgT[:, :], a_heads[:, :], start=True, stop=True).then_inc(const, 1)
                eng.wait_ge(vec, at["consts"])
                for s in range(NS):
                    if layer == 0:
                        eng.wait_ge(mixed, s + 1)
                        if s:
                            eng.wait_ge(soft_ok, s)
                        for b in range(NBG):
                            ins = eng.transpose(head[:, node_cols(b)], last_rows[:, NBG * s + b, :], g.ident[:, :])
                        ins.then_inc(head_ok, 1)
                        eng.wait_ge(soft_ok, s + 1)
                        if s:
                            eng.wait_ge(vec, at[f"out{s - 1}"])
                        linear(outp, xT2, w3, b3).then_inc(out_ok, 1)
                    elif layer == 1:
                        if s:
                            eng.wait_ge(soft_ok, 2 * s)
                            eng.wait_ge(vec, at[f"att{s - 1}"])
                        for h in range(2):
                            ins = eng.matmul(head[:, 512 * h:512 * h + 448], wo1[:, :], g.acc[:, NW * s + 448 * h:NW * s + 448 * h + 448],
                                             start=True, stop=True)
                        ins.then_inc(head_ok, 1)
                        eng.wait_ge(soft_ok, 2 * s + 2)
                        if s:
                            eng.wait_ge(vec, at[f"out{s - 1}"])
                        linear(outp, xT2, wo2, bo2).then_inc(out_ok, 1)
                    else:
                        if s:
                            eng.wait_ge(vec, at[f"out{s - 1}"])
                        for b in range(NBG):
                            ins = eng.transpose(outp[:, node_cols(b)], g.acc[:, P * (NBG * s + b):P * (NBG * s + b) + P], g.ident[:, :])
                        ins.then_inc(out_ok, 1)
                    if layer == 3:
                        continue
                    eng.wait_ge(vec, at[f"x{s}"])
                    if s:
                        eng.wait_ge(xT_ok, s)
                    for b in range(NBG):
                        ins = eng.transpose(xTp[:, node_cols(b)], g.x[:, NBG * s + b, :], g.ident[:, :])
                    ins.then_inc(xT_ps, 1)
                    eng.wait_ge(xT_ok, s + 1)
                    if s:
                        eng.wait_ge(vec, at[f"tab{s - 1}"])
                    if layer == 0:
                        linear(tabp, xT, w_in, b_in).then_inc(tab_ps, 1)
                    elif layer == 1:
                        linear(tabp, xT, wg, None)
                        eng.wait_ge(soft_ok, 2 * s + 2)
                        for b in range(NBG):
                            ins = eng.matmul(head[:, 2 * HEADS * b:2 * HEADS * (b + 1)], xT[:, node_cols(b)], w_att[:, :], start=True, stop=True)
                        ins.then_inc(tab_ps, 1)
                    else:
                        linear(tabp, xT, ws, bse)
                        linear(head, xT, wr, br).then_inc(tab_ps, 1)

            @block.gpsimd
            def _(pool):
                if layer == 0:
                    for b in range(NB):
                        pool.indirect_dma_start(last_rows[:, b, :], None, d["rows"],
                                                bass.IndirectOffsetOnAxis(ap=g.last_edge[:, b:b + 1], axis=0)).then_inc(gathered, 16)
                        pool.indirect_dma_start(g.x[:, b, :], None, d["x"],
                                                bass.IndirectOffsetOnAxis(ap=g.node[:, b:b + 1], axis=0)).then_inc(gathered, 16)
                    return
                table = {1: d["table_heads"], 2: d["table"], 3: d["out"]}[layer]
                for s in range(NS):
                    pool.wait_ge(vec, at[f"x{s}"] if layer == 3 else at[f"tab{s}"])
                    for b in range(NBG):
                        row = g.x[:, NBG * s + b, :] if layer == 3 else tab[:, s % 2, b, :]
                        pool.indirect_dma_start(table, bass.IndirectOffsetOnAxis(ap=g.node[:, NBG * s + b:NBG * s + b + 1], axis=0),
                                                row, None, bounds_check=table.shape[0] - 1, oob_is_err=False).then_inc(sent[s % 2], 16)
                pool.wait_ge(sent[0], 16 * NBG * (NS - NS // 2))
                pool.wait_ge(sent[1], 16 * NBG * (NS // 2))

            @block.sync
            def _(sp):
                for dst, src in loads:
                    sp.dma_start(dst[:, :], src).then_inc(weights, 16)
                if layer == 0:
                    sp.wait_ge(vec, at["zeros"])
                    for table in d["sums"]:
                        sp.dma_start(table.rearrange("(b p) f -> p b f", p=P), bcast(zeros[:, :], 1, NB + 1)).then_inc(cleared, 16)
                    sp.wait_ge(cleared, 16 * NA)


def filter_sums(nc, g, d):
    with ExitStack() as c:
        sb = lambda n, s, t=F32: c.enter_context(nc.sbuf_tensor("fs_" + n, s, t))
        two = lambda n, s, t=F32: [sb(n + "_a", s, t), sb(n + "_b", s, t)]
        sem = phase_semaphores(nc, c, "fs_")
        two_sems = lambda n: [sem(n + "0"), sem(n + "1")]
        K = d["f20"].shape[0]
        wf1, wf2, bf2, clamp, one_c = sb("wf1", [K, F]), sb("wf2", [F, F]), sb("bf2", [1, F]), sb("clamp", [P, 1]), sb("one_c", [P, 1])
        bias3, bias_rows, ones3, bf2_b, power, lower, spare = sb("bias3", [1, 3, 4, F], BF16), sb("bias_rows", [3, 4 * F], BF16), sb("ones3", [3, P], BF16), sb("bf2_b", [1, F]), sb("power", [P, 1]), sb("lower", [P, 1]), sb("spare", [P, 1])
        src_i, src_f = sb("src_i", [P, NT], I32), sb("src_f", [P, NT])
        f20, rel, row, hotT = two("f20", [K, GE]), two("rel", [P, GE], BF16), two("row", [P, GE], I32), two("hotT", [P, 2, GE])
        parts, soft, filt_w, msg, same, total = (sb("parts", [P, GE]), two("soft", [P, GE]), two("filt_w", [P, GE]), two("msg", [P, GE]),
                                                 two("same", [P, GE]), two("total", [P, GE]))
        same_b, power_b = two("same_b", [P, GE], BF16), sb("power_b", [P, 1], BF16)
        wt, cols, first, away, to = two("wt", [P, GT]), two("cols", [P, GT]), sb("first", [P, GT]), sb("away", [P, GT]), two("to", [P, GT], I32)
        weights, vec, shift_ok = sem("weights"), sem("vec"), sem("shift_ok")
        f20_in, rel_in, row_in = two_sems("f20_in"), two_sems("rel_in"), two_sems("row_in")
        z_ok, parts_ok, soft_ok, filt_ok, wt_ok, filt_w_ok, hotT_ok, dst_ok, msg_ok, cols_ok, same_ok, count_ok, idx_mid, total_ps, total_ok, idx_ok, go, same_b_ok = (
            sem(x) for x in ("z_ok", "parts_ok", "soft_ok", "filt_ok", "wt_ok", "filt_w_ok", "hotT_ok", "dst_ok", "msg_ok", "cols_ok",
                             "same_ok", "count_ok", "idx_mid", "total_ps", "total_ok", "idx_ok", "go", "same_b_ok"))
        bias_ok, at = sem("bias_ok"), {}
        added = [sem(f"added{i}") for i in range(GT)]
        z, filt, hd, tot = g.psA, g.psB, g.psC, g.psD
        counts = filt[:, 0:GT]

        with nc.Block() as block:
            @block.vector
            def _(eng):
                do = Chain(eng, vec, at)
                do(eng.memset(clamp[:, :], CLAMP))
                do(eng.memset(one_c[:, :], 1.0))
                do(eng.tensor_scalar(spare[:, :], g.iota_col[:, :], float(NP), None, ALU.add))
                eng.wait_ge(weights, 80)
                do(eng.reciprocal(lower[:, :], power[:, :]))
                eng.wait_ge(shift_ok, 1)
                do(eng.scalar_tensor_tensor(bf2[:, :], filt[0:1, 0:F], -LN2, bf2[:, :], ALU.mult, ALU.add))
                for q in range(3):
                    do(eng.tensor_copy(bias3[:, q, :, :], bcast(bf2[:, :], 1, 4)))
                    do(eng.tensor_copy(bf2_b[:, :], bias3[:, q, 0, :]))
                    do(eng.tensor_tensor(bf2[:, :], bf2[:, :], bf2_b[:, :], ALU.subtract))
                do(eng.memset(ones3[:, :], 1.0))
                do(eng.tensor_copy(src_f[:, :], src_i[:, :]))
                do(eng.tensor_copy(power_b[:, :], power[:, :]), "consts")

                def step(s):
                    if (t := s.ago(1)) is not None:
                        eng.wait_ge(rel_in[t.slot], 16 * (t.pair + 1))
                        wait_pos(eng, dst_ok, t.n - 1)
                        for b, place in enumerate((g.iota_col, g.iota_col2)):
                            eng.tensor_scalar(hotT[t.slot][:, b, :], rel[t.slot][:, :], place[:, 0:1], None, ALU.is_equal).then_inc(hotT_ok, 1)
                        wait_pos(eng, filt_w_ok, t.n - 1)
                        eng.tensor_copy(wt[t.slot][:, :], g.ewT[:, bass.ds(t.n * GT, GT)]).then_inc(wt_ok, 1)
                    if (t := s.ago(2)) is not None:
                        wait_pos(eng, same_ok, t.n)
                        eng.tensor_copy(cols[t.slot][:, :], src_f[:, bass.ds(t.n * GT, GT)]).then_inc(cols_ok, 1)
                        eng.wait_ge(row_in[t.slot], 16 * (t.pair + 1))
                        wait_pos(eng, total_ps, t.n - 1)
                        wait_pos(eng, same_b_ok, t.n - 1)
                        eng.wait_ge(cols_ok, t.n + 1)
                        for k in range(GT):
                            ins = eng.tensor_scalar(same[t.slot][:, P * k:P * k + P], row[t.slot][:, P * k:P * k + P], cols[t.slot][:, k:k + 1], None,
                                                    ALU.is_equal)
                        ins.then_inc(same_ok, 1)
                    if (t := s.ago(3)) is not None:
                        eng.wait_ge(count_ok, t.n + 1)
                        wait_pos(eng, idx_ok, 3 * t.n)
                        eng.tensor_scalar(first[:, :], counts, lower[:, 0:1], 2.5, ALU.mult, ALU.is_lt).then_inc(idx_ok, 1)
                        eng.tensor_scalar(away[:, :], cols[t.slot][:, :], spare[:, 0:1], None, ALU.subtract).then_inc(idx_ok, 1)
                    if (t := s.ago(2)) is not None:
                        eng.wait_ge(filt_w_ok, t.n + 1)
                        eng.wait_ge(dst_ok, t.n + 1)
                        wait_pos(eng, total_ps, t.n - 1)
                        eng.tensor_tensor(msg[t.slot][:, :], hd[:, :], filt_w[t.slot][:, :], ALU.mult).then_inc(msg_ok, 1)
                    if (t := s.ago(3)) is not None:
                        eng.wait_ge(idx_ok, 3 * t.n + 2)
                        for k in range(GT):
                            wait_pos(eng, added[k], 16 * (t.n - 1))
                        eng.tensor_tensor(away[:, :], away[:, :], first[:, :], ALU.mult).then_inc(idx_mid, 1)
                        eng.wait_ge(idx_mid, t.n + 1)
                        eng.tensor_scalar(to[t.slot][:, :], away[:, :], spare[:, 0:1], None, ALU.add).then_inc(idx_ok, 1)
                    if (t := s.ago(0)) is not None:
                        eng.wait_ge(parts_ok, 3 * t.n + 3)
                        wait_pos(eng, filt_ok, t.n - 1)
                        eng.tensor_tensor(soft[t.slot][:, :], z[:, :], parts[:, :], ALU.max).then_inc(soft_ok, 1)
                over_groups(eng, step, 3)

            @block.sync
            def _(sp):
                for dst, src in ((wf1, d["wf1"]), (wf2, d["wf2"]), (bf2, d["bf2"]), (src_i, d["srcT"]), (power, d["power"])):
                    sp.dma_start(dst[:, :], src).then_inc(weights, 16)

                sp.wait_ge(vec, at["consts"])
                for q in range(3):
                    sp.dma_start(bias_rows[q:q + 1, :], bias3[:, q, :, :].rearrange("o k f -> o (k f)")).then_inc(bias_ok, 16)

                def step(s):
                    if (t := s.ago(0)) is not None:
                        wait_pos(sp, hotT_ok, 2 * (t.n - 1))
                        wait_pos(sp, z_ok, t.n - 1)
                        sp.dma_start(f20[t.slot][:, :], d["f20"][:, bass.ds(t.n * GE, GE)]).then_inc(f20_in[t.slot], 16)
                        sp.dma_start(rel[t.slot][:, :], bcast(d["rel"][bass.ds(t.n * GE, GE)], 0, P)).then_inc(rel_in[t.slot], 16)
                        wait_pos(sp, same_ok, t.n - 1)
                        sp.dma_start(row[t.slot][:, :], bcast(d["src"][bass.ds(t.n * GE, GE)], 0, P)).then_inc(row_in[t.slot], 16)
                over_groups(sp, step, 0)

            @block.gpsimd
            def _(pool):
                def step(s):
                    if (t := s.ago(4)) is not None:
                        pool.wait_ge(idx_ok, 3 * t.n + 3)
                        pool.wait_ge(total_ok, t.n + 1)
                        for k in range(GT):
                            wait_pos(pool, added[k], 16 * t.n)
                            pool.sem_inc(go, 1)
                            pool.indirect_dma_start(d["sums"][k % NA], bass.IndirectOffsetOnAxis(ap=to[t.slot][:, k:k + 1], axis=0),
                                                    total[t.slot][:, P * k:P * k + P], None, bounds_check=NP + P - 1,
                                                    compute_op=ALU.add).then_inc(added[k], 16)
                over_groups(pool, step, 4)
                for sem_k in added:
                    pool.wait_ge(sem_k, 16 * NG)

            @block.scalar
            def _(eng):
                eng.wait_ge(vec, 1)

                def step(s):
                    if (t := s.ago(4)) is not None:
                        eng.wait_ge(total_ps, t.n + 1)
                        for k in range(GT):
                            wait_pos(eng, added[k], 16 * (t.n - 1))
                        eng.copy(total[t.slot][:, :], tot[:, :]).then_inc(total_ok, 1)
                    if (t := s.ago(2)) is not None:
                        eng.wait_ge(filt_ok, t.n + 1)
                        eng.wait_ge(wt_ok, t.n + 1)
                        wait_pos(eng, msg_ok, t.n - 1)
                        for k in range(GT):
                            ins = eng.activation(filt_w[t.slot][:, P * k:P * k + P], filt[:, P * k:P * k + P], ACT.Copy, scale=wt[t.slot][:, k:k + 1])
                        ins.then_inc(filt_w_ok, 1)
                        eng.wait_ge(same_ok, t.n + 1)
                        wait_pos(eng, count_ok, t.n - 1)
                        eng.copy(same_b[t.slot][:, :], same[t.slot][:, :]).then_inc(same_b_ok, 1)
                    if (t := s.ago(0)) is not None:
                        eng.wait_ge(z_ok, t.n + 1)
                        wait_pos(eng, soft_ok, t.n)
                        softplus_parts(eng, clamp[:, 0:1], z[:, :], parts[:, :], parts_ok, 3 * t.n, clamp[:, 0:1])
                over_groups(eng, step, 4)

            @block.tensor
            def _(eng):
                eng.wait_ge(weights, 80)
                eng.wait_ge(vec, 2)
                eng.matmul(filt[0:1, 0:F], one_c[:, :], wf2[:, :], start=True, stop=True).then_inc(shift_ok, 1)
                eng.wait_ge(bias_ok, 48)

                def step(s):
                    if (t := s.ago(2)) is not None:
                        block0 = load_ints(nc, PE, g.block0, t.n, NB - 1)
                        eng.wait_ge(hotT_ok, 2 * t.n + 2)
                        wait_pos(eng, msg_ok, t.n)
                        expand_destination(eng, hd, hotT[t.slot], g.recv, block0).then_inc(dst_ok, 1)
                    if (t := s.ago(0)) is not None:
                        eng.wait_ge(f20_in[t.slot], 16 * (t.pair + 1))
                        wait_pos(eng, soft_ok, t.n)
                        for h in range(2):
                            ins = eng.matmul(psum_half(z, h), wf1[:, :], f20[t.slot][:, 512 * h:512 * h + 512], start=True, stop=True)
                        ins.then_inc(z_ok, 1)
                    if (t := s.ago(3)) is not None:
                        eng.wait_ge(same_b_ok, t.n + 1)
                        eng.wait_ge(filt_w_ok, (s.ago(2) or t).n + 1)
                        wait_pos(eng, idx_ok, 3 * t.n)
                        for k in range(GT):
                            ins = eng.matmul(counts[:, k:k + 1], same_b[t.slot][:, P * k:P * k + P], power_b[:, :], start=True, stop=True)
                        ins.then_inc(count_ok, 1)
                        eng.wait_ge(msg_ok, t.n + 1)
                        wait_pos(eng, total_ok, t.n)
                        for k in range(GT):
                            ins = eng.matmul(tot[:, P * k:P * k + P], same[t.slot][:, P * k:P * k + P], msg[t.slot][:, P * k:P * k + P],
                                             start=True, stop=True)
                        ins.then_inc(total_ps, 1)
                    if (t := s.ago(1)) is not None:
                        eng.wait_ge(soft_ok, t.n + 1)
                        wait_pos(eng, idx_ok, 3 * (t.n - 1))
                        wait_pos(eng, filt_w_ok, t.n)
                        for h in range(2):
                            eng.matmul(psum_half(filt, h), ones3[:, :], bias_rows[:, :], start=True, stop=False)
                            for k in range(4 * h, 4 * h + 4):
                                ins = eng.matmul(filt[:, P * k:P * k + P], soft[t.slot][:, P * k:P * k + P], wf2[:, :],
                                                 start=False, stop=(k % 4 == 3))
                        ins.then_inc(filt_ok, 1)
                over_groups(eng, step, 3)


def collect_sums(nc, g, d):
    with ExitStack() as c:
        sb = lambda n, s, t=F32: c.enter_context(nc.sbuf_tensor("cs_" + n, s, t))
        sem = phase_semaphores(nc, c, "cs_")
        parts, got = [sb(f"parts{i}", [P, NA, NW]) for i in range(2)], [sb(f"got{i}", [P, NBG, F]) for i in range(2)]
        loaded, stored = [sem("loaded0"), sem("loaded1")], sem("stored")
        summed, turned, copied = (sem(x) for x in ("summed", "turned", "copied"))
        gathered = [sem("gathered0"), sem("gathered1")]
        ps = [g.psA, g.psB]
        node_rows = lambda t, s: t[NW * s:NW * s + NW, :].rearrange("(b p) f -> p b f", p=P)

        with nc.Block() as block:
            @block.sync
            def _(sp):
                for s in range(NS + 1):
                    if s < NS:
                        if s > 1:
                            sp.wait_ge(stored, 16 * (s - 1))
                        for a in range(NA):
                            sp.dma_start(parts[s % 2][:, a, :].rearrange("p (b f) -> p b f", f=F), node_rows(d["sums"][a], s)).then_inc(loaded[s % 2], 16)
                    if s:
                        sp.wait_ge(summed, (NA - 1) * s)
                        sp.dma_start(node_rows(d["table"], s - 1), parts[(s - 1) % 2][:, 0, :].rearrange("p (b f) -> p b f", f=F)).then_inc(stored, 16)

            @block.vector
            def _(eng):
                done = 0
                for s in range(NS):
                    eng.wait_ge(loaded[s % 2], 16 * NA * (s // 2 + 1))
                    for a in range(1, NA):
                        eng.tensor_tensor(parts[s % 2][:, 0, :], parts[s % 2][:, 0, :], parts[s % 2][:, a, :], ALU.add).then_inc(summed, 1)
                        done += 1
                        eng.wait_ge(summed, done)

            @block.gpsimd
            def _(pool):
                pool.wait_ge(stored, 16 * NS)
                for s in range(NS):
                    if s > 1:
                        pool.wait_ge(turned, s - 1)
                    for b in range(NBG):
                        node = g.node[:, NBG * s + b:NBG * s + b + 1]
                        pool.indirect_dma_start(got[s % 2][:, b, :], None, d["table"], bass.IndirectOffsetOnAxis(ap=node, axis=0)).then_inc(gathered[s % 2], 16)

            @block.tensor
            def _(eng):
                for s in range(NS):
                    eng.wait_ge(gathered[s % 2], 16 * NBG * (s // 2 + 1))
                    if s > 1:
                        eng.wait_ge(copied, s - 1)
                    for b in range(NBG):
                        ins = eng.transpose(ps[s % 2][:, node_cols(b)], got[s % 2][:, b, :], g.ident[:, :])
                    ins.then_inc(turned, 1)

            @block.scalar
            def _(eng):
                for s in range(NS):
                    eng.wait_ge(turned, s + 1)
                    eng.copy(g.acc[:, NW * s:NW * s + NW], ps[s % 2][:, 0:NW]).then_inc(copied, 1)


def attention_scores(nc, g, d):
    with ExitStack() as c:
        sb = lambda n, s, t=F32: c.enter_context(nc.sbuf_tensor("as_" + n, s, t))
        two = lambda n, s, t=F32: [sb(n + "_a", s, t), sb(n + "_b", s, t)]
        sem = phase_semaphores(nc, c, "as_")
        two_sems = lambda n: [sem(n + "0"), sem(n + "1")]
        W = F + HEADS
        idx, G, rel, hotT = two("idx", [P, GT], I32), two("G", [P, GT * W]), two("rel", [P, GE], BF16), two("hotT", [P, 2, GE], BF16)
        dst_s, e = sb("dst_s", [P, GT, HEADS]), sb("e", [P, GT, HEADS])
        idx_in, rel_in, G_in, stored = (two_sems(x) for x in ("idx_in", "rel_in", "G_in", "stored"))
        go, hotT_ok, ed_ok, dst_ok, e_ok, score_ok = (sem(x) for x in ("go", "hotT_ok", "ed_ok", "dst_ok", "e_ok", "score_ok"))
        parts = g.psA[:, 0:GT * 3 * HEADS]

        with nc.Block() as block:
            @block.sync
            def _(sp):
                def step(s):
                    if (t := s.ago(0)) is not None:
                        wait_pos(sp, G_in[t.slot], 16 * GT * t.pair)
                        sp.dma_start(idx[t.slot][:, :], d["srcG"][bass.ds(t.n, 1)].rearrange("o p k -> (o p) k")).then_inc(idx_in[t.slot], 16)
                    if (t := s.ago(1)) is not None:
                        sp.wait_ge(G_in[t.slot], 16 * GT * (t.pair + 1))
                        sp.dma_start(d["rows"][bass.ds(t.n * GE, GE), :].rearrange("(k p) f -> p k f", p=P),
                                     G[t.slot][:, :].rearrange("p (k w) -> p k w", w=W)[:, :, 0:F]).then_inc(stored[t.slot], 16)
                over_groups(sp, step, 1)
                for s in stored:
                    sp.wait_ge(s, 16 * (NG // 2))

            @block.scalar
            def _(eng):
                def step(s):
                    if (t := s.ago(0)) is not None:
                        wait_pos(eng, hotT_ok, 2 * (t.n - 1))
                        eng.dma_start(rel[t.slot][:, :], bcast(d["rel"][bass.ds(t.n * GE, GE)], 0, P)).then_inc(rel_in[t.slot], 16)
                over_groups(eng, step, 0)

            @block.gpsimd
            def _(pool):
                def step(s):
                    if (t := s.ago(0)) is not None:
                        gather_group(pool, t, d["table_heads"], idx, G, idx_in, [(e_ok, t.n - 1), (stored[t.slot], 16 * t.pair)], go, G_in)
                over_groups(pool, step, 0)

            @block.tensor
            def _(eng):
                def step(s):
                    if (t := s.ago(2)) is not None:
                        block0 = load_ints(nc, PE, g.block0, t.n, NB - 1)
                        eng.wait_ge(hotT_ok, 2 * t.n + 2)
                        wait_pos(eng, dst_ok, t.n)
                        for k in range(GT):
                            for b in range(2):
                                ins = eng.matmul(parts[:, 12 * k:12 * k + 12], hotT[t.slot][:, b, P * k:P * k + P],
                                                 g.ed[:, :, :, :].rearrange("p b k h -> p (b k h)")[:, bass.ds(block0[k] * 12 + 12 * b, 12)],
                                                 start=(b == 0), stop=(b == 1))
                        ins.then_inc(ed_ok, 1)
                over_groups(eng, step, 2)

            @block.vector
            def _(eng):
                def step(s):
                    if (t := s.ago(1)) is not None:
                        eng.wait_ge(rel_in[t.slot], 16 * (t.pair + 1))
                        wait_pos(eng, ed_ok, t.n - 1)
                        for b, place in enumerate((g.iota_col, g.iota_col2)):
                            eng.tensor_scalar(hotT[t.slot][:, b, :], rel[t.slot][:, :], place[:, 0:1], None, ALU.is_equal).then_inc(hotT_ok, 1)
                    if (t := s.ago(3)) is not None:
                        eng.wait_ge(ed_ok, t.n + 1)
                        wait_pos(eng, e_ok, t.n)
                        eng.tensor_reduce(dst_s[:, :, :], parts.rearrange("p (k q h) -> p k h q", q=3, h=HEADS), AX.X, ALU.add).then_inc(dst_ok, 1)
                        eng.wait_ge(dst_ok, t.n + 1)
                        eng.wait_ge(G_in[t.slot], 16 * GT * (t.pair + 1))
                        wait_pos(eng, score_ok, t.n)
                        eng.tensor_tensor(e[:, :, :], dst_s[:, :, :], G[t.slot][:, :].rearrange("p (k w) -> p k w", w=W)[:, :, F:W], ALU.add).then_inc(e_ok, 1)
                        eng.wait_ge(e_ok, t.n + 1)
                        eng.scalar_tensor_tensor(g.scores[:, bass.ds(t.n * GT, GT), :], e[:, :, :], SLOPE, e[:, :, :], ALU.mult, ALU.max).then_inc(score_ok, 1)
                over_groups(eng, step, 3)


def edge_attention(nc, g, d):
    with ExitStack() as c:
        sb = lambda n, s, t=F32: c.enter_context(nc.sbuf_tensor("ea_" + n, s, t))
        two = lambda n, s, t=F32: [sb(n + "_a", s, t), sb(n + "_b", s, t)]
        sem = phase_semaphores(nc, c, "ea_")
        two_sems = lambda n: [sem(n + "0"), sem(n + "1")]
        we, aw, ab, clamp = sb("we", [F, F]), sb("aw", [P, F]), sb("ab", [P, 1]), sb("clamp", [P, 1])
        idx, ef, G, rel, hotT = two("idx", [P, GT], I32), two("ef", [P, GE]), two("G", [P, GE]), two("rel", [P, GE], BF16), two("hotT", [P, 2, GE])
        att, X, rr, Y, lg = two("att", [P, GE]), two("X", [P, GE]), two("rr", [P, GE]), sb("Y", [P, GE]), sb("lg", [P, GT * HEADS])
        weights, vec = sem("weights"), sem("vec")
        idx_in, ef_in, rel_in, G_in, stored = (two_sems(x) for x in ("idx_in", "ef_in", "rel_in", "G_in", "stored"))
        go, proj_ok, att_ok, hotT_ok, recv_ok, X_ok, mish_ok, Y_ok, Yw_ok, lg_ok, score_ok = (
            sem(x) for x in ("go", "proj_ok", "att_ok", "hotT_ok", "recv_ok", "X_ok", "mish_ok", "Y_ok", "Yw_ok", "lg_ok", "score_ok"))
        proj, recv = [g.psA, g.psB], [g.psC, g.psD]

        with nc.Block() as block:
            @block.sync
            def _(sp):
                sp.dma_start(we[:, :], d["we"]).then_inc(weights, 16)
                sp.dma_start(aw[:, :], d["aw"].broadcast_to([P, F])).then_inc(weights, 16)
                sp.dma_start(ab[:, :], d["ab"].broadcast_to([P, 1])).then_inc(weights, 16)

                def step(s):
                    if (t := s.ago(0)) is not None:
                        wait_pos(sp, G_in[t.slot], 16 * GT * t.pair)
                        sp.dma_start(idx[t.slot][:, :], d["srcG"][bass.ds(t.n, 1)].rearrange("o p k -> (o p) k")).then_inc(idx_in[t.slot], 16)
                        wait_pos(sp, hotT_ok, 2 * (t.n - 1))
                        wait_pos(sp, proj_ok, t.n - 1)
                        sp.dma_start(ef[t.slot][:, :], d["ef"][:, bass.ds(t.n * GE, GE)]).then_inc(ef_in[t.slot], 16)
                        sp.dma_start(rel[t.slot][:, :], bcast(d["rel"][bass.ds(t.n * GE, GE)], 0, P)).then_inc(rel_in[t.slot], 16)
                    if (t := s.ago(3)) is not None:
                        sp.wait_ge(att_ok, t.n + 1)
                        sp.dma_start(d["rows"][bass.ds(t.n * GE, GE), :].rearrange("(k p) f -> p k f", p=P),
                                     att[t.slot][:, :].rearrange("p (k f) -> p k f", f=F)).then_inc(stored[t.slot], 16)
                over_groups(sp, step, 3)
                for s in stored:
                    sp.wait_ge(s, 16 * (NG // 2))

            @block.gpsimd
            def _(pool):
                def step(s):
                    if (t := s.ago(0)) is not None:
                        gather_group(pool, t, d["table"], idx, G, idx_in, [(att_ok, t.n - 1)], go, G_in)
                over_groups(pool, step, 0)

            @block.tensor
            def _(eng):
                eng.wait_ge(weights, 48)

                def step(s):
                    if (t := s.ago(2)) is not None:
                        block0 = load_ints(nc, PE, g.block0, t.n, NB - 1)
                    if (u := s.ago(1)) is not None:
                        eng.wait_ge(ef_in[u.slot], 16 * (u.pair + 1))
                        wait_pos(eng, att_ok, u.n - 1)
                        for k in range(GT):
                            ins = eng.matmul(proj[u.slot][:, P * k:P * k + P], ef[u.slot][:, P * k:P * k + P], we[:, :], start=True, stop=True)
                        ins.then_inc(proj_ok, 1)
                    if t is not None:
                        eng.wait_ge(hotT_ok, 2 * t.n + 2)
                        wait_pos(eng, X_ok, t.n - 1)
                        expand_destination(eng, recv[t.slot], hotT[t.slot], g.recv, block0).then_inc(recv_ok, 1)
                over_groups(eng, step, 2)

            @block.scalar
            def _(eng):
                eng.wait_ge(vec, 1)

                def step(s):
                    if (t := s.ago(3)) is not None:
                        r = rr[t.slot][:, :]
                        eng.wait_ge(X_ok, t.n + 1)
                        wait_pos(eng, Y_ok, t.n - 1)
                        eng.activation(r, X[t.slot][:, :], ACT.Relu, bias=clamp[:, 0:1], scale=-1.0).then_inc(mish_ok, 1)
                        eng.wait_ge(mish_ok, 5 * t.n + 1)
                        eng.activation(r, r, ACT.Exp, bias=clamp[:, 0:1], scale=-1.0).then_inc(mish_ok, 1)
                        eng.wait_ge(mish_ok, 5 * t.n + 2)
                        eng.activation(r, r, ACT.Square, bias=1.0).then_inc(mish_ok, 1)
                        eng.wait_ge(mish_ok, 5 * t.n + 3)
                        eng.activation(r, r, ACT.Ln, bias=1.0).then_inc(mish_ok, 1)
                        eng.wait_ge(mish_ok, 5 * t.n + 4)
                        eng.activation(r, r, ACT.Exp, scale=-1.0).then_inc(mish_ok, 1)
                over_groups(eng, step, 3)

            @block.vector
            def _(eng):
                eng.memset(clamp[:, :], MISH_CLAMP).then_inc(vec, 1)
                eng.wait_ge(weights, 48)
                eng.tensor_scalar(aw[:, :], aw[:, :], -2.0, None, ALU.mult).then_inc(vec, 1)
                eng.wait_ge(vec, 2)

                def step(s):
                    if (t := s.ago(2)) is not None:
                        eng.wait_ge(proj_ok, t.n + 1)
                        eng.wait_ge(G_in[t.slot], 16 * GT * (t.pair + 1))
                        wait_pos(eng, stored[t.slot], 16 * t.pair)
                        wait_pos(eng, X_ok, t.n - 1)
                        eng.tensor_tensor(att[t.slot][:, :], proj[t.slot][:, :], G[t.slot][:, :], ALU.add).then_inc(att_ok, 1)
                    if (t := s.ago(3)) is not None:
                        eng.wait_ge(recv_ok, t.n + 1)
                        eng.wait_ge(att_ok, t.n + 1)
                        wait_pos(eng, Y_ok, t.n - 1)
                        wait_pos(eng, mish_ok, 5 * (t.n - 1))
                        eng.tensor_tensor(X[t.slot][:, :], recv[t.slot][:, :], att[t.slot][:, :], ALU.add).then_inc(X_ok, 1)
                    if (t := s.ago(1)) is not None:
                        eng.wait_ge(rel_in[t.slot], 16 * (t.pair + 1))
                        wait_pos(eng, recv_ok, t.n - 1)
                        for b, place in enumerate((g.iota_col, g.iota_col2)):
                            eng.tensor_scalar(hotT[t.slot][:, b, :], rel[t.slot][:, :], place[:, 0:1], None, ALU.is_equal).then_inc(hotT_ok, 1)
                    if (t := s.ago(4)) is not None:
                        eng.wait_ge(mish_ok, 5 * t.n + 5)
                        wait_pos(eng, lg_ok, t.n)
                        eng.scalar_tensor_tensor(Y[:, :], rr[t.slot][:, :], -0.5, X[t.slot][:, :], ALU.add, ALU.mult).then_inc(Y_ok, 1)
                        eng.wait_ge(Y_ok, t.n + 1)
                        heads = Y[:, :].rearrange("p (k f) -> p k f", f=F)
                        eng.tensor_tensor(heads, heads, bcast(aw[:, :], 1, GT), ALU.mult).then_inc(Yw_ok, 1)
                        eng.wait_ge(Yw_ok, t.n + 1)
                        wait_pos(eng, score_ok, t.n)
                        eng.tensor_reduce(lg[:, :], Y[:, :].rearrange("p (k f) -> p k f", f=HD), AX.X, ALU.add).then_inc(lg_ok, 1)
                        eng.wait_ge(lg_ok, t.n + 1)
                        eng.tensor_scalar(g.scores[:, bass.ds(t.n * GT, GT), :], lg[:, :].rearrange("p (k h) -> p k h", h=HEADS), ab[:, 0:1], None,
                                          ALU.add).then_inc(score_ok, 1)
                over_groups(eng, step, 4)


def segment_softmax(nc, g, d, layer):
    with ExitStack() as c:
        sb = lambda n, s, t=F32: c.enter_context(nc.sbuf_tensor(f"sm{layer}_{n}", s, t))
        sem = phase_semaphores(nc, c, f"sm{layer}_")
        vec, turned, stage_ok, stored, fetched, exp_ok, ends_t, chain_t, half_ok = (
            sem(x) for x in ("vec", "turned", "stage_ok", "stored", "fetched", "exp_ok", "ends_t", "chain_t", "half_ok"))
        stage = sb("stage", [SEGC, HEADS, SEGN, P])
        L, A, B = (sb(x, [P, HEADS, PB]) for x in ("L", "A", "B"))
        ends, chain, chain2 = sb("ends", [P, HEADS]), sb("chain", [HEADS, P]), sb("chain2", [HEADS, P])
        carry = sb("carry", [P, HEADS])
        at = {}
        rows = lambda t: t.rearrange("h (k t p) -> t h k p", t=SEGC, p=P)
        seg_ps = [g.psA, g.psB, g.psC, g.psD]
        n_small = [0]

        with nc.Block() as block:
            @block.vector
            def _(eng):
                do = Chain(eng, vec, at)

                def carried(kind, backward):
                    i = n_small[0]
                    n_small[0] += 1
                    at[f"ends{i}"] = do.count
                    eng.wait_ge(ends_t, i + 1)
                    mask = g.chain_mask[:, {"max": 0, "sum": 1, "spread": 2}[kind], :]
                    one = g.psD[0:HEADS, 896:1024]
                    do(eng.tensor_copy(chain2[:, :], one))
                    if kind == "max":
                        do(eng.tensor_tensor_scan(chain[:, :], mask, chain2[:, :], -BIG, ALU.add, ALU.max))
                    elif not backward:
                        do(eng.tensor_tensor_scan(chain[:, :], mask, chain2[:, :], 0.0, ALU.mult, ALU.add))
                    else:
                        do(eng.tensor_tensor_scan(chain[:, ::-1], mask[:, ::-1], chain2[:, ::-1], 0.0, ALU.mult, ALU.add))
                    if backward:
                        do(eng.tensor_copy(chain2[:, 0:P - 1], chain[:, 1:P]))
                        do(eng.memset(chain2[:, P - 1:P], 0.0), f"chain{i}")
                    else:
                        do(eng.tensor_copy(chain2[:, 1:P], chain[:, 0:P - 1]))
                        do(eng.memset(chain2[:, 0:1], -BIG if kind == "max" else 0.0), f"chain{i}")
                    eng.wait_ge(chain_t, i + 1)
                    do(eng.tensor_copy(carry[:, :], g.psC[:, 896:896 + HEADS]))

                def over_destination(kind, src, tmp):
                    for h in range(HEADS):
                        if kind == "max":
                            do(eng.tensor_tensor_scan(tmp[:, h, :], g.reset[:, :], src[:, h, :], -BIG, ALU.add, ALU.max))
                        else:
                            do(eng.tensor_tensor_scan(tmp[:, h, :], g.keep_s[:, :], src[:, h, :], 0.0, ALU.mult, ALU.add))
                    do(eng.tensor_copy(ends[:, :], tmp[:, :, PB - 1]))
                    carried(kind, False)
                    for h in range(HEADS):
                        if kind == "max":
                            do(eng.scalar_tensor_tensor(tmp[:, h, :], g.pre_neg[:, :], carry[:, h:h + 1], tmp[:, h, :], ALU.add, ALU.max))
                        else:
                            do(eng.scalar_tensor_tensor(tmp[:, h, :], g.pre[:, :], carry[:, h:h + 1], tmp[:, h, :], ALU.mult, ALU.add))
                    do(eng.tensor_tensor(tmp[:, :, :], tmp[:, :, :], bcast(g.last[:, :], 1, HEADS), ALU.mult))
                    for h in range(HEADS):
                        do(eng.tensor_tensor_scan(tmp[:, h, ::-1], g.keep_l[:, ::-1], tmp[:, h, ::-1], 0.0, ALU.mult, ALU.add))
                    do(eng.tensor_copy(ends[:, :], tmp[:, :, 0]))
                    carried("spread", True)
                    for h in range(HEADS):
                        do(eng.scalar_tensor_tensor(tmp[:, h, :], g.suf[:, :], carry[:, h:h + 1], tmp[:, h, :], ALU.mult, ALU.add))

                eng.wait_ge(fetched, 16)
                over_destination("max", L, A)
                if layer == 2:
                    do(eng.tensor_scalar(A[:, :, :], A[:, :, :], 0.0, None, ALU.max))
                do(eng.tensor_tensor(L[:, :, :], L[:, :, :], A[:, :, :], ALU.subtract), "shifted")
                eng.wait_ge(exp_ok, 1)
                over_destination("sum", L, A)
                if layer == 2:
                    do(eng.tensor_scalar(A[:, :, :], A[:, :, :], ALPHA_EPS, None, ALU.add))
                do(eng.reciprocal(A[:, :, :], A[:, :, :]))
                do(eng.tensor_tensor(L[:, :, :], L[:, :, :], A[:, :, :], ALU.mult), "alpha")

            @block.tensor
            def _(eng):
                for h in range(HEADS):
                    for k in range(SEGN):
                        ins = eng.transpose(seg_ps[h][0:SEGC, P * k:P * k + P], g.scores[:, SEGC * k:SEGC * (k + 1), h], g.ident[:, :])
                    ins.then_inc(turned, 1)
                for i in range(4):
                    eng.wait_ge(vec, at[f"ends{i}"])
                    if i == 0:
                        eng.wait_ge(stage_ok, 4)
                    eng.transpose(g.psD[0:HEADS, 896:1024], ends[:, :], g.ident[:, :]).then_inc(ends_t, 1)
                    eng.wait_ge(vec, at[f"chain{i}"])
                    eng.transpose(g.psC[:, 896:896 + HEADS], chain2[:, :], g.ident[0:HEADS, 0:HEADS]).then_inc(chain_t, 1)
                eng.wait_ge(fetched, 32)
                for h in range(HEADS):
                    for k in range(SEGN):
                        ins = eng.transpose(seg_ps[h][:, P * k:P * k + SEGC], stage[:, h, k, :], g.ident[0:SEGC, 0:SEGC])
                    ins.then_inc(turned, 1)

            @block.scalar
            def _(eng):
                for h in range(HEADS):
                    eng.wait_ge(turned, h + 1)
                    eng.copy(stage[:, h, :, :], seg_ps[h][0:SEGC, 0:SEGN * P].rearrange("t (k p) -> t k p", p=P)).then_inc(stage_ok, 1)
                eng.wait_ge(vec, at["shifted"])
                eng.activation(L[:, :, :], L[:, :, :], ACT.Exp).then_inc(exp_ok, 1)
                for h in range(HEADS):
                    eng.wait_ge(turned, HEADS + h + 1)
                    eng.copy(g.scores[:, :, h].rearrange("p (k t) -> p k t", t=SEGC),
                             seg_ps[h][:, 0:SEGN * P].rearrange("p (k t) -> p k t", t=P)[:, :, 0:SEGC]).then_inc(stage_ok, 1)

            @block.sync
            def _(sp):
                sp.wait_ge(stage_ok, 4)
                for h in range(HEADS):
                    sp.dma_start(rows(d["logits"])[:, h], stage[:, h, :, :]).then_inc(stored, 16)
                sp.wait_ge(stored, 64)
                sp.dma_start(L[:, :, :], d["logits"].rearrange("h (q j) -> q h j", q=P)).then_inc(fetched, 16)
                sp.wait_ge(vec, at["alpha"])
                sp.dma_start(d["alpha"].rearrange("h (q j) -> q h j", q=P), L[:, :, :]).then_inc(half_ok, 16)
                sp.wait_ge(half_ok, 16)
                for h in range(HEADS):
                    sp.dma_start(stage[:, h, :, :], rows(d["alpha"])[:, h]).then_inc(half_ok, 16)
                sp.wait_ge(half_ok, 80)
                sp.sem_inc(fetched, 16)


def weighted_sums(nc, g, d, layer):
    with ExitStack() as c:
        sb = lambda n, s, t=F32: c.enter_context(nc.sbuf_tensor(f"ws{layer}_{n}", s, t))
        two = lambda n, s, t=F32: [sb(n + "_a", s, t), sb(n + "_b", s, t)]
        sem = phase_semaphores(nc, c, f"ws{layer}_")
        V, msg, hot, lr = two("V", [P, GE]), two("msg", [P, GE]), two("hot", [P, GE]), two("lr", [P, GT])
        acc_b, away = sb("acc_b", [P, RW]), sb("away", [P, GE])
        V_in = [sem("V_in0"), sem("V_in1")]
        cleared, msg_ok, cols_ok, away_ok, hot_ok, win_ok, added = (
            sem(x) for x in ("cleared", "msg_ok", "cols_ok", "away_ok", "hot_ok", "win_ok", "added"))
        win = [g.psA, g.psB]

        with nc.Block() as block:
            @block.sync
            def _(sp):
                def step(s):
                    if (t := s.ago(0)) is not None:
                        wait_pos(sp, msg_ok, t.n - 1)
                        sp.dma_start(V[t.slot][:, :].rearrange("p (k f) -> p k f", f=F),
                                     d["rows"][bass.ds(t.n * GE, GE), :].rearrange("(k p) f -> p k f", p=P)).then_inc(V_in[t.slot], 16)
                over_groups(sp, step, 0)

            @block.tensor
            def _(eng):
                def step(s):
                    if (t := s.ago(1)) is not None:
                        eng.wait_ge(msg_ok, t.n + 1)
                        eng.wait_ge(hot_ok, t.n + 1)
                        wait_pos(eng, added, (t.n - 1) * GT)
                        for k in range(GT):
                            ins = eng.matmul(win[t.slot][:, P * k:P * k + P], msg[t.slot][:, P * k:P * k + P], hot[t.slot][:, P * k:P * k + P],
                                             start=True, stop=True)
                        ins.then_inc(win_ok, 1)
                over_groups(eng, step, 1)

            @block.scalar
            def _(eng):
                def step(s):
                    if (t := s.ago(0)) is not None:
                        eng.wait_ge(cols_ok, t.n + 1)
                        wait_pos(eng, hot_ok, t.n)
                        for k in range(GT):
                            ins = eng.activation(away[:, P * k:P * k + P], g.iota_row[:, :], ACT.Square, bias=lr[t.slot][:, k:k + 1], scale=-1.0)
                        ins.then_inc(away_ok, 1)
                        eng.wait_ge(away_ok, t.n + 1)
                        wait_pos(eng, win_ok, t.n - 1)
                        eng.activation(hot[t.slot][:, :], away[:, :], ACT.Relu, bias=1.0, scale=-1.0).then_inc(hot_ok, 1)
                over_groups(eng, step, 0)

            @block.vector
            def _(eng):
                eng.memset(g.acc[:, :], 0.0).then_inc(cleared, 1)
                eng.memset(acc_b[:, :], 0.0).then_inc(cleared, 1)
                eng.wait_ge(cleared, 2)

                def step(s):
                    if (old := s.ago(2)) is not None:
                        rank0 = load_ints(nc, DVE, g.rank0, old.n, N)
                    if (t := s.ago(0)) is not None:
                        wait_pos(eng, away_ok, t.n - 1)
                        eng.tensor_copy(lr[t.slot][:, :], g.lr[:, bass.ds(t.n * GT, GT)]).then_inc(cols_ok, 1)
                        eng.wait_ge(V_in[t.slot], 16 * (t.pair + 1))
                        wait_pos(eng, win_ok, t.n - 1)
                        eng.tensor_tensor(msg[t.slot][:, :].rearrange("p (k h f) -> p (k h) f", h=HEADS, f=HD),
                                          V[t.slot][:, :].rearrange("p (k h f) -> p (k h) f", h=HEADS, f=HD),
                                          bcast(g.scores[:, bass.ds(t.n * GT, GT), :].rearrange("p k h -> p (k h)"), 2, HD), ALU.mult).then_inc(msg_ok, 1)
                    if old is not None:
                        eng.wait_ge(win_ok, old.n + 1)
                        for k in range(GT):
                            sums, cols = (g.acc, acc_b)[k % 2], bass.ds(rank0[k], P)
                            wait_pos(eng, added, old.n * GT + k - 1)
                            eng.tensor_tensor(sums[:, cols], sums[:, cols], win[old.slot][:, P * k:P * k + P], ALU.add).then_inc(added, 1)
                over_groups(eng, step, 2)
                eng.wait_ge(added, NT)
                eng.tensor_tensor(g.acc[:, :], g.acc[:, :], acc_b[:, :], ALU.add).then_inc(cleared, 1)


def program(nc, d):
    with ExitStack() as c:
        sb = lambda n, s, t=F32: c.enter_context(nc.sbuf_tensor(n, s, t))
        g = Shared()
        g.psA, g.psB, g.psC, g.psD = (c.enter_context(nc.psum_tensor(n, [P, 1024], F32)) for n in ("psA", "psB", "psC", "psD"))
        g.iota_row, g.iota_col, g.iota_col2 = sb("iota_row", [P, P]), sb("iota_col", [P, 1]), sb("iota_col2", [P, 1])
        g.ident, g.ones_row = sb("ident", [P, P]), sb("ones_row", [1, P])
        g.ewT, g.lr, g.cut = sb("ewT_sb", [P, NT]), sb("lr", [P, NT]), sb("cut", [P, NT])
        g.rank0, g.block0 = sb("rank0", [1, NT], I32), sb("block0", [1, NT], I32)
        g.last_edge, g.node, g.has_edge = sb("last_edge", [P, NB], I32), sb("node", [P, NB], I32), sb("has_edge", [P, NB])
        g.last, g.reset, g.keep_s, g.keep_l = (sb(x, [P, PB]) for x in ("last", "reset", "keep_s", "keep_l"))
        g.pre, g.pre_neg, g.suf = (sb(x, [P, PB]) for x in ("pre", "pre_neg", "suf"))
        g.chain_mask = sb("chain_mask", [HEADS, 3, P])
        g.x = sb("x_sb", [P, NB, F])
        setup(nc, g, d)
        scan_masks(nc, g, d)
        filter_products(nc, g, d)
        g.recv = sb("recv", [P, RW])
        node_stage(nc, g, d, 0)
        filter_sums(nc, g, d)
        g.acc, g.ed = sb("acc", [P, RW]), sb("ed", [P, RB, 3, HEADS], BF16)
        collect_sums(nc, g, d)
        node_stage(nc, g, d, 1)
        g.scores = sb("scores", [P, NT, HEADS])
        attention_scores(nc, g, d)
        segment_softmax(nc, g, d, 2)
        weighted_sums(nc, g, d, 2)
        node_stage(nc, g, d, 2)
        edge_attention(nc, g, d)
        segment_softmax(nc, g, d, 3)
        weighted_sums(nc, g, d, 3)
        node_stage(nc, g, d, 3)


def kernel(**inputs):
    import concourse.bacc as bacc
    from concourse.bass_utils import run_bass_kernel_spmd

    a = {k: np.asarray(v) for k, v in inputs.items()}
    src = np.zeros(EP, np.int32)
    src[:E] = a["src"]
    dst = np.full(EP + 2, N, np.int32)
    dst[0], dst[1:E + 1], dst[-1] = -1, a["dst"], N + 1
    ew = np.zeros(EP, np.float32)
    ew[:E] = a["edge_weight"]
    ef = np.zeros((F, EP), np.float32)
    ef[:, :E] = a["edge_attr_128"].T
    rbf_in = a["edge_attr_20"].shape[1]
    f20 = np.zeros((rbf_in + 1, EP), np.float32)
    f20[:rbf_in, :E], f20[rbf_in] = a["edge_attr_20"].T, 1.0
    x = np.zeros((NP, F), np.float32)
    x[:N] = a["x"]
    tiles = lambda v: np.ascontiguousarray(v.reshape(NT, P).T)
    a_heads = np.zeros((F, 2 * HEADS), np.float32)
    for h in range(HEADS):
        a_heads[HD * h:HD * h + HD, h] = a["L2_gnn_a_src"][h, :, 0]
        a_heads[HD * h:HD * h + HD, HEADS + h] = a["L2_gnn_a_dst"][h, :, 0]
    w2 = a["L2_gnn_W"].transpose(1, 0, 2).reshape(F, F)
    arrays = dict(
        x=x, srcG=np.ascontiguousarray(src.reshape(NG, GT, P).transpose(0, 2, 1)),
        src=src, srcT=tiles(src), power=(2.0 ** (63 - np.arange(P, dtype=np.float32)))[:, None].astype(np.float32),
        dstT=tiles(dst[1:-1]), prevT=tiles(dst[:-2]),
        dstP=dst[1:-1].reshape(P, PB), prevP=dst[:-2].reshape(P, PB), nextP=dst[2:].reshape(P, PB),
        ewT=tiles(ew), ew=ew.reshape(1, EP), ef=ef, f20=f20,
        w1=a["L0_gnn_W1"], b1=a["L0_gnn_b1"][:, None], w2=a["L0_gnn_W2"], b2=a["L0_gnn_b2"][:, None],
        w3=a["L0_gnn_W3"], b3=a["L0_gnn_b3"][None],
        mu=np.linspace(0.0, 1.0, F, dtype=np.float32)[:, None],
        w_in=a["L1_gnn_W_in"], b_in=a["L1_gnn_b_in"][None],
        wf1=np.concatenate([a["L1_gnn_Wf1"], a["L1_gnn_bf1"][None]]), wf2=a["L1_gnn_Wf2"], bf2=a["L1_gnn_bf2"][None],
        wo1=a["L1_gnn_Wo1"], bo1=a["L1_gnn_bo1"][:, None], wo2=a["L1_gnn_Wo2"], bo2=a["L1_gnn_bo2"][None],
        wg=w2, wgT=w2.T, a_heads=a_heads,
        ws=a["L3_gnn_Ws_k"].reshape(F, F), wr=a["L3_gnn_Wr_k"].reshape(F, F), we=a["L3_gnn_We_k"].reshape(F, F),
        bs=a["L3_gnn_Ws_b"].reshape(1, F), br=a["L3_gnn_Wr_b"].reshape(1, F), be=a["L3_gnn_We_b"].reshape(1, F),
        aw=np.tile(a["L3_gnn_attn_w"][:, 0], HEADS)[None], ab=a["L3_gnn_attn_b"][None],
    )
    nc = bacc.Bacc("TRN2", target_bir_lowering=False, num_devices=1)
    d = {}
    feed = {}
    for name, v in arrays.items():
        v = np.ascontiguousarray(v)
        feed["in_" + name] = v
        d[name] = (nc.dram_tensor("in_" + name, v.shape, mybir.dt.from_np(v.dtype), kind="ExternalInput").ap())
    d["out"] = nc.dram_tensor("out_0_dram", (N, F), F32, kind="ExternalOutput").ap()
    d["rel"] = nc.dram_tensor("rel", (EP,), BF16, kind="Internal").ap()
    d["keep"] = nc.dram_tensor("keep_rows", (EP,), BF16, kind="Internal").ap()
    d["perm"] = nc.dram_tensor("perm", (NP, 4), F32, kind="Internal").ap()
    d["table"] = nc.dram_tensor("table", (NP, F), F32, kind="Internal").ap()
    d["table_heads"] = nc.dram_tensor("table_heads", (NP, F + HEADS), F32, kind="Internal").ap()
    d["sums"] = [nc.dram_tensor(f"sums{i}", (NP + P, F), F32, kind="Internal").ap() for i in range(NA)]
    d["rows"] = nc.dram_tensor("rows", (EP, F), F32, kind="Internal").ap()
    d["logits"] = nc.dram_tensor("logits", (HEADS, EP), F32, kind="Internal").ap()
    d["alpha"] = nc.dram_tensor("alpha", (HEADS, EP), F32, kind="Internal").ap()
    program(nc, d)
    return run_bass_kernel_spmd(nc, [feed], core_ids=[0]).results[0]["out_0_dram"]
```

```python
from contextlib import ExitStack

import numpy as np
import concourse.bass as bass
from concourse import mybir

F32 = mybir.dt.float32
BF16 = mybir.dt.bfloat16
I32 = mybir.dt.int32
ALU = mybir.AluOpType
ACT = mybir.ActivationFunctionType
AX = mybir.AxisListType
DVE = mybir.EngineType.DVE
PE = mybir.EngineType.PE

P = 128
N, E, F = 6250, 100000, 128
HEADS, HD = 4, 32
GT = 8
GE = GT * P
NG = -(-E // GE)
NG += NG % 2
NT = NG * GT
EP = NT * P
NB = -(-(N + 1) // P)
NP = NB * P
RB = NB + 1
RW = RB * P
NBG = 7
NS = NB // NBG
NW = NBG * P
NA = 4
SEGC = 112
SEGN = NT // SEGC
PB = EP // P
assert NB % NBG == 0 and NT % SEGC == 0 and GT == 8
BIG = 1.5e38
CLAMP = 44.0
MISH_CLAMP = 20.0
LN2 = float(np.log(2.0))
LN_EPS = 1e-5
ALPHA_EPS = 1e-10
SLOPE = 0.2
PAIRS0 = 3


class Shared:
    pass


class Group:

    def __init__(self, pair, slot):
        self.n, self.pair, self.slot = 2 * pair + slot, pair, slot


class Step:

    def __init__(self, pair, odd):
        self.pair, self.odd = pair, odd

    def ago(self, k):
        total = self.odd - k
        g = Group(self.pair + total // 2, total % 2)
        return None if isinstance(g.n, int) and not 0 <= g.n < NG else g


def over_groups(eng, body, lag):
    for i in range(2 * PAIRS0):
        body(Step(i // 2, i % 2))
    with eng.Fori(PAIRS0, NG // 2) as pair:
        body(Step(pair, 0))
        body(Step(pair, 1))
    for i in range(NG, NG + lag):
        body(Step(i // 2, i % 2))


def wait_pos(eng, sem, count):
    if not (isinstance(count, int) and count <= 0):
        eng.wait_ge(sem, count)


class Chain:

    def __init__(self, eng, sem, at=None):
        self.eng, self.sem, self.count, self.at = eng, sem, 0, at

    def __call__(self, ins, name=None):
        self.count += 1
        ins.then_inc(self.sem, 1)
        self.eng.wait_ge(self.sem, self.count)
        if name:
            self.at[name] = self.count


def phase_semaphores(nc, stack, prefix):
    taken = []

    def allocate(name):
        taken.append(nc.alloc_semaphore(name=prefix + name))
        return taken[-1]

    def give_back():
        nc.clear_and_free_semaphores(taken)
        nc.all_engine_barrier()
    stack.callback(give_back)
    return allocate


def bcast(ap, axis, n):
    shape = list(ap.shape)
    shape.insert(axis, n)
    return ap.unsqueeze(axis).broadcast_to(shape)


def psum_half(ps, h):
    return ps[:, 512 * h:512 * h + 512]


def node_cols(b):
    return slice(P * b, P * b + P)


def setup(nc, g, d):
    half = NT // 2
    with ExitStack() as c:
        sb = lambda n, s, t=F32: c.enter_context(nc.sbuf_tensor(n, s, t))
        sem = phase_semaphores(nc, c, "st_")
        loaded, consts, vec, cut_sin, rel_sb, stored = (sem(x) for x in ("loaded", "consts", "vec", "cut_sin", "rel_sb", "stored"))
        hot_hi, off_ok = sem("hot_hi"), sem("off_ok")
        off, off2 = sb("off", [P, 2, GT, NB], BF16), sb("off2", [P, GT, NB], BF16)
        tile_sums, base_bc, rel_t, hot, counted, block_sums, turned, scattered, back = (
            sem(x) for x in ("tile_sums", "base_bc", "rel_t", "hot", "counted", "block_sums", "turned", "scattered", "back"))
        dst_i, prev_i = sb("dst_i", [P, NT], I32), sb("prev_i", [P, NT], I32)
        hi, lo = sb("hi", [P, NT]), sb("lo", [P, NT])
        ta, tb = sb("ta", [P, NT]), sb("tb", [P, NT])
        start, ones = sb("start", [P, NT]), sb("ones", [P, NT])
        tri0, tris, ones_sq = sb("tri0", [P, P]), sb("tris", [P, P]), sb("ones_sq", [P, P])
        half_pi = sb("half_pi", [P, 1])
        row_a, row_b = sb("row_a", [1, NT]), sb("row_b", [1, NT])
        relc, keepc = sb("relc", [SEGC, SEGN, P], BF16), sb("keepc", [SEGC, SEGN, P], BF16)
        ohi, olo = sb("ohi", [P, 2, GT, NB], BF16), sb("olo", [P, 2, GT, P], BF16)
        iota_b, zero_b = sb("iota_b", [P, P], BF16), sb("zero_b", [P, P], BF16)
        cnt, has, ccnt, chas = (sb(x, [NB, P]) for x in ("cnt", "has", "ccnt", "chas"))
        tot, pre = sb("tot", [NB, 2]), sb("sums_before", [NB, 3])
        nid, rnk, tmpn = sb("nid", [NB, P]), sb("rnk", [NB, P]), sb("tmpn", [NB, P])
        rank_of = sb("rank_of", [P, NB], I32)
        payload, pay_r = sb("payload", [P, NB, 4]), sb("pay_r", [P, NB, 4])
        A, B, C = g.psA, g.psB, g.psC
        rows = lambda r: r[:, :].rearrange("a (h n) -> a h n", h=2)
        halves = lambda ps, n: ps[0:n, :].rearrange("a (h n) -> a h n", h=2)[:, :, 0:half]
        at = {}

        with nc.Block() as block:
            @block.vector
            def _(eng):
                do = Chain(eng, vec, at)
                eng.wait_ge(consts, 8)
                eng.wait_ge(loaded, 48)
                do(eng.tensor_scalar(g.ident[:, :], g.iota_row[:, :], g.iota_col[:, 0:1], None, ALU.is_equal))
                do(eng.tensor_scalar(g.iota_col2[:, :], g.iota_col[:, :], float(P), None, ALU.add))
                do(eng.tensor_scalar(tri0[:, :], g.iota_row[:, :], g.iota_col[:, 0:1], None, ALU.is_ge))
                do(eng.memset(tri0[0:1, :], 0.0))
                do(eng.tensor_scalar(tris[:, :], g.iota_row[:, :], g.iota_col[:, 0:1], None, ALU.is_gt))
                do(eng.memset(half_pi[:, :], float(np.pi / 2)))
                do(eng.tensor_scalar(tb[:, :], g.ewT[:, :], -0.8, float(1 / (1.0 - 0.8)), ALU.add, ALU.mult))
                do(eng.tensor_scalar(tb[:, :], tb[:, :], 0.0, 1.0, ALU.max, ALU.min), "ramp")
                do(eng.tensor_copy(hi[:, :], dst_i[:, :]))
                do(eng.tensor_copy(lo[:, :], prev_i[:, :]))
                do(eng.tensor_tensor(start[:, :], hi[:, :], lo[:, :], ALU.not_equal), "start")
                eng.wait_ge(cut_sin, 1)
                do(eng.tensor_scalar(ta[:, :], ta[:, :], 1.0, 0.5, ALU.add, ALU.mult))
                do(eng.scalar_tensor_tensor(ta[:, :], g.ewT[:, :], 1.0, ta[:, :], ALU.is_le, ALU.mult))
                do(eng.tensor_copy(g.cut[:, :], ta[:, :]))
                do(eng.tensor_scalar(tb[:, :], start[:, :], -1.0, 1.0, ALU.mult, ALU.add))
                do(eng.tensor_scalar(prev_i[:, :], dst_i[:, :], 7, None, ALU.logical_shift_right))
                do(eng.tensor_scalar(dst_i[:, :], dst_i[:, :], P - 1, None, ALU.bitwise_and))
                do(eng.tensor_copy(hi[:, :], prev_i[:, :]))
                do(eng.tensor_copy(lo[:, :], dst_i[:, :]), "places")
                eng.wait_ge(tile_sums, 1)
                do(eng.tensor_copy(rows(g.lr), halves(A, P)))
                do(eng.tensor_copy(rows(row_a), halves(B, 1)))
                do(eng.tensor_tensor_scan(row_b[:, :], ones[0:1, :], row_a[:, :], -1.0, ALU.mult, ALU.add))
                do(eng.tensor_tensor(row_b[:, :], row_b[:, :], row_a[:, :], ALU.subtract))
                do(eng.tensor_tensor(row_b[:, :], row_b[:, :], start[0:1, :], ALU.add))
                do(eng.tensor_copy(g.rank0[:, :], row_b[:, :]))
                do(eng.tensor_scalar(g.block0[:, :], g.rank0[:, :], 7, None, ALU.logical_shift_right))
                do(eng.tensor_copy(row_a[:, :], g.block0[:, :]))
                do(eng.scalar_tensor_tensor(row_a[:, :], row_a[:, :], -float(P), row_b[:, :], ALU.mult, ALU.add), "base_row")
                eng.wait_ge(base_bc, 1)
                do(eng.tensor_tensor(rows(ta), rows(g.lr), halves(B, P), ALU.add), "rel")

                def one_hots(step):
                    t = step.ago(0)
                    if t is None:
                        return
                    wait_pos(eng, counted, t.n - 1)
                    cols = bass.ds(t.n * GT, GT)
                    eng.tensor_tensor(olo[:, t.slot], bcast(iota_b[:, :], 1, GT), bcast(lo[:, cols], 2, P),
                                      ALU.is_equal).then_inc(hot, 1)
                over_groups(eng, one_hots, 0)

                eng.wait_ge(counted, NG)
                do(eng.tensor_copy(cnt[:, :], C[0:NB, 0:P]))
                do(eng.tensor_scalar(has[:, :], cnt[:, :], 1.0, None, ALU.min))
                do(eng.tensor_tensor_scan(ccnt[:, :], ones[0:NB, 0:P], cnt[:, :], 0.0, ALU.mult, ALU.add))
                do(eng.tensor_tensor_scan(chas[:, :], ones[0:NB, 0:P], has[:, :], 0.0, ALU.mult, ALU.add))
                do(eng.tensor_copy(tot[:, 0:1], ccnt[:, P - 1:P]))
                do(eng.tensor_copy(tot[:, 1:2], chas[:, P - 1:P]), "totals")
                eng.wait_ge(block_sums, 1)
                do(eng.tensor_copy(pre[:, :], B[0:NB, 0:3]))
                do(eng.tensor_scalar(ccnt[:, :], ccnt[:, :], pre[:, 0:1], -1.0, ALU.add, ALU.add))
                do(eng.tensor_scalar(ccnt[:, :], ccnt[:, :], 0.0, None, ALU.max))
                do(eng.tensor_scalar(chas[:, :], chas[:, :], pre[:, 1:2], None, ALU.add))
                do(eng.tensor_tensor(rnk[:, :], nid[:, :], chas[:, :], ALU.subtract))
                do(eng.tensor_scalar(rnk[:, :], rnk[:, :], pre[:, 2:3], None, ALU.add))
                do(eng.tensor_scalar(chas[:, :], chas[:, :], -1.0, None, ALU.add))
                do(eng.tensor_tensor(tmpn[:, :], chas[:, :], rnk[:, :], ALU.subtract))
                do(eng.tensor_tensor(tmpn[:, :], tmpn[:, :], has[:, :], ALU.mult))
                do(eng.tensor_tensor(rnk[:, :], rnk[:, :], tmpn[:, :], ALU.add), "ranks")
                eng.wait_ge(turned, 1)
                do(eng.tensor_copy(rank_of[:, :], A[:, 0:NB]))
                for k in range(3):
                    do(eng.tensor_copy(payload[:, :, k], A[:, 64 * (k + 1):64 * (k + 1) + NB]))
                do(eng.memset(payload[:, :, 3], 0.0), "payload")
                eng.wait_ge(back, 16)
                do(eng.tensor_copy(g.last_edge[:, :], pay_r[:, :, 0]))
                do(eng.tensor_copy(g.has_edge[:, :], pay_r[:, :, 1]))
                do(eng.tensor_copy(g.node[:, :], pay_r[:, :, 2]))

            @block.tensor
            def _(eng):
                eng.wait_ge(vec, at["start"])
                for h in range(2):
                    eng.matmul(A[:, 512 * h:512 * h + half], tri0[:, :], start[:, half * h:half * (h + 1)], start=True, stop=True)
                for h in range(2):
                    ins = eng.matmul(B[0:1, 512 * h:512 * h + half], ones_sq[:, 0:1], start[:, half * h:half * (h + 1)],
                                     start=True, stop=True)
                ins.then_inc(tile_sums, 1)
                eng.wait_ge(vec, at["base_row"])
                for h in range(2):
                    ins = eng.matmul(B[:, 512 * h:512 * h + half], g.ones_row[:, :], row_a[:, half * h:half * (h + 1)],
                                     start=True, stop=True)
                ins.then_inc(base_bc, 1)
                eng.wait_ge(vec, at["rel"])
                for k in range(SEGN):
                    eng.transpose(A[0:SEGC, P * k:P * k + P], ta[:, SEGC * k:SEGC * (k + 1)], g.ident[:, :])
                    ins = eng.transpose(g.psD[0:SEGC, P * k:P * k + P], tb[:, SEGC * k:SEGC * (k + 1)], g.ident[:, :])
                ins.then_inc(rel_t, 1)

                def count(step):
                    t = step.ago(0)
                    if t is None:
                        return
                    eng.wait_ge(hot, t.n + 1)
                    eng.wait_ge(hot_hi, 2 * t.n + 2)
                    for k in range(GT):
                        ins = eng.matmul(C[0:NB, 0:P], ohi[:, t.slot, k, :], olo[:, t.slot, k, :], start=False, stop=False,
                                         skip_group_check=True)
                    ins.then_inc(counted, 1)
                eng.wait_ge(consts, 8)
                eng.matmul(C[0:NB, 0:P], zero_b[:, 0:NB], zero_b[:, :], start=True, stop=False, skip_group_check=True)
                over_groups(eng, count, 0)
                eng.wait_ge(vec, at["totals"])
                eng.matmul(B[0:NB, 0:2], tris[0:NB, 0:NB], tot[:, :], start=True, stop=True)
                eng.matmul(B[0:NB, 2:3], ones_sq[0:NB, 0:NB], tot[:, 1:2], start=True, stop=True).then_inc(block_sums, 1)
                eng.wait_ge(vec, at["ranks"])
                eng.wait_ge(rel_sb, 1)
                for k, m in enumerate((rnk, ccnt, has, nid)):
                    ins = eng.transpose(A[:, 64 * k:64 * k + NB], m[:, :], g.ident[0:NB, 0:NB])
                ins.then_inc(turned, 1)

            @block.scalar
            def _(eng):
                eng.wait_ge(vec, at["ramp"])
                eng.activation(ta[:, :], tb[:, :], ACT.Sin, bias=half_pi[:, 0:1], scale=-float(np.pi)).then_inc(cut_sin, 1)
                eng.preload_act_table_set("natural_log_exp_and_others")
                eng.wait_ge(rel_t, 1)
                eng.copy(relc[:, :, :], A[0:SEGC, 0:SEGN * P].rearrange("t (k p) -> t k p", p=P)).then_inc(rel_sb, 1)
                eng.copy(keepc[:, :, :], g.psD[0:SEGC, 0:SEGN * P].rearrange("t (k p) -> t k p", p=P)).then_inc(rel_sb, 1)

                def one_hots(step):
                    t = step.ago(0)
                    eng.wait_ge(off_ok, t.n + 1)
                    wait_pos(eng, hot_hi, 2 * t.n)
                    eng.activation(off2[:, :, :], off[:, t.slot], ACT.Square).then_inc(hot_hi, 1)
                    eng.wait_ge(hot_hi, 2 * t.n + 1)
                    wait_pos(eng, counted, t.n - 1)
                    eng.activation(ohi[:, t.slot], off2[:, :, :], ACT.Relu, bias=1.0, scale=-1.0).then_inc(hot_hi, 1)
                over_groups(eng, one_hots, 0)

            @block.gpsimd
            def _(pool):
                for t, step, mul, n in ((g.iota_row, 1, 0, P), (g.iota_col, 0, 1, 1), (nid, 1, P, P), (iota_b, 1, 0, P)):
                    pool.iota(t[:, :], [[step, n]], base=0, channel_multiplier=mul,
                              allow_small_or_imprecise_dtypes=True).then_inc(consts, 1)
                for t in (ones, ones_sq, g.ones_row):
                    pool.memset(t[:, :], 1.0).then_inc(consts, 1)
                pool.memset(zero_b[:, :], 0.0).then_inc(consts, 1)
                pool.wait_ge(vec, at["places"])

                def one_hots(step):
                    t = step.ago(0)
                    wait_pos(pool, hot_hi, 2 * t.n - 3)
                    pool.tensor_tensor(off[:, t.slot], bcast(iota_b[:, 0:NB], 1, GT), bcast(hi[:, bass.ds(t.n * GT, GT)], 2, NB),
                                       ALU.subtract).then_inc(off_ok, 1)
                over_groups(pool, one_hots, 0)
                pool.wait_ge(vec, at["payload"])
                for b in range(NB):
                    pool.indirect_dma_start(d["perm"], bass.IndirectOffsetOnAxis(ap=rank_of[:, b:b + 1], axis=0),
                                            payload[:, b, :], None).then_inc(scattered, 16)

            @block.sync
            def _(sp):
                for dst, src in ((dst_i, d["dstT"]), (prev_i, d["prevT"]), (g.ewT, d["ewT"])):
                    sp.dma_start(dst[:, :], src).then_inc(loaded, 16)
                sp.wait_ge(rel_sb, 2)
                sp.dma_start(d["rel"].rearrange("(k t p) -> t k p", k=SEGN, p=P), relc[:, :, :]).then_inc(stored, 16)
                sp.dma_start(d["keep"].rearrange("(k t p) -> t k p", k=SEGN, p=P), keepc[:, :, :]).then_inc(stored, 16)
                sp.wait_ge(stored, 32)
                sp.wait_ge(scattered, 16 * NB)
                sp.dma_start(pay_r[:, :, :], d["perm"].rearrange("(b p) w -> p b w", p=P)).then_inc(back, 16)
                sp.wait_ge(back, 16)


def scan_masks(nc, g, d):
    with ExitStack() as c:
        sb = lambda n, s, t=F32: c.enter_context(nc.sbuf_tensor(n, s, t))
        sem = phase_semaphores(nc, c, "sm_")
        loaded, vec, turned = (sem(x) for x in ("loaded", "vec", "turned"))
        dP, pP, nP = (sb(x, [P, PB], I32) for x in ("dP", "pP", "nP"))
        df, of = sb("df", [P, PB]), sb("of", [P, PB])
        sP, ones = sb("sP", [P, PB]), sb("onesP", [P, PB])
        any_s, any_l, wide = sb("any_s", [P, 1]), sb("any_l", [P, 1]), sb("wide", [P, 3, HEADS])
        at = {}
        with nc.Block() as block:
            @block.vector
            def _(eng):
                do = Chain(eng, vec, at)
                do(eng.memset(ones[:, :], 1.0))
                eng.wait_ge(loaded, 48)
                do(eng.tensor_copy(df[:, :], dP[:, :]))
                do(eng.tensor_copy(of[:, :], pP[:, :]))
                do(eng.tensor_tensor(sP[:, :], df[:, :], of[:, :], ALU.not_equal))
                do(eng.tensor_copy(of[:, :], nP[:, :]))
                do(eng.tensor_tensor(g.last[:, :], df[:, :], of[:, :], ALU.not_equal))
                do(eng.tensor_scalar(g.reset[:, :], sP[:, :], -BIG, None, ALU.mult))
                do(eng.tensor_scalar(g.keep_s[:, :], sP[:, :], -1.0, 1.0, ALU.mult, ALU.add))
                do(eng.tensor_scalar(g.keep_l[:, :], g.last[:, :], -1.0, 1.0, ALU.mult, ALU.add))
                do(eng.tensor_tensor_scan(df[:, :], ones[:, :], sP[:, :], 0.0, ALU.mult, ALU.max))
                do(eng.tensor_copy(any_s[:, :], df[:, PB - 1:PB]))
                do(eng.tensor_scalar(g.pre[:, :], df[:, :], -1.0, 1.0, ALU.mult, ALU.add))
                do(eng.tensor_scalar(g.pre_neg[:, :], df[:, :], -BIG, None, ALU.mult))
                do(eng.tensor_tensor_scan(of[:, ::-1], ones[:, :], g.last[:, ::-1], 0.0, ALU.mult, ALU.max))
                do(eng.tensor_copy(any_l[:, :], of[:, 0:1]))
                do(eng.tensor_scalar(g.suf[:, :], of[:, :], -1.0, 1.0, ALU.mult, ALU.add))
                do(eng.tensor_scalar(wide[:, 0, :], bcast(any_s[:, 0], 1, HEADS), -BIG, None, ALU.mult))
                do(eng.tensor_scalar(wide[:, 1, :], bcast(any_s[:, 0], 1, HEADS), -1.0, 1.0, ALU.mult, ALU.add))
                do(eng.tensor_scalar(wide[:, 2, :], bcast(any_l[:, 0], 1, HEADS), -1.0, 1.0, ALU.mult, ALU.add), "wide")
                eng.wait_ge(turned, 1)
                do(eng.tensor_copy(g.chain_mask[:, :, :], g.psA[0:HEADS, 0:3 * P].rearrange("h (k p) -> h k p", p=P)))

            @block.tensor
            def _(eng):
                eng.wait_ge(vec, at["wide"])
                for k in range(3):
                    ins = eng.transpose(g.psA[0:HEADS, P * k:P * k + P], wide[:, k, :], g.ident[:, :])
                ins.then_inc(turned, 1)

            @block.sync
            def _(sp):
                for dst, src in ((dP, d["dstP"]), (pP, d["prevP"]), (nP, d["nextP"])):
                    sp.dma_start(dst[:, :], src).then_inc(loaded, 16)


def gather_group(pool, t, table, idx, rows, idx_landed, slot_free, go, landed):
    width = table.shape[1]
    pool.wait_ge(idx_landed[t.slot], 16 * (t.pair + 1))
    for sem, count in slot_free:
        wait_pos(pool, sem, count)
    pool.sem_inc(go, 1)
    for k in range(GT):
        pool.indirect_dma_start(rows[t.slot][:, k * width:(k + 1) * width], None, table,
                                bass.IndirectOffsetOnAxis(ap=idx[t.slot][:, k:k + 1], axis=0)).then_inc(landed[t.slot], 16)


def load_ints(nc, engine, row, n, most):
    return nc.values_load_multi_w_load_instructions(
        row[0:1, bass.ds(n * GT, GT)], engines=(engine,), min_val=0, max_val=most,
        skip_runtime_bounds_check_because="ranks are at most the number of nodes")[1]


def expand_destination(eng, ps, hotT, state, block0):
    for k in range(GT):
        for b in range(2):
            ins = eng.matmul(ps[:, P * k:P * k + P], hotT[:, b, P * k:P * k + P], state[:, bass.ds(block0[k] * F + F * b, F)],
                             start=b == 0, stop=b == 1)
    return ins


def softplus_parts(eng, at_44, z, out, ready, n, clamp):
    eng.activation(out, z, ACT.Relu, bias=at_44, scale=-1.0).then_inc(ready, 1)
    eng.wait_ge(ready, n + 1)
    eng.activation(out, out, ACT.Exp, bias=clamp, scale=-1.0).then_inc(ready, 1)
    eng.wait_ge(ready, n + 2)
    eng.activation(out, out, ACT.Ln, bias=1.0).then_inc(ready, 1)


def filter_products(nc, g, d):
    with ExitStack() as c:
        sb = lambda n, s, t=F32: c.enter_context(nc.sbuf_tensor(n, s, t))
        two = lambda n, s, t=F32: [sb(n + "_a", s, t), sb(n + "_b", s, t)]
        sem = phase_semaphores(nc, c, "fp_")
        two_sems = lambda n: [sem(n + "0"), sem(n + "1")]
        w1, w2 = sb("w1", [F, F]), sb("w2", [F, F])
        b1, b2, mu, neg_mu, lift1, lift2, clamp = (sb(x, [P, 1]) for x in ("b1", "b2", "mu", "neg_mu", "lift1", "lift2", "clamp0"))
        dist, idx, ef, G = two("dist", [P, GE]), two("idx", [P, GT], I32), two("ef", [P, GE]), two("G", [P, GE])
        sq, rbf, parts1, sp1 = sb("sq", [P, GE]), two("rbf", [P, GE]), sb("parts1", [P, GE]), two("sp1_", [P, GE])
        parts2, sp2, prod = sb("parts2", [P, GE]), sb("sp2", [P, GE]), sb("prod", [P, GE])
        keep = two("keep", [P, GE], BF16)
        Gc, D, D0, D1 = (sb(x, [P, GE]) for x in ("Gc", "D", "D0", "D1"))
        cut, run, rows = sb("cut_now", [P, GT]), two("run", [P, GE]), two("rows_sb", [P, GE])
        weights, vec = sem("weights"), sem("vec")
        dist_in, idx_in, ef_in, G_in, stored = (two_sems(x) for x in ("dist_in", "idx_in", "ef_in", "G_in", "stored"))
        go, squared, rbf_ok, z1_ok, parts1_ok, sp1_ok, z2_ok, parts2_ok = (
            sem(x) for x in ("go", "squared", "rbf_ok", "z1_ok", "parts1_ok", "sp1_ok", "z2_ok", "parts2_ok"))
        cut_ok, scaled, sp2_ok, prod_ok, turned, D_ok, run_ok, back_ok, rows_ok = (
            sem(x) for x in ("cut_ok", "scaled", "sp2_ok", "prod_ok", "turned", "D_ok", "run_ok", "back_ok", "rows_ok"))
        keep_in, zeros, zero_ok, cleared = two_sems("keep_in"), sb("zeros", [P, F]), sem("zero_ok"), sem("cleared")
        ones_col, shift = sb("ones_col", [P, 1]), g.psD[:, 0:1]
        shift_ok, b2_ok = sem("shift_ok"), sem("b2_ok")
        z1, z2, back, gt = g.psA, g.psB, g.psC, g.psD
        at = {}

        with nc.Block() as block:
            @block.sync
            def _(sp):
                for dst, src in ((w1, d["w1"]), (w2, d["w2"]), (b1, d["b1"]), (b2, d["b2"]), (mu, d["mu"])):
                    sp.dma_start(dst[:, :], src).then_inc(weights, 16)

                def step(s):
                    if (t := s.ago(0)) is not None:
                        wait_pos(sp, squared, t.n - 1)
                        sp.dma_start(dist[t.slot][:, :], d["ew"][:, bass.ds(t.n * GE, GE)].broadcast_to([P, GE])).then_inc(dist_in[t.slot], 16)
                        wait_pos(sp, G_in[t.slot], 16 * GT * t.pair)
                        sp.dma_start(idx[t.slot][:, :], d["srcG"][bass.ds(t.n, 1)].rearrange("o p k -> (o p) k")).then_inc(idx_in[t.slot], 16)
                    if (t := s.ago(2)) is not None:
                        wait_pos(sp, D_ok, 3 * (t.n - 1))
                        wait_pos(sp, prod_ok, t.n - 1)
                        sp.dma_start(ef[t.slot][:, :], d["ef"][:, bass.ds(t.n * GE, GE)]).then_inc(ef_in[t.slot], 16)
                        sp.dma_start(keep[t.slot][:, :], bcast(d["keep"][bass.ds(t.n * GE, GE)], 0, P)).then_inc(keep_in[t.slot], 16)
                    if (t := s.ago(5)) is not None:
                        sp.wait_ge(rows_ok, t.n + 1)
                        sp.dma_start(d["rows"][bass.ds(t.n * GE, GE), :].rearrange("(k p) f -> p k f", p=P),
                                     rows[t.slot][:, :].rearrange("p (k f) -> p k f", k=GT)).then_inc(stored[t.slot], 16)
                over_groups(sp, step, 5)
                for s in stored:
                    sp.wait_ge(s, 16 * (NG // 2))

            @block.gpsimd
            def _(pool):
                def step(s):
                    if (t := s.ago(0)) is not None:
                        gather_group(pool, t, d["x"], idx, G, idx_in, [(scaled, t.n - 1)], go, G_in)
                over_groups(pool, step, 0)

            @block.scalar
            def _(eng):
                eng.wait_ge(zero_ok, 1)
                for table in d["sums"]:
                    eng.dma_start(table.rearrange("(b p) f -> p b f", p=P), bcast(zeros[:, :], 1, NB + 1)).then_inc(cleared, 16)
                eng.wait_ge(vec, 5)

                def step(s):
                    if (t := s.ago(0)) is not None:
                        eng.wait_ge(dist_in[t.slot], 16 * (t.pair + 1))
                        wait_pos(eng, rbf_ok, t.n)
                        eng.activation(sq[:, :], dist[t.slot][:, :], ACT.Square, bias=neg_mu[:, 0:1]).then_inc(squared, 1)
                        eng.wait_ge(squared, t.n + 1)
                        wait_pos(eng, z1_ok, t.n - 1)
                        eng.activation(rbf[t.slot][:, :], sq[:, :], ACT.Exp, scale=-float(F)).then_inc(rbf_ok, 1)
                    if (t := s.ago(1)) is not None:
                        eng.wait_ge(z1_ok, t.n + 1)
                        wait_pos(eng, sp1_ok, t.n)
                        softplus_parts(eng, lift1[:, 0:1], z1[:, :], parts1[:, :], parts1_ok, 3 * t.n, clamp[:, 0:1])
                    if (t := s.ago(2)) is not None:
                        eng.wait_ge(z2_ok, t.n + 1)
                        wait_pos(eng, sp2_ok, t.n)
                        softplus_parts(eng, lift2[:, 0:1], z2[:, :], parts2[:, :], parts2_ok, 3 * t.n, clamp[:, 0:1])
                    if (t := s.ago(4)) is not None:
                        eng.wait_ge(back_ok, t.n + 1)
                        wait_pos(eng, stored[t.slot], 16 * t.pair)
                        eng.copy(rows[t.slot][:, :], back[:, :]).then_inc(rows_ok, 1)
                over_groups(eng, step, 4)
                eng.wait_ge(cleared, 16 * NA)

            @block.tensor
            def _(eng):
                eng.wait_ge(weights, 80)
                eng.wait_ge(vec, 1)
                eng.matmul(shift, w2[:, :], ones_col[:, :], start=True, stop=True).then_inc(shift_ok, 1)
                eng.wait_ge(vec, 5)

                def step(s):
                    if (t := s.ago(1)) is not None:
                        eng.wait_ge(rbf_ok, t.n + 1)
                        wait_pos(eng, sp1_ok, t.n)
                        for h in range(2):
                            ins = eng.matmul(psum_half(z1, h), w1[:, :], rbf[t.slot][:, 512 * h:512 * h + 512], start=True, stop=True)
                        ins.then_inc(z1_ok, 1)
                    if (t := s.ago(2)) is not None:
                        eng.wait_ge(sp1_ok, t.n + 1)
                        wait_pos(eng, sp2_ok, t.n)
                        for h in range(2):
                            ins = eng.matmul(psum_half(z2, h), w2[:, :], sp1[t.slot][:, 512 * h:512 * h + 512], start=True, stop=True)
                        ins.then_inc(z2_ok, 1)
                    if (t := s.ago(4)) is not None:
                        eng.wait_ge(run_ok, t.n + 1)
                        wait_pos(eng, rows_ok, t.n)
                        for k in range(GT):
                            ins = eng.transpose(back[:, P * k:P * k + P], run[t.slot][:, P * k:P * k + P], g.ident[:, :])
                        ins.then_inc(back_ok, 1)
                    if (t := s.ago(2)) is not None:
                        eng.wait_ge(scaled, t.n + 1)
                        wait_pos(eng, D_ok, 3 * t.n - 2)
                        for k in range(GT):
                            ins = eng.transpose(gt[:, P * k:P * k + P], Gc[:, P * k:P * k + P], g.ident[:, :])
                        ins.then_inc(turned, 1)
                over_groups(eng, step, 4)

            @block.vector
            def _(eng):
                eng.memset(zeros[:, :], 0.0).then_inc(zero_ok, 1)
                eng.wait_ge(weights, 80)
                eng.memset(ones_col[:, :], 1.0).then_inc(vec, 1)
                eng.memset(clamp[:, :], CLAMP).then_inc(vec, 1)
                eng.tensor_scalar(neg_mu[:, :], mu[:, :], -1.0, None, ALU.mult).then_inc(vec, 1)
                eng.tensor_scalar(lift1[:, :], b1[:, :], -1.0, CLAMP, ALU.mult, ALU.add).then_inc(vec, 1)
                eng.wait_ge(shift_ok, 1)
                eng.scalar_tensor_tensor(b2[:, :], shift, -LN2, b2[:, :], ALU.mult, ALU.add).then_inc(b2_ok, 1)
                eng.wait_ge(b2_ok, 1)
                eng.tensor_scalar(lift2[:, :], b2[:, :], -1.0, CLAMP, ALU.mult, ALU.add).then_inc(vec, 1)

                def step(s):
                    if (t := s.ago(3)) is not None:
                        eng.wait_ge(parts2_ok, 3 * t.n + 3)
                        wait_pos(eng, prod_ok, t.n)
                        eng.scalar_tensor_tensor(sp2[:, :], z2[:, :], b2[:, 0:1], parts2[:, :], ALU.add, ALU.max).then_inc(sp2_ok, 1)
                        eng.wait_ge(sp2_ok, t.n + 1)
                        eng.wait_ge(ef_in[t.slot], 16 * (t.pair + 1))
                        wait_pos(eng, D_ok, 3 * t.n)
                        eng.scalar_tensor_tensor(prod[:, :], sp2[:, :], -LN2, ef[t.slot][:, :], ALU.add, ALU.mult).then_inc(prod_ok, 1)
                        eng.wait_ge(prod_ok, t.n + 1)
                        eng.wait_ge(turned, t.n + 1)
                        eng.tensor_tensor(D[:, :], prod[:, :], gt[:, :], ALU.mult).then_inc(D_ok, 1)
                    if (t := s.ago(2)) is not None:
                        wait_pos(eng, scaled, t.n)
                        eng.tensor_copy(cut[:, :], g.cut[:, bass.ds(t.n * GT, GT)]).then_inc(cut_ok, 1)
                        eng.wait_ge(G_in[t.slot], 16 * GT * (t.pair + 1))
                        wait_pos(eng, turned, t.n)
                        eng.wait_ge(cut_ok, t.n + 1)
                        for k in range(GT):
                            ins = eng.tensor_scalar(Gc[:, P * k:P * k + P], G[t.slot][:, P * k:P * k + P], cut[:, k:k + 1], None, ALU.mult)
                        ins.then_inc(scaled, 1)
                    if (t := s.ago(3)) is not None:
                        eng.wait_ge(D_ok, 3 * t.n + 1)
                        eng.wait_ge(keep_in[t.slot], 16 * (t.pair + 1))
                        wait_pos(eng, run_ok, t.n)
                        eng.tensor_tensor(D0[:, :], D[:, :], keep[t.slot][:, :], ALU.mult).then_inc(D_ok, 1)
                    if (t := s.ago(1)) is not None:
                        eng.wait_ge(parts1_ok, 3 * t.n + 3)
                        wait_pos(eng, z2_ok, t.n - 1)
                        eng.scalar_tensor_tensor(sp1[t.slot][:, :], z1[:, :], b1[:, 0:1], parts1[:, :], ALU.add, ALU.max).then_inc(sp1_ok, 1)
                    if (t := s.ago(3)) is not None:
                        eng.wait_ge(D_ok, 3 * t.n + 2)
                        eng.tensor_tensor(D1[:, :], D[:, :], D0[:, :], ALU.subtract).then_inc(D_ok, 1)
                        eng.wait_ge(D_ok, 3 * t.n + 3)
                        wait_pos(eng, back_ok, t.n - 1)
                        initial = 1.0 if isinstance(t.n, int) and t.n == 0 else run[1 - t.slot][:, GE - 1:GE]
                        eng.tensor_tensor_scan(run[t.slot][:, :], D0[:, :], D1[:, :], initial, ALU.mult, ALU.add).then_inc(run_ok, 1)
                over_groups(eng, step, 3)


def node_stage(nc, g, d, layer):
    with ExitStack() as c:
        sb = lambda n, s, t=F32: c.enter_context(nc.sbuf_tensor(f"n{layer}_{n}", s, t))
        sem = phase_semaphores(nc, c, f"n{layer}_")
        weights, const, head_ok, mixed, parts_ok, soft_ok, out_ok, vec, rstd_ok, xT_ps, xT_ok, tab_ps, sent = (
            sem(x) for x in ("weights", "const", "head_ok", "mixed", "parts_ok", "soft_ok", "out_ok", "vec",
                             "rstd_ok", "xT_ps", "xT_ok", "tab_ps", "sent_a"))
        sent = [sent, sem("sent_b")]
        cols = lambda s: slice(NW * s, NW * s + NW)
        blocks = lambda s: slice(NBG * s, NBG * s + NBG)
        view = lambda t: t[:, 0:NW].rearrange("p (b f) -> p b f", b=NBG)
        head, outp, xTp, tabp = g.psA, g.psB, g.psC, g.psD
        wide = F + HEADS if layer == 1 else F
        y, sq, xT, tab = [sb("y_a", [P, NW]), sb("y_b", [P, NW])], sb("sq", [P, NW]), sb("xT", [P, NW]), sb("tab", [P, 2, NBG, wide])
        mean, t0 = sb("mean", [P, NBG]), sb("t0", [P, NBG])
        var, rstd = sb("var", [P, 2, NBG]), sb("rstd", [P, 2, NBG])
        clamp, one_c = sb("clamp", [P, 1]), sb("one_c", [P, 1])
        loads, w = [], {}

        def weight(name, shape):
            w[name] = sb("w_" + name, shape)
            loads.append((w[name], d[name].broadcast_to(shape)))
            return w[name]

        if layer == 0:
            w3, b3, w_in, b_in = weight("w3", [F, F]), weight("b3", [1, F]), weight("w_in", [F, F]), weight("b_in", [P, F])
            gathered = [sem(f"gathered{s}") for s in range(NS)]
            last_rows, no_edge = sb("last_rows", [P, NB, F]), sb("no_edge", [P, NB])
        elif layer == 1:
            wo1, bo1, wo2, bo2 = weight("wo1", [F, F]), weight("bo1", [F, 1]), weight("wo2", [F, F]), weight("bo2", [1, F])
            wg, wgT, a_heads = weight("wg", [F, F]), weight("wgT", [F, F]), weight("a_heads", [F, 2 * HEADS])
            w_att, lift = sb("w_att", [F, 2 * HEADS]), sb("lift", [P, 1])
            att = tabp[:, NW:NW + 2 * HEADS * NBG].rearrange("p (b k) -> p b k", b=NBG)
        elif layer == 2:
            ws, wr = weight("ws", [F, F]), weight("wr", [F, F])
            bs, be, br = weight("bs", [P, F]), weight("be", [P, F]), weight("br", [P, F])
            bse = sb("bse", [P, F])
        soft, xT2 = sb("soft", [P, NW]), sb("xT2", [P, NW])
        at = {}

        with nc.Block() as block:
            @block.vector
            def _(eng):
                do = Chain(eng, vec, at)
                do(eng.memset(clamp[:, :], CLAMP))
                do(eng.memset(one_c[:, :], 1.0), "ones")
                eng.wait_ge(weights, 16 * len(loads))
                if layer == 0:
                    do(eng.tensor_scalar(no_edge[:, :], g.has_edge[:, :], -1.0, 1.0, ALU.mult, ALU.add))
                if layer == 1:
                    do(eng.tensor_scalar(lift[:, :], bo1[:, :], -1.0, CLAMP, ALU.mult, ALU.add))
                    eng.wait_ge(const, 1)
                    do(eng.scalar_tensor_tensor(bo2[:, :], tabp[0:1, 0:F], -LN2, bo2[:, :], ALU.mult, ALU.add))
                    do(eng.tensor_copy(w_att[:, :], xTp[:, 0:2 * HEADS]))
                if layer == 2:
                    do(eng.tensor_tensor(bse[:, :], bs[:, :], be[:, :], ALU.add))
                if layer == 0:
                    do(eng.memset(g.recv[:, NB * F:RW], 0.0))
                at["consts"] = do.count

                def layer_output(s):
                    if layer == 0:
                        eng.wait_ge(gathered[s], 16 * 2 * NBG)
                        for b in range(NBG * s, NBG * s + NBG):
                            ins = eng.tensor_scalar(last_rows[:, b, :], last_rows[:, b, :], g.has_edge[:, b:b + 1],
                                                    no_edge[:, b:b + 1], ALU.mult, ALU.add)
                        ins.then_inc(mixed, 1)
                    if layer == 1:
                        eng.wait_ge(parts_ok, 3 * s + 3)
                        if s:
                            eng.wait_ge(out_ok, s)
                        for h in range(2):
                            ins = eng.scalar_tensor_tensor(xT2[:, 448 * h:448 * h + 448], head[:, 512 * h:512 * h + 448], bo1[:, 0:1],
                                                           soft[:, 448 * h:448 * h + 448], ALU.add, ALU.max)
                            ins.then_inc(soft_ok, 1)

                def norm_sums(s):
                    ys, vs = y[s % 2], var[:, s % 2, :]
                    if layer == 0:
                        eng.wait_ge(parts_ok, 3 * s + 3)
                        do(eng.tensor_tensor(ys[:, :], outp[:, 0:NW], soft[:, :], ALU.max))
                        do(eng.scalar_tensor_tensor(view(ys), view(ys), -LN2, g.x[:, blocks(s), :], ALU.add, ALU.add), f"out{s}")
                    else:
                        eng.wait_ge(out_ok, s + 1)
                        do(eng.tensor_tensor(ys[:, :], outp[:, 0:NW], g.x[:, blocks(s), :].rearrange("p b f -> p (b f)"), ALU.add), f"out{s}")
                    do(eng.tensor_reduce(mean[:, :], view(ys), AX.X, ALU.add))
                    do(eng.tensor_scalar(mean[:, :], mean[:, :], 1.0 / F, None, ALU.mult))
                    do(eng.tensor_tensor(view(ys), view(ys), bcast(mean[:, :], 2, F), ALU.subtract))
                    do(eng.tensor_tensor(sq[:, :], ys[:, :], ys[:, :], ALU.mult))
                    do(eng.tensor_reduce(vs, view(sq), AX.X, ALU.add))
                    do(eng.tensor_scalar(vs, vs, 1.0 / F, LN_EPS, ALU.mult, ALU.add), f"var{s}")

                def norm(s):
                    vs, rs = var[:, s % 2, :], rstd[:, s % 2, :]
                    eng.wait_ge(rstd_ok, 2 * s + 2)
                    do(eng.tensor_tensor(t0[:, :], rs, rs, ALU.mult))
                    do(eng.tensor_tensor(t0[:, :], t0[:, :], vs, ALU.mult))
                    do(eng.tensor_scalar(t0[:, :], t0[:, :], -0.5, 1.5, ALU.mult, ALU.add))
                    do(eng.tensor_tensor(rs, rs, t0[:, :], ALU.mult))
                    do(eng.tensor_tensor(g.x[:, blocks(s), :], view(y[s % 2]), bcast(rs, 2, F), ALU.mult), f"x{s}")

                def tables(s):
                    eng.wait_ge(tab_ps, s + 1)
                    if s > 1 and layer > 0:
                        eng.wait_ge(sent[s % 2], 16 * NBG * (s // 2))
                    rows_of = lambda t: t.rearrange("p (b f) -> p b f", b=NBG)
                    if layer == 0:
                        do(eng.tensor_tensor(rows_of(g.recv[:, cols(s)]), view(tabp), bcast(b_in[:, :], 1, NBG), ALU.add))
                    if layer == 1:
                        do(eng.tensor_copy(tab[:, s % 2, :, 0:F], view(tabp)))
                        do(eng.tensor_copy(tab[:, s % 2, :, F:wide], att[:, :, 0:HEADS]))
                        do(eng.tensor_copy(g.ed[:, blocks(s), :], att[:, :, HEADS:]))
                    if layer == 2:
                        do(eng.tensor_tensor(tab[:, s % 2, :, :], view(tabp), bcast(bse[:, :], 1, NBG), ALU.add))
                        do(eng.tensor_tensor(rows_of(g.recv[:, cols(s)]), view(head), bcast(br[:, :], 1, NBG), ALU.add))
                    at[f"tab{s}"] = do.count

                if layer == 0:
                    layer_output(0)
                for s in range(NS + 3):
                    if s >= 3 and layer < 3:
                        tables(s - 3)
                    if 0 <= s - 1 < NS:
                        norm_sums(s - 1)
                    if 0 <= s - 2 < NS:
                        norm(s - 2)
                    ahead = s + 1 if layer == 0 else s
                    if ahead < NS:
                        layer_output(ahead)
                if layer == 1:
                    do(eng.memset(g.ed[:, NB, :], 0.0))

            @block.scalar
            def _(eng):
                eng.wait_ge(vec, at["consts"])
                for s in range(NS + 2):
                    if s >= 2:
                        eng.wait_ge(vec, at[f"var{s - 2}"])
                        rs = rstd[:, s % 2, :]
                        eng.activation(rs, var[:, s % 2, :], ACT.Ln).then_inc(rstd_ok, 1)
                        eng.wait_ge(rstd_ok, 2 * (s - 2) + 1)
                        eng.activation(rs, rs, ACT.Exp, scale=-0.5).then_inc(rstd_ok, 1)
                    if s < NS and layer == 0:
                        eng.wait_ge(head_ok, s + 1)
                        if s:
                            eng.wait_ge(out_ok, s)
                        eng.copy(xT2[:, :], head[:, 0:NW]).then_inc(soft_ok, 1)
                        eng.wait_ge(out_ok, s + 1)
                        if s:
                            eng.wait_ge(vec, at[f"out{s - 1}"])
                        softplus_parts(eng, clamp[:, 0:1], outp[:, 0:NW], soft[:, :], parts_ok, 3 * s, clamp[:, 0:1])
                    if s < NS and layer == 1:
                        eng.wait_ge(head_ok, s + 1)
                        if s:
                            eng.wait_ge(soft_ok, 2 * s)
                        softplus_parts(eng, lift[:, 0:1], head[:, :].rearrange("p (h n) -> p h n", h=2)[:, :, 0:448],
                                       soft[:, :].rearrange("p (h n) -> p h n", h=2),
                                       parts_ok, 3 * s, clamp[:, 0:1])
                    if s >= 2 and layer < 3:
                        eng.wait_ge(xT_ps, s - 1)
                        if s > 2:
                            eng.wait_ge(tab_ps, s - 2)
                        eng.copy(xT[:, :], xTp[:, 0:NW]).then_inc(xT_ok, 1)

            @block.tensor
            def _(eng):
                def linear(ps, lhs, wt, bias):
                    for b in range(NBG):
                        if bias is not None:
                            eng.matmul(ps[:, node_cols(b)], g.ones_row[:, :], bias[:, :], start=True, stop=False)
                        ins = eng.matmul(ps[:, node_cols(b)], lhs[:, node_cols(b)], wt[:, :], start=bias is None, stop=True)
                    return ins

                def next_tables(s):
                    eng.wait_ge(vec, at[f"x{s}"])
                    if s:
                        eng.wait_ge(xT_ok, s)
                    for b in range(NBG):
                        ins = eng.transpose(xTp[:, node_cols(b)], g.x[:, NBG * s + b, :], g.ident[:, :])
                    ins.then_inc(xT_ps, 1)
                    eng.wait_ge(xT_ok, s + 1)
                    if s:
                        eng.wait_ge(vec, at[f"tab{s - 1}"])
                    if layer == 0:
                        linear(tabp, xT, w_in, None).then_inc(tab_ps, 1)
                    elif layer == 1:
                        linear(tabp, xT, wg, None)
                        for b in range(NBG):
                            ins = eng.matmul(att[:, b, :], xT[:, node_cols(b)], w_att[:, :], start=True, stop=True)
                        ins.then_inc(tab_ps, 1)
                    else:
                        linear(tabp, xT, ws, None)
                        linear(head, xT, wr, None).then_inc(tab_ps, 1)

                eng.wait_ge(weights, 16 * len(loads))
                if layer == 1:
                    eng.wait_ge(vec, at["ones"])
                    eng.matmul(tabp[0:1, 0:F], one_c[:, :], wo2[:, :], start=True, stop=True)
                    eng.matmul(xTp[:, 0:2 * HEADS], wgT[:, :], a_heads[:, :], start=True, stop=True).then_inc(const, 1)
                eng.wait_ge(vec, at["consts"])
                for s in range(NS + 2):
                    if s < NS and layer == 0:
                        eng.wait_ge(mixed, s + 1)
                        if s:
                            eng.wait_ge(soft_ok, s)
                        for b in range(NBG):
                            ins = eng.transpose(head[:, node_cols(b)], last_rows[:, NBG * s + b, :], g.ident[:, :])
                        ins.then_inc(head_ok, 1)
                        eng.wait_ge(soft_ok, s + 1)
                        if s:
                            eng.wait_ge(vec, at[f"out{s - 1}"])
                        linear(outp, xT2, w3, b3).then_inc(out_ok, 1)
                    if s < NS and layer == 1:
                        if s:
                            eng.wait_ge(soft_ok, 2 * s)
                        for h in range(2):
                            ins = eng.matmul(head[:, 512 * h:512 * h + 448], wo1[:, :], g.acc[:, NW * s + 448 * h:NW * s + 448 * h + 448],
                                             start=True, stop=True)
                        ins.then_inc(head_ok, 1)
                    if s < NS and layer >= 2:
                        if s:
                            eng.wait_ge(vec, at[f"out{s - 1}"])
                        for b in range(NBG):
                            ins = eng.transpose(outp[:, node_cols(b)], g.acc[:, P * (NBG * s + b):P * (NBG * s + b) + P], g.ident[:, :])
                        ins.then_inc(out_ok, 1)
                    if s >= 2 and layer < 3:
                        next_tables(s - 2)
                    if s < NS and layer == 1:
                        eng.wait_ge(soft_ok, 2 * s + 2)
                        if s:
                            eng.wait_ge(vec, at[f"out{s - 1}"])
                        linear(outp, xT2, wo2, bo2).then_inc(out_ok, 1)

            @block.gpsimd
            def _(pool):
                if layer == 0:
                    for b in range(NB):
                        here = gathered[b // NBG]
                        pool.indirect_dma_start(last_rows[:, b, :], None, d["rows"],
                                                bass.IndirectOffsetOnAxis(ap=g.last_edge[:, b:b + 1], axis=0)).then_inc(here, 16)
                        pool.indirect_dma_start(g.x[:, b, :], None, d["x"],
                                                bass.IndirectOffsetOnAxis(ap=g.node[:, b:b + 1], axis=0)).then_inc(here, 16)
                    return
                table = {1: d["table_heads"], 2: d["table"], 3: d["out"]}[layer]
                for s in range(NS):
                    pool.wait_ge(vec, at[f"x{s}"] if layer == 3 else at[f"tab{s}"])
                    for b in range(NBG):
                        row = g.x[:, NBG * s + b, :] if layer == 3 else tab[:, s % 2, b, :]
                        pool.indirect_dma_start(table, bass.IndirectOffsetOnAxis(ap=g.node[:, NBG * s + b:NBG * s + b + 1], axis=0),
                                                row, None, bounds_check=table.shape[0] - 1, oob_is_err=False).then_inc(sent[s % 2], 16)
                pool.wait_ge(sent[0], 16 * NBG * (NS - NS // 2))
                pool.wait_ge(sent[1], 16 * NBG * (NS // 2))

            @block.sync
            def _(sp):
                for dst, src in loads:
                    sp.dma_start(dst[:, :], src).then_inc(weights, 16)


def filter_sums(nc, g, d):
    with ExitStack() as c:
        sb = lambda n, s, t=F32: c.enter_context(nc.sbuf_tensor("fs_" + n, s, t))
        two = lambda n, s, t=F32: [sb(n + "_a", s, t), sb(n + "_b", s, t)]
        sem = phase_semaphores(nc, c, "fs_")
        two_sems = lambda n: [sem(n + "0"), sem(n + "1")]
        K = d["f20"].shape[0]
        wf1, wf2, bf2, clamp, one_c = sb("wf1", [K, F]), sb("wf2", [F, F]), sb("bf2", [1, F]), sb("clamp", [P, 1]), sb("one_c", [P, 1])
        bias3, bias_rows, ones3, bf2_b, spare = sb("bias3", [1, 3, 4, F], BF16), sb("bias_rows", [3, 4 * F], BF16), sb("ones3", [3, P], BF16), sb("bf2_b", [1, F]), sb("spare", [P, 1])
        src_i, src_f = sb("src_i", [P, NT], I32), sb("src_f", [P, NT])
        f20, rel, row, hotT = two("f20", [K, GE]), two("rel", [P, GE], BF16), two("row", [P, GE], I32), two("hotT", [P, 2, GE])
        parts, soft, filt_w, msg, same, total = (sb("parts", [P, GE]), two("soft", [P, GE]), two("filt_w", [P, GE]), two("msg", [P, GE]),
                                                 two("same", [P, GE]), two("total", [P, GE]))
        before, earlier, count = sb("before", [P, P]), sb("earlier", [P, GE]), sb("count", [P, GT])
        wt, cols, first, away, to = two("wt", [P, GT]), two("cols", [P, GT]), sb("first", [P, GT]), sb("away", [P, GT]), two("to", [P, GT], I32)
        weights, vec, shift_ok = sem("weights"), sem("vec"), sem("shift_ok")
        f20_in, rel_in, row_in = two_sems("f20_in"), two_sems("rel_in"), two_sems("row_in")
        z_ok, parts_ok, soft_ok, filt_ok, wt_ok, filt_w_ok, hotT_ok, dst_ok, msg_ok, cols_ok, same_ok, total_ps, total_ok, idx_ok, go, first_ok = (
            sem(x) for x in ("z_ok", "parts_ok", "soft_ok", "filt_ok", "wt_ok", "filt_w_ok", "hotT_ok", "dst_ok", "msg_ok", "cols_ok",
                             "same_ok", "total_ps", "total_ok", "idx_ok", "go", "first_ok"))
        bias_ok, at = sem("bias_ok"), {}
        added = [sem(f"added{i}") for i in range(NA)]
        z, filt, hd, tot = g.psA, g.psB, g.psC, g.psD

        with nc.Block() as block:
            @block.vector
            def _(eng):
                do = Chain(eng, vec, at)
                do(eng.memset(clamp[:, :], CLAMP))
                do(eng.memset(one_c[:, :], 1.0))
                do(eng.tensor_scalar(spare[:, :], g.iota_col[:, :], float(NP), None, ALU.add))
                eng.wait_ge(weights, 64)
                eng.wait_ge(shift_ok, 1)
                do(eng.scalar_tensor_tensor(bf2[:, :], filt[0:1, 0:F], -LN2, bf2[:, :], ALU.mult, ALU.add))
                for q in range(3):
                    do(eng.tensor_copy(bias3[:, q, :, :], bcast(bf2[:, :], 1, 4)))
                    do(eng.tensor_copy(bf2_b[:, :], bias3[:, q, 0, :]))
                    do(eng.tensor_tensor(bf2[:, :], bf2[:, :], bf2_b[:, :], ALU.subtract))
                do(eng.memset(ones3[:, :], 1.0))
                do(eng.tensor_scalar(before[:, :], g.iota_row[:, :], g.iota_col[:, 0:1], None, ALU.is_lt))
                do(eng.tensor_copy(src_f[:, :], src_i[:, :]), "consts")

                def step(s):
                    if (t := s.ago(1)) is not None:
                        eng.wait_ge(rel_in[t.slot], 16 * (t.pair + 1))
                        wait_pos(eng, dst_ok, t.n - 1)
                        for b, place in enumerate((g.iota_col, g.iota_col2)):
                            eng.tensor_scalar(hotT[t.slot][:, b, :], rel[t.slot][:, :], place[:, 0:1], None, ALU.is_equal).then_inc(hotT_ok, 1)
                        wait_pos(eng, filt_w_ok, t.n - 1)
                        eng.tensor_copy(wt[t.slot][:, :], g.ewT[:, bass.ds(t.n * GT, GT)]).then_inc(wt_ok, 1)
                    if (t := s.ago(2)) is not None:
                        wait_pos(eng, same_ok, t.n)
                        eng.tensor_copy(cols[t.slot][:, :], src_f[:, bass.ds(t.n * GT, GT)]).then_inc(cols_ok, 1)
                        eng.wait_ge(row_in[t.slot], 16 * (t.pair + 1))
                        wait_pos(eng, total_ps, t.n - 1)
                        wait_pos(eng, first_ok, 5 * (t.n - 1))
                        eng.wait_ge(cols_ok, t.n + 1)
                        for k in range(GT):
                            ins = eng.tensor_scalar(same[t.slot][:, P * k:P * k + P], row[t.slot][:, P * k:P * k + P], cols[t.slot][:, k:k + 1], None,
                                                    ALU.is_equal)
                        ins.then_inc(same_ok, 1)
                    if (t := s.ago(3)) is not None:
                        wait_pos(eng, first_ok, 5 * t.n)
                        wait_pos(eng, idx_ok, t.n)
                        eng.tensor_tensor(earlier[:, :].rearrange("p (k e) -> p k e", e=P), same[t.slot][:, :].rearrange("p (k e) -> p k e", e=P),
                                          bcast(before[:, :], 1, GT), ALU.mult).then_inc(first_ok, 1)
                        eng.tensor_scalar(away[:, :], cols[t.slot][:, :], spare[:, 0:1], None, ALU.subtract).then_inc(first_ok, 1)
                    if (t := s.ago(2)) is not None:
                        eng.wait_ge(filt_w_ok, t.n + 1)
                        eng.wait_ge(dst_ok, t.n + 1)
                        wait_pos(eng, total_ps, t.n - 1)
                        eng.tensor_tensor(msg[t.slot][:, :], hd[:, :], filt_w[t.slot][:, :], ALU.mult).then_inc(msg_ok, 1)
                    if (t := s.ago(3)) is not None:
                        eng.wait_ge(first_ok, 5 * t.n + 2)
                        eng.tensor_reduce(count[:, :], earlier[:, :].rearrange("p (k e) -> p k e", e=P), AX.X, ALU.add).then_inc(first_ok, 1)
                        eng.wait_ge(first_ok, 5 * t.n + 3)
                        eng.tensor_scalar(first[:, :], count[:, :], 0.0, None, ALU.is_equal).then_inc(first_ok, 1)
                        eng.wait_ge(first_ok, 5 * t.n + 4)
                        for sem_k in added:
                            wait_pos(eng, sem_k, 16 * (GT // NA) * (t.n - 1))
                        eng.tensor_tensor(away[:, :], away[:, :], first[:, :], ALU.mult).then_inc(first_ok, 1)
                        eng.wait_ge(first_ok, 5 * t.n + 5)
                        eng.tensor_scalar(to[t.slot][:, :], away[:, :], spare[:, 0:1], None, ALU.add).then_inc(idx_ok, 1)
                    if (t := s.ago(0)) is not None:
                        eng.wait_ge(parts_ok, 3 * t.n + 3)
                        wait_pos(eng, filt_ok, t.n - 1)
                        eng.tensor_tensor(soft[t.slot][:, :], z[:, :], parts[:, :], ALU.max).then_inc(soft_ok, 1)
                over_groups(eng, step, 3)

            @block.sync
            def _(sp):
                for dst, src in ((wf1, d["wf1"]), (wf2, d["wf2"]), (bf2, d["bf2"]), (src_i, d["srcT"])):
                    sp.dma_start(dst[:, :], src).then_inc(weights, 16)

                sp.wait_ge(vec, at["consts"])
                for q in range(3):
                    sp.dma_start(bias_rows[q:q + 1, :], bias3[:, q, :, :].rearrange("o k f -> o (k f)")).then_inc(bias_ok, 16)

                def step(s):
                    if (t := s.ago(0)) is not None:
                        wait_pos(sp, hotT_ok, 2 * (t.n - 1))
                        wait_pos(sp, z_ok, t.n - 1)
                        sp.dma_start(f20[t.slot][:, :], d["f20"][:, bass.ds(t.n * GE, GE)]).then_inc(f20_in[t.slot], 16)
                        sp.dma_start(rel[t.slot][:, :], bcast(d["rel"][bass.ds(t.n * GE, GE)], 0, P)).then_inc(rel_in[t.slot], 16)
                        wait_pos(sp, same_ok, t.n - 1)
                        sp.dma_start(row[t.slot][:, :], bcast(d["src"][bass.ds(t.n * GE, GE)], 0, P)).then_inc(row_in[t.slot], 16)
                over_groups(sp, step, 0)

            @block.gpsimd
            def _(pool):
                def step(s):
                    if (t := s.ago(4)) is not None:
                        pool.wait_ge(idx_ok, t.n + 1)
                        pool.wait_ge(total_ok, t.n + 1)
                        for k in range(GT):
                            wait_pos(pool, added[k % NA], 16 * (t.n * (GT // NA) + k // NA))
                            pool.sem_inc(go, 1)
                            pool.indirect_dma_start(d["sums"][k % NA], bass.IndirectOffsetOnAxis(ap=to[t.slot][:, k:k + 1], axis=0),
                                                    total[t.slot][:, P * k:P * k + P], None, bounds_check=NP + P - 1,
                                                    compute_op=ALU.add).then_inc(added[k % NA], 16)
                over_groups(pool, step, 4)
                for sem_k in added:
                    pool.wait_ge(sem_k, 16 * NG * (GT // NA))

            @block.scalar
            def _(eng):
                eng.wait_ge(vec, 1)

                def step(s):
                    if (t := s.ago(4)) is not None:
                        eng.wait_ge(total_ps, t.n + 1)
                        for sem_k in added:
                            wait_pos(eng, sem_k, 16 * (GT // NA) * (t.n - 1))
                        eng.copy(total[t.slot][:, :], tot[:, :]).then_inc(total_ok, 1)
                    if (t := s.ago(2)) is not None:
                        eng.wait_ge(filt_ok, t.n + 1)
                        eng.wait_ge(wt_ok, t.n + 1)
                        wait_pos(eng, msg_ok, t.n - 1)
                        for k in range(GT):
                            ins = eng.activation(filt_w[t.slot][:, P * k:P * k + P], filt[:, P * k:P * k + P], ACT.Copy, scale=wt[t.slot][:, k:k + 1])
                        ins.then_inc(filt_w_ok, 1)
                    if (t := s.ago(0)) is not None:
                        eng.wait_ge(z_ok, t.n + 1)
                        wait_pos(eng, soft_ok, t.n)
                        softplus_parts(eng, clamp[:, 0:1], z[:, :], parts[:, :], parts_ok, 3 * t.n, clamp[:, 0:1])
                over_groups(eng, step, 4)

            @block.tensor
            def _(eng):
                eng.wait_ge(weights, 64)
                eng.wait_ge(vec, 2)
                eng.matmul(filt[0:1, 0:F], one_c[:, :], wf2[:, :], start=True, stop=True).then_inc(shift_ok, 1)
                eng.wait_ge(bias_ok, 48)

                def step(s):
                    if (t := s.ago(2)) is not None:
                        block0 = load_ints(nc, PE, g.block0, t.n, NB - 1)
                        eng.wait_ge(hotT_ok, 2 * t.n + 2)
                        wait_pos(eng, msg_ok, t.n)
                        expand_destination(eng, hd, hotT[t.slot], g.recv, block0).then_inc(dst_ok, 1)
                    if (t := s.ago(0)) is not None:
                        eng.wait_ge(f20_in[t.slot], 16 * (t.pair + 1))
                        wait_pos(eng, soft_ok, t.n)
                        for h in range(2):
                            ins = eng.matmul(psum_half(z, h), wf1[:, :], f20[t.slot][:, 512 * h:512 * h + 512], start=True, stop=True)
                        ins.then_inc(z_ok, 1)
                    if (t := s.ago(3)) is not None:
                        eng.wait_ge(same_ok, t.n + 1)
                        eng.wait_ge(msg_ok, t.n + 1)
                        wait_pos(eng, total_ok, t.n)
                        for k in range(GT):
                            ins = eng.matmul(tot[:, P * k:P * k + P], same[t.slot][:, P * k:P * k + P], msg[t.slot][:, P * k:P * k + P],
                                             start=True, stop=True)
                        ins.then_inc(total_ps, 1)
                    if (t := s.ago(1)) is not None:
                        eng.wait_ge(soft_ok, t.n + 1)
                        wait_pos(eng, filt_w_ok, t.n)
                        for h in range(2):
                            eng.matmul(psum_half(filt, h), ones3[:, :], bias_rows[:, :], start=True, stop=False)
                            for k in range(4 * h, 4 * h + 4):
                                ins = eng.matmul(filt[:, P * k:P * k + P], soft[t.slot][:, P * k:P * k + P], wf2[:, :],
                                                 start=False, stop=(k % 4 == 3))
                        ins.then_inc(filt_ok, 1)
                over_groups(eng, step, 3)


def collect_sums(nc, g, d):
    with ExitStack() as c:
        sb = lambda n, s, t=F32: c.enter_context(nc.sbuf_tensor("cs_" + n, s, t))
        sem = phase_semaphores(nc, c, "cs_")
        parts, got = [sb(f"parts{i}", [P, NA, NW]) for i in range(2)], [sb(f"got{i}", [P, NBG, F]) for i in range(2)]
        loaded, stored = [sem("loaded0"), sem("loaded1")], sem("stored")
        summed, turned, copied = (sem(x) for x in ("summed", "turned", "copied"))
        gathered = [sem("gathered0"), sem("gathered1")]
        ps = [g.psA, g.psB]
        node_rows = lambda t, s: t[NW * s:NW * s + NW, :].rearrange("(b p) f -> p b f", p=P)

        with nc.Block() as block:
            @block.sync
            def _(sp):
                for s in range(NS + 1):
                    if s < NS:
                        if s > 1:
                            sp.wait_ge(stored, 16 * (s - 1))
                        for a in range(NA):
                            sp.dma_start(parts[s % 2][:, a, :].rearrange("p (b f) -> p b f", f=F), node_rows(d["sums"][a], s)).then_inc(loaded[s % 2], 16)
                    if s:
                        sp.wait_ge(summed, (NA - 1) * s)
                        sp.dma_start(node_rows(d["table"], s - 1), parts[(s - 1) % 2][:, 0, :].rearrange("p (b f) -> p b f", f=F)).then_inc(stored, 16)

            @block.vector
            def _(eng):
                done = 0
                for s in range(NS):
                    eng.wait_ge(loaded[s % 2], 16 * NA * (s // 2 + 1))
                    for a in range(1, NA):
                        eng.tensor_tensor(parts[s % 2][:, 0, :], parts[s % 2][:, 0, :], parts[s % 2][:, a, :], ALU.add).then_inc(summed, 1)
                        done += 1
                        eng.wait_ge(summed, done)

            @block.gpsimd
            def _(pool):
                pool.wait_ge(stored, 16 * NS)
                for s in range(NS):
                    if s > 1:
                        pool.wait_ge(turned, s - 1)
                    for b in range(NBG):
                        node = g.node[:, NBG * s + b:NBG * s + b + 1]
                        pool.indirect_dma_start(got[s % 2][:, b, :], None, d["table"], bass.IndirectOffsetOnAxis(ap=node, axis=0)).then_inc(gathered[s % 2], 16)

            @block.tensor
            def _(eng):
                for s in range(NS):
                    eng.wait_ge(gathered[s % 2], 16 * NBG * (s // 2 + 1))
                    if s > 1:
                        eng.wait_ge(copied, s - 1)
                    for b in range(NBG):
                        ins = eng.transpose(ps[s % 2][:, node_cols(b)], got[s % 2][:, b, :], g.ident[:, :])
                    ins.then_inc(turned, 1)

            @block.scalar
            def _(eng):
                for s in range(NS):
                    eng.wait_ge(turned, s + 1)
                    eng.copy(g.acc[:, NW * s:NW * s + NW], ps[s % 2][:, 0:NW]).then_inc(copied, 1)


def attention_scores(nc, g, d):
    with ExitStack() as c:
        sb = lambda n, s, t=F32: c.enter_context(nc.sbuf_tensor("as_" + n, s, t))
        two = lambda n, s, t=F32: [sb(n + "_a", s, t), sb(n + "_b", s, t)]
        sem = phase_semaphores(nc, c, "as_")
        two_sems = lambda n: [sem(n + "0"), sem(n + "1")]
        W = F + HEADS
        idx, G, rel, hotT = two("idx", [P, GT], I32), two("G", [P, GT * W]), two("rel", [P, GE], BF16), two("hotT", [P, 2, GE])
        e = sb("e", [P, GT, HEADS])
        idx_in, rel_in, G_in, stored = (two_sems(x) for x in ("idx_in", "rel_in", "G_in", "stored"))
        go, hotT_ok, ed_ok, e_ok, score_ok = (sem(x) for x in ("go", "hotT_ok", "ed_ok", "e_ok", "score_ok"))
        dst_s = g.psA[:, 0:GT * HEADS]

        with nc.Block() as block:
            @block.sync
            def _(sp):
                def step(s):
                    if (t := s.ago(0)) is not None:
                        wait_pos(sp, G_in[t.slot], 16 * GT * t.pair)
                        sp.dma_start(idx[t.slot][:, :], d["srcG"][bass.ds(t.n, 1)].rearrange("o p k -> (o p) k")).then_inc(idx_in[t.slot], 16)
                    if (t := s.ago(1)) is not None:
                        sp.wait_ge(G_in[t.slot], 16 * GT * (t.pair + 1))
                        sp.dma_start(d["rows"][bass.ds(t.n * GE, GE), :].rearrange("(k p) f -> p k f", p=P),
                                     G[t.slot][:, :].rearrange("p (k w) -> p k w", w=W)[:, :, 0:F]).then_inc(stored[t.slot], 16)
                over_groups(sp, step, 1)
                for s in stored:
                    sp.wait_ge(s, 16 * (NG // 2))

            @block.scalar
            def _(eng):
                def step(s):
                    if (t := s.ago(0)) is not None:
                        wait_pos(eng, hotT_ok, 2 * (t.n - 1))
                        eng.dma_start(rel[t.slot][:, :], bcast(d["rel"][bass.ds(t.n * GE, GE)], 0, P)).then_inc(rel_in[t.slot], 16)
                over_groups(eng, step, 0)

            @block.gpsimd
            def _(pool):
                def step(s):
                    if (t := s.ago(0)) is not None:
                        gather_group(pool, t, d["table_heads"], idx, G, idx_in, [(e_ok, t.n - 1), (stored[t.slot], 16 * t.pair)], go, G_in)
                over_groups(pool, step, 0)

            @block.tensor
            def _(eng):
                def step(s):
                    if (t := s.ago(2)) is not None:
                        block0 = load_ints(nc, PE, g.block0, t.n, NB - 1)
                        eng.wait_ge(hotT_ok, 2 * t.n + 2)
                        wait_pos(eng, e_ok, t.n)
                        for k in range(GT):
                            for b in range(2):
                                ins = eng.matmul(dst_s[:, HEADS * k:HEADS * k + HEADS], hotT[t.slot][:, b, P * k:P * k + P],
                                                 g.ed[:, :, :].rearrange("p b h -> p (b h)")[:, bass.ds(block0[k] * HEADS + HEADS * b, HEADS)],
                                                 start=(b == 0), stop=(b == 1))
                        ins.then_inc(ed_ok, 1)
                over_groups(eng, step, 2)

            @block.vector
            def _(eng):
                def step(s):
                    if (t := s.ago(3)) is not None:
                        eng.wait_ge(ed_ok, t.n + 1)
                        eng.wait_ge(G_in[t.slot], 16 * GT * (t.pair + 1))
                        wait_pos(eng, score_ok, t.n)
                        eng.tensor_tensor(e[:, :, :], dst_s.rearrange("p (k h) -> p k h", h=HEADS),
                                          G[t.slot][:, :].rearrange("p (k w) -> p k w", w=W)[:, :, F:W], ALU.add).then_inc(e_ok, 1)
                        eng.wait_ge(e_ok, t.n + 1)
                        eng.scalar_tensor_tensor(g.scores[:, bass.ds(t.n * GT, GT), :], e[:, :, :], SLOPE, e[:, :, :], ALU.mult, ALU.max).then_inc(score_ok, 1)
                    if (t := s.ago(1)) is not None:
                        eng.wait_ge(rel_in[t.slot], 16 * (t.pair + 1))
                        wait_pos(eng, ed_ok, t.n - 1)
                        for b, place in enumerate((g.iota_col, g.iota_col2)):
                            eng.tensor_scalar(hotT[t.slot][:, b, :], rel[t.slot][:, :], place[:, 0:1], None, ALU.is_equal).then_inc(hotT_ok, 1)
                over_groups(eng, step, 3)


def edge_attention(nc, g, d):
    with ExitStack() as c:
        sb = lambda n, s, t=F32: c.enter_context(nc.sbuf_tensor("ea_" + n, s, t))
        two = lambda n, s, t=F32: [sb(n + "_a", s, t), sb(n + "_b", s, t)]
        sem = phase_semaphores(nc, c, "ea_")
        two_sems = lambda n: [sem(n + "0"), sem(n + "1")]
        we, aw, ab, clamp = sb("we", [F, F]), sb("aw", [P, F]), sb("ab", [P, 1]), sb("clamp", [P, 1])
        idx, ef, G, rel, hotT = two("idx", [P, GT], I32), two("ef", [P, GE]), two("G", [P, GE]), two("rel", [P, GE], BF16), two("hotT", [P, 2, GE])
        att, X, rr, Y, lg = two("att", [P, GE]), two("X", [P, GE]), two("rr", [P, GE]), sb("Y", [P, GE]), sb("lg", [P, GT * HEADS])
        weights, vec = sem("weights"), sem("vec")
        idx_in, ef_in, rel_in, G_in, stored = (two_sems(x) for x in ("idx_in", "ef_in", "rel_in", "G_in", "stored"))
        go, proj_ok, att_ok, hotT_ok, recv_ok, X_ok, mish_ok, Y_ok, Yw_ok, lg_ok, score_ok = (
            sem(x) for x in ("go", "proj_ok", "att_ok", "hotT_ok", "recv_ok", "X_ok", "mish_ok", "Y_ok", "Yw_ok", "lg_ok", "score_ok"))
        proj, recv = [g.psA, g.psB], [g.psC, g.psD]

        with nc.Block() as block:
            @block.sync
            def _(sp):
                sp.dma_start(we[:, :], d["we"]).then_inc(weights, 16)
                sp.dma_start(aw[:, :], d["aw"].broadcast_to([P, F])).then_inc(weights, 16)
                sp.dma_start(ab[:, :], d["ab"].broadcast_to([P, 1])).then_inc(weights, 16)

                def step(s):
                    if (t := s.ago(0)) is not None:
                        wait_pos(sp, G_in[t.slot], 16 * GT * t.pair)
                        sp.dma_start(idx[t.slot][:, :], d["srcG"][bass.ds(t.n, 1)].rearrange("o p k -> (o p) k")).then_inc(idx_in[t.slot], 16)
                        wait_pos(sp, hotT_ok, 2 * (t.n - 1))
                        wait_pos(sp, proj_ok, t.n - 1)
                        sp.dma_start(ef[t.slot][:, :], d["ef"][:, bass.ds(t.n * GE, GE)]).then_inc(ef_in[t.slot], 16)
                        sp.dma_start(rel[t.slot][:, :], bcast(d["rel"][bass.ds(t.n * GE, GE)], 0, P)).then_inc(rel_in[t.slot], 16)
                    if (t := s.ago(3)) is not None:
                        sp.wait_ge(att_ok, t.n + 1)
                        sp.dma_start(d["rows"][bass.ds(t.n * GE, GE), :].rearrange("(k p) f -> p k f", p=P),
                                     att[t.slot][:, :].rearrange("p (k f) -> p k f", f=F)).then_inc(stored[t.slot], 16)
                over_groups(sp, step, 3)
                for s in stored:
                    sp.wait_ge(s, 16 * (NG // 2))

            @block.gpsimd
            def _(pool):
                def step(s):
                    if (t := s.ago(0)) is not None:
                        gather_group(pool, t, d["table"], idx, G, idx_in, [(att_ok, t.n - 1)], go, G_in)
                over_groups(pool, step, 0)

            @block.tensor
            def _(eng):
                eng.wait_ge(weights, 48)

                def step(s):
                    if (t := s.ago(2)) is not None:
                        block0 = load_ints(nc, PE, g.block0, t.n, NB - 1)
                    if (u := s.ago(1)) is not None:
                        eng.wait_ge(ef_in[u.slot], 16 * (u.pair + 1))
                        wait_pos(eng, att_ok, u.n - 1)
                        for k in range(GT):
                            ins = eng.matmul(proj[u.slot][:, P * k:P * k + P], ef[u.slot][:, P * k:P * k + P], we[:, :], start=True, stop=True)
                        ins.then_inc(proj_ok, 1)
                    if t is not None:
                        eng.wait_ge(hotT_ok, 2 * t.n + 2)
                        wait_pos(eng, X_ok, t.n - 1)
                        expand_destination(eng, recv[t.slot], hotT[t.slot], g.recv, block0).then_inc(recv_ok, 1)
                over_groups(eng, step, 2)

            @block.scalar
            def _(eng):
                eng.wait_ge(vec, 1)

                def step(s):
                    if (t := s.ago(3)) is not None:
                        r = rr[t.slot][:, :]
                        eng.wait_ge(X_ok, t.n + 1)
                        wait_pos(eng, Y_ok, t.n - 1)
                        eng.activation(r, X[t.slot][:, :], ACT.Relu, bias=clamp[:, 0:1], scale=-1.0).then_inc(mish_ok, 1)
                        eng.wait_ge(mish_ok, 5 * t.n + 1)
                        eng.activation(r, r, ACT.Exp, bias=clamp[:, 0:1], scale=-1.0).then_inc(mish_ok, 1)
                        eng.wait_ge(mish_ok, 5 * t.n + 2)
                        eng.activation(r, r, ACT.Square, bias=1.0).then_inc(mish_ok, 1)
                        eng.wait_ge(mish_ok, 5 * t.n + 3)
                        eng.activation(r, r, ACT.Ln, bias=1.0).then_inc(mish_ok, 1)
                        eng.wait_ge(mish_ok, 5 * t.n + 4)
                        eng.activation(r, r, ACT.Exp, scale=-1.0).then_inc(mish_ok, 1)
                over_groups(eng, step, 3)

            @block.vector
            def _(eng):
                eng.memset(clamp[:, :], MISH_CLAMP).then_inc(vec, 1)
                eng.wait_ge(weights, 48)
                eng.tensor_scalar(aw[:, :], aw[:, :], -2.0, None, ALU.mult).then_inc(vec, 1)
                eng.wait_ge(vec, 2)

                def step(s):
                    if (t := s.ago(2)) is not None:
                        eng.wait_ge(proj_ok, t.n + 1)
                        eng.wait_ge(G_in[t.slot], 16 * GT * (t.pair + 1))
                        wait_pos(eng, stored[t.slot], 16 * t.pair)
                        wait_pos(eng, X_ok, t.n - 1)
                        eng.tensor_tensor(att[t.slot][:, :], proj[t.slot][:, :], G[t.slot][:, :], ALU.add).then_inc(att_ok, 1)
                    if (t := s.ago(3)) is not None:
                        eng.wait_ge(recv_ok, t.n + 1)
                        eng.wait_ge(att_ok, t.n + 1)
                        wait_pos(eng, Y_ok, t.n - 1)
                        wait_pos(eng, mish_ok, 5 * (t.n - 1))
                        eng.tensor_tensor(X[t.slot][:, :], recv[t.slot][:, :], att[t.slot][:, :], ALU.add).then_inc(X_ok, 1)
                    if (t := s.ago(1)) is not None:
                        eng.wait_ge(rel_in[t.slot], 16 * (t.pair + 1))
                        wait_pos(eng, recv_ok, t.n - 1)
                        for b, place in enumerate((g.iota_col, g.iota_col2)):
                            eng.tensor_scalar(hotT[t.slot][:, b, :], rel[t.slot][:, :], place[:, 0:1], None, ALU.is_equal).then_inc(hotT_ok, 1)
                    if (t := s.ago(4)) is not None:
                        eng.wait_ge(mish_ok, 5 * t.n + 5)
                        wait_pos(eng, lg_ok, t.n)
                        eng.scalar_tensor_tensor(Y[:, :], rr[t.slot][:, :], -0.5, X[t.slot][:, :], ALU.add, ALU.mult).then_inc(Y_ok, 1)
                        eng.wait_ge(Y_ok, t.n + 1)
                        heads = Y[:, :].rearrange("p (k f) -> p k f", f=F)
                        eng.tensor_tensor(heads, heads, bcast(aw[:, :], 1, GT), ALU.mult).then_inc(Yw_ok, 1)
                        eng.wait_ge(Yw_ok, t.n + 1)
                        wait_pos(eng, score_ok, t.n)
                        eng.tensor_reduce(lg[:, :], Y[:, :].rearrange("p (k f) -> p k f", f=HD), AX.X, ALU.add).then_inc(lg_ok, 1)
                        eng.wait_ge(lg_ok, t.n + 1)
                        eng.tensor_scalar(g.scores[:, bass.ds(t.n * GT, GT), :], lg[:, :].rearrange("p (k h) -> p k h", h=HEADS), ab[:, 0:1], None,
                                          ALU.add).then_inc(score_ok, 1)
                over_groups(eng, step, 4)


def segment_softmax(nc, g, d, layer):
    with ExitStack() as c:
        sb = lambda n, s, t=F32: c.enter_context(nc.sbuf_tensor(f"sm{layer}_{n}", s, t))
        sem = phase_semaphores(nc, c, f"sm{layer}_")
        vec, turned, stage_ok, stored, fetched, exp_ok, ends_t, chain_t, half_ok = (
            sem(x) for x in ("vec", "turned", "stage_ok", "stored", "fetched", "exp_ok", "ends_t", "chain_t", "half_ok"))
        stage = sb("stage", [SEGC, HEADS, SEGN, P])
        L, A, B = (sb(x, [P, HEADS, PB]) for x in ("L", "A", "B"))
        ends, chain, chain2 = sb("ends", [P, HEADS]), sb("chain", [HEADS, P]), sb("chain2", [HEADS, P])
        carry = sb("carry", [P, HEADS])
        at = {}
        rows = lambda t: t.rearrange("h (k t p) -> t h k p", t=SEGC, p=P)
        seg_ps = [g.psA, g.psB, g.psC, g.psD]
        n_small = [0]

        with nc.Block() as block:
            @block.vector
            def _(eng):
                do = Chain(eng, vec, at)

                def carried(kind, backward):
                    i = n_small[0]
                    n_small[0] += 1
                    at[f"ends{i}"] = do.count
                    eng.wait_ge(ends_t, i + 1)
                    mask = g.chain_mask[:, {"max": 0, "sum": 1, "spread": 2}[kind], :]
                    one = g.psD[0:HEADS, 896:1024]
                    do(eng.tensor_copy(chain2[:, :], one))
                    if kind == "max":
                        do(eng.tensor_tensor_scan(chain[:, :], mask, chain2[:, :], -BIG, ALU.add, ALU.max))
                    elif not backward:
                        do(eng.tensor_tensor_scan(chain[:, :], mask, chain2[:, :], 0.0, ALU.mult, ALU.add))
                    else:
                        do(eng.tensor_tensor_scan(chain[:, ::-1], mask[:, ::-1], chain2[:, ::-1], 0.0, ALU.mult, ALU.add))
                    if backward:
                        do(eng.tensor_copy(chain2[:, 0:P - 1], chain[:, 1:P]))
                        do(eng.memset(chain2[:, P - 1:P], 0.0), f"chain{i}")
                    else:
                        do(eng.tensor_copy(chain2[:, 1:P], chain[:, 0:P - 1]))
                        do(eng.memset(chain2[:, 0:1], -BIG if kind == "max" else 0.0), f"chain{i}")
                    eng.wait_ge(chain_t, i + 1)
                    do(eng.tensor_copy(carry[:, :], g.psC[:, 896:896 + HEADS]))

                def over_destination(kind, src, tmp):
                    for h in range(HEADS):
                        if kind == "max":
                            do(eng.tensor_tensor_scan(tmp[:, h, :], g.reset[:, :], src[:, h, :], -BIG, ALU.add, ALU.max))
                        else:
                            do(eng.tensor_tensor_scan(tmp[:, h, :], g.keep_s[:, :], src[:, h, :], 0.0, ALU.mult, ALU.add))
                    do(eng.tensor_copy(ends[:, :], tmp[:, :, PB - 1]))
                    carried(kind, False)
                    for h in range(HEADS):
                        if kind == "max":
                            do(eng.scalar_tensor_tensor(tmp[:, h, :], g.pre_neg[:, :], carry[:, h:h + 1], tmp[:, h, :], ALU.add, ALU.max))
                        else:
                            do(eng.scalar_tensor_tensor(tmp[:, h, :], g.pre[:, :], carry[:, h:h + 1], tmp[:, h, :], ALU.mult, ALU.add))
                    do(eng.tensor_tensor(tmp[:, :, :], tmp[:, :, :], bcast(g.last[:, :], 1, HEADS), ALU.mult))
                    for h in range(HEADS):
                        do(eng.tensor_tensor_scan(tmp[:, h, ::-1], g.keep_l[:, ::-1], tmp[:, h, ::-1], 0.0, ALU.mult, ALU.add))
                    do(eng.tensor_copy(ends[:, :], tmp[:, :, 0]))
                    carried("spread", True)
                    for h in range(HEADS):
                        do(eng.scalar_tensor_tensor(tmp[:, h, :], g.suf[:, :], carry[:, h:h + 1], tmp[:, h, :], ALU.mult, ALU.add))

                eng.wait_ge(fetched, 16)
                over_destination("max", L, A)
                if layer == 2:
                    do(eng.tensor_scalar(A[:, :, :], A[:, :, :], 0.0, None, ALU.max))
                do(eng.tensor_tensor(L[:, :, :], L[:, :, :], A[:, :, :], ALU.subtract), "shifted")
                eng.wait_ge(exp_ok, 1)
                over_destination("sum", L, A)
                if layer == 2:
                    do(eng.tensor_scalar(A[:, :, :], A[:, :, :], ALPHA_EPS, None, ALU.add))
                do(eng.reciprocal(A[:, :, :], A[:, :, :]))
                do(eng.tensor_tensor(L[:, :, :], L[:, :, :], A[:, :, :], ALU.mult), "alpha")

            @block.tensor
            def _(eng):
                for h in range(HEADS):
                    for k in range(SEGN):
                        ins = eng.transpose(seg_ps[h][0:SEGC, P * k:P * k + P], g.scores[:, SEGC * k:SEGC * (k + 1), h], g.ident[:, :])
                    ins.then_inc(turned, 1)
                for i in range(4):
                    eng.wait_ge(vec, at[f"ends{i}"])
                    if i == 0:
                        eng.wait_ge(stage_ok, 4)
                    eng.transpose(g.psD[0:HEADS, 896:1024], ends[:, :], g.ident[:, :]).then_inc(ends_t, 1)
                    eng.wait_ge(vec, at[f"chain{i}"])
                    eng.transpose(g.psC[:, 896:896 + HEADS], chain2[:, :], g.ident[0:HEADS, 0:HEADS]).then_inc(chain_t, 1)
                eng.wait_ge(fetched, 32)
                for h in range(HEADS):
                    for k in range(SEGN):
                        ins = eng.transpose(seg_ps[h][:, P * k:P * k + SEGC], stage[:, h, k, :], g.ident[0:SEGC, 0:SEGC])
                    ins.then_inc(turned, 1)

            @block.scalar
            def _(eng):
                for h in range(HEADS):
                    eng.wait_ge(turned, h + 1)
                    eng.copy(stage[:, h, :, :], seg_ps[h][0:SEGC, 0:SEGN * P].rearrange("t (k p) -> t k p", p=P)).then_inc(stage_ok, 1)
                eng.wait_ge(vec, at["shifted"])
                eng.activation(L[:, :, :], L[:, :, :], ACT.Exp).then_inc(exp_ok, 1)
                for h in range(HEADS):
                    eng.wait_ge(turned, HEADS + h + 1)
                    eng.copy(g.scores[:, :, h].rearrange("p (k t) -> p k t", t=SEGC),
                             seg_ps[h][:, 0:SEGN * P].rearrange("p (k t) -> p k t", t=P)[:, :, 0:SEGC]).then_inc(stage_ok, 1)

            @block.sync
            def _(sp):
                sp.wait_ge(stage_ok, 4)
                for h in range(HEADS):
                    sp.dma_start(rows(d["logits"])[:, h], stage[:, h, :, :]).then_inc(stored, 16)
                sp.wait_ge(stored, 64)
                sp.dma_start(L[:, :, :], d["logits"].rearrange("h (q j) -> q h j", q=P)).then_inc(fetched, 16)
                sp.wait_ge(vec, at["alpha"])
                sp.dma_start(d["alpha"].rearrange("h (q j) -> q h j", q=P), L[:, :, :]).then_inc(half_ok, 16)
                sp.wait_ge(half_ok, 16)
                for h in range(HEADS):
                    sp.dma_start(stage[:, h, :, :], rows(d["alpha"])[:, h]).then_inc(half_ok, 16)
                sp.wait_ge(half_ok, 80)
                sp.sem_inc(fetched, 16)


def weighted_sums(nc, g, d, layer):
    with ExitStack() as c:
        sb = lambda n, s, t=F32: c.enter_context(nc.sbuf_tensor(f"ws{layer}_{n}", s, t))
        two = lambda n, s, t=F32: [sb(n + "_a", s, t), sb(n + "_b", s, t)]
        sem = phase_semaphores(nc, c, f"ws{layer}_")
        V, msg, hot, lr = two("V", [P, GE]), two("msg", [P, GE]), two("hot", [P, GE]), two("lr", [P, GT])
        acc_b, away = sb("acc_b", [P, RW]), sb("away", [P, GE])
        V_in = [sem("V_in0"), sem("V_in1")]
        cleared, msg_ok, cols_ok, away_ok, hot_ok, win_ok, added, go = (
            sem(x) for x in ("cleared", "msg_ok", "cols_ok", "away_ok", "hot_ok", "win_ok", "added", "go"))
        win = [g.psA, g.psB]

        with nc.Block() as block:
            @block.sync
            def _(sp):
                def step(s):
                    if (t := s.ago(0)) is not None:
                        wait_pos(sp, msg_ok, t.n - 1)
                        sp.dma_start(V[t.slot][:, :].rearrange("p (k f) -> p k f", f=F),
                                     d["rows"][bass.ds(t.n * GE, GE), :].rearrange("(k p) f -> p k f", p=P)).then_inc(V_in[t.slot], 16)
                over_groups(sp, step, 0)

            @block.tensor
            def _(eng):
                def step(s):
                    if (t := s.ago(1)) is not None:
                        eng.wait_ge(msg_ok, t.n + 1)
                        eng.wait_ge(hot_ok, t.n + 1)
                        wait_pos(eng, added, (t.n - 1) * GT)
                        for k in range(GT):
                            ins = eng.matmul(win[t.slot][:, P * k:P * k + P], msg[t.slot][:, P * k:P * k + P], hot[t.slot][:, P * k:P * k + P],
                                             start=True, stop=True)
                        ins.then_inc(win_ok, 1)
                over_groups(eng, step, 1)

            @block.scalar
            def _(eng):
                def step(s):
                    if (t := s.ago(0)) is not None:
                        eng.wait_ge(cols_ok, t.n + 1)
                        wait_pos(eng, hot_ok, t.n)
                        for k in range(GT):
                            ins = eng.activation(away[:, P * k:P * k + P], g.iota_row[:, :], ACT.Square, bias=lr[t.slot][:, k:k + 1], scale=-1.0)
                        ins.then_inc(away_ok, 1)
                        eng.wait_ge(away_ok, t.n + 1)
                        wait_pos(eng, win_ok, t.n - 1)
                        eng.activation(hot[t.slot][:, :], away[:, :], ACT.Relu, bias=1.0, scale=-1.0).then_inc(hot_ok, 1)
                over_groups(eng, step, 0)

            @block.gpsimd
            def _(pool):
                def step(s):
                    if (t := s.ago(0)) is not None:
                        pool.wait_ge(V_in[t.slot], 16 * (t.pair + 1))
                        wait_pos(pool, win_ok, t.n - 1)
                        pool.sem_inc(go, 1)
                        pool.tensor_tensor(msg[t.slot][:, :].rearrange("p (k h f) -> p (k h) f", h=HEADS, f=HD),
                                           V[t.slot][:, :].rearrange("p (k h f) -> p (k h) f", h=HEADS, f=HD),
                                           bcast(g.scores[:, bass.ds(t.n * GT, GT), :].rearrange("p k h -> p (k h)"), 2, HD), ALU.mult).then_inc(msg_ok, 1)
                over_groups(pool, step, 0)

            @block.vector
            def _(eng):
                eng.memset(g.acc[:, :], 0.0).then_inc(cleared, 1)
                eng.memset(acc_b[:, :], 0.0).then_inc(cleared, 1)
                eng.wait_ge(cleared, 2)

                def step(s):
                    if (old := s.ago(2)) is not None:
                        rank0 = load_ints(nc, DVE, g.rank0, old.n, N)
                    if (t := s.ago(0)) is not None:
                        wait_pos(eng, away_ok, t.n - 1)
                        eng.tensor_copy(lr[t.slot][:, :], g.lr[:, bass.ds(t.n * GT, GT)]).then_inc(cols_ok, 1)
                    if old is not None:
                        eng.wait_ge(win_ok, old.n + 1)
                        for k in range(GT):
                            sums, cols = (g.acc, acc_b)[k % 2], bass.ds(rank0[k], P)
                            wait_pos(eng, added, old.n * GT + k - 1)
                            eng.tensor_tensor(sums[:, cols], sums[:, cols], win[old.slot][:, P * k:P * k + P], ALU.add).then_inc(added, 1)
                over_groups(eng, step, 2)
                eng.wait_ge(added, NT)
                eng.tensor_tensor(g.acc[:, :], g.acc[:, :], acc_b[:, :], ALU.add).then_inc(cleared, 1)


def program(nc, d):
    with ExitStack() as c:
        sb = lambda n, s, t=F32: c.enter_context(nc.sbuf_tensor(n, s, t))
        g = Shared()
        g.psA, g.psB, g.psC, g.psD = (c.enter_context(nc.psum_tensor(n, [P, 1024], F32)) for n in ("psA", "psB", "psC", "psD"))
        g.iota_row, g.iota_col, g.iota_col2 = sb("iota_row", [P, P]), sb("iota_col", [P, 1]), sb("iota_col2", [P, 1])
        g.ident, g.ones_row = sb("ident", [P, P]), sb("ones_row", [1, P])
        g.ewT, g.lr, g.cut = sb("ewT_sb", [P, NT]), sb("lr", [P, NT]), sb("cut", [P, NT])
        g.rank0, g.block0 = sb("rank0", [1, NT], I32), sb("block0", [1, NT], I32)
        g.last_edge, g.node, g.has_edge = sb("last_edge", [P, NB], I32), sb("node", [P, NB], I32), sb("has_edge", [P, NB])
        g.last, g.reset, g.keep_s, g.keep_l = (sb(x, [P, PB]) for x in ("last", "reset", "keep_s", "keep_l"))
        g.pre, g.pre_neg, g.suf = (sb(x, [P, PB]) for x in ("pre", "pre_neg", "suf"))
        g.chain_mask = sb("chain_mask", [HEADS, 3, P])
        g.x = sb("x_sb", [P, NB, F])
        setup(nc, g, d)
        scan_masks(nc, g, d)
        filter_products(nc, g, d)
        g.recv = sb("recv", [P, RW])
        node_stage(nc, g, d, 0)
        filter_sums(nc, g, d)
        g.acc, g.ed = sb("acc", [P, RW]), sb("ed", [P, RB, HEADS])
        collect_sums(nc, g, d)
        node_stage(nc, g, d, 1)
        g.scores = sb("scores", [P, NT, HEADS])
        attention_scores(nc, g, d)
        segment_softmax(nc, g, d, 2)
        weighted_sums(nc, g, d, 2)
        node_stage(nc, g, d, 2)
        edge_attention(nc, g, d)
        segment_softmax(nc, g, d, 3)
        weighted_sums(nc, g, d, 3)
        node_stage(nc, g, d, 3)


def kernel(**inputs):
    import concourse.bacc as bacc
    from concourse.bass_utils import run_bass_kernel_spmd

    a = {k: np.asarray(v) for k, v in inputs.items()}
    src = np.zeros(EP, np.int32)
    src[:E] = a["src"]
    dst = np.full(EP + 2, N, np.int32)
    dst[0], dst[1:E + 1], dst[-1] = -1, a["dst"], N + 1
    ew = np.zeros(EP, np.float32)
    ew[:E] = a["edge_weight"]
    ef = np.zeros((F, EP), np.float32)
    ef[:, :E] = a["edge_attr_128"].T
    rbf_in = a["edge_attr_20"].shape[1]
    f20 = np.zeros((rbf_in + 1, EP), np.float32)
    f20[:rbf_in, :E], f20[rbf_in] = a["edge_attr_20"].T, 1.0
    x = np.zeros((NP, F), np.float32)
    x[:N] = a["x"]
    tiles = lambda v: np.ascontiguousarray(v.reshape(NT, P).T)
    a_heads = np.zeros((F, 2 * HEADS), np.float32)
    for h in range(HEADS):
        a_heads[HD * h:HD * h + HD, h] = a["L2_gnn_a_src"][h, :, 0]
        a_heads[HD * h:HD * h + HD, HEADS + h] = a["L2_gnn_a_dst"][h, :, 0]
    w2 = a["L2_gnn_W"].transpose(1, 0, 2).reshape(F, F)
    arrays = dict(
        x=x, srcG=np.ascontiguousarray(src.reshape(NG, GT, P).transpose(0, 2, 1)),
        src=src, srcT=tiles(src),
        dstT=tiles(dst[1:-1]), prevT=tiles(dst[:-2]),
        dstP=dst[1:-1].reshape(P, PB), prevP=dst[:-2].reshape(P, PB), nextP=dst[2:].reshape(P, PB),
        ewT=tiles(ew), ew=ew.reshape(1, EP), ef=ef, f20=f20,
        w1=a["L0_gnn_W1"], b1=a["L0_gnn_b1"][:, None], w2=a["L0_gnn_W2"], b2=a["L0_gnn_b2"][:, None],
        w3=a["L0_gnn_W3"], b3=a["L0_gnn_b3"][None],
        mu=np.linspace(0.0, 1.0, F, dtype=np.float32)[:, None],
        w_in=a["L1_gnn_W_in"], b_in=a["L1_gnn_b_in"][None],
        wf1=np.concatenate([a["L1_gnn_Wf1"], a["L1_gnn_bf1"][None]]), wf2=a["L1_gnn_Wf2"], bf2=a["L1_gnn_bf2"][None],
        wo1=a["L1_gnn_Wo1"], bo1=a["L1_gnn_bo1"][:, None], wo2=a["L1_gnn_Wo2"], bo2=a["L1_gnn_bo2"][None],
        wg=w2, wgT=w2.T, a_heads=a_heads,
        ws=a["L3_gnn_Ws_k"].reshape(F, F), wr=a["L3_gnn_Wr_k"].reshape(F, F), we=a["L3_gnn_We_k"].reshape(F, F),
        bs=a["L3_gnn_Ws_b"].reshape(1, F), br=a["L3_gnn_Wr_b"].reshape(1, F), be=a["L3_gnn_We_b"].reshape(1, F),
        aw=np.tile(a["L3_gnn_attn_w"][:, 0], HEADS)[None], ab=a["L3_gnn_attn_b"][None],
    )
    nc = bacc.Bacc("TRN2", target_bir_lowering=False, num_devices=1)
    d = {}
    feed = {}
    for name, v in arrays.items():
        v = np.ascontiguousarray(v)
        feed["in_" + name] = v
        d[name] = (nc.dram_tensor("in_" + name, v.shape, mybir.dt.from_np(v.dtype), kind="ExternalInput").ap())
    d["out"] = nc.dram_tensor("out_0_dram", (N, F), F32, kind="ExternalOutput").ap()
    d["rel"] = nc.dram_tensor("rel", (EP,), BF16, kind="Internal").ap()
    d["keep"] = nc.dram_tensor("keep_rows", (EP,), BF16, kind="Internal").ap()
    d["perm"] = nc.dram_tensor("perm", (NP, 4), F32, kind="Internal").ap()
    d["table"] = nc.dram_tensor("table", (NP, F), F32, kind="Internal").ap()
    d["table_heads"] = nc.dram_tensor("table_heads", (NP, F + HEADS), F32, kind="Internal").ap()
    d["sums"] = [nc.dram_tensor(f"sums{i}", (NP + P, F), F32, kind="Internal").ap() for i in range(NA)]
    d["rows"] = nc.dram_tensor("rows", (EP, F), F32, kind="Internal").ap()
    d["logits"] = nc.dram_tensor("logits", (HEADS, EP), F32, kind="Internal").ap()
    d["alpha"] = nc.dram_tensor("alpha", (HEADS, EP), F32, kind="Internal").ap()
    program(nc, d)
    return run_bass_kernel_spmd(nc, [feed], core_ids=[0]).results[0]["out_0_dram"]
```
